# Optimizing a Trainium2 kernel written in Bass

```python
import numpy as np
import jax
import jax.numpy as jnp

def _softmax(x, axis=-1):
    return jax.nn.softmax(x, axis=axis)

def _gelu(x):
    return jax.nn.gelu(x, approximate=True)

def _silu(x):
    return jax.nn.silu(x)

def _sigmoid(x):
    return jax.nn.sigmoid(x)

def _layernorm(x, axis=-1, eps=1e-05):
    m = jnp.mean(x, axis=axis, keepdims=True)
    v = jnp.var(x, axis=axis, keepdims=True)
    return (x - m) / jnp.sqrt(v + eps)

def _scatter_add(tgt, idx, src, axis=0):
    return tgt.at[idx].add(src)

def _segment_sum(src, seg, n):
    return jax.ops.segment_sum(src, seg, n)
kernel_name = 'mk_gnn_preln_d4_gnn_r64_31b297'

def setup_inputs(seed: int=0):
    np.random.seed(seed)
    _w = jnp.asarray

    def _rec_inputs():
        import jax
        import jax.numpy as jnp
        _gk = jax.random.key(seed)
        x = -0.0003713 + 1 * jax.random.normal(jax.random.fold_in(_gk, 1), (50000, 128), jnp.float32)
        src = jax.random.randint(jax.random.fold_in(_gk, 2), (12500,), 0, 50000, jnp.int32)
        dst = jax.random.randint(jax.random.fold_in(_gk, 3), (12500,), 0, 50000, jnp.int32)
        _o = jnp.argsort(dst, stable=True)
        src = src[_o]
        dst = dst[_o]
        edge_type_100 = jax.random.randint(jax.random.fold_in(_gk, 14), (12500,), 0, 100, jnp.int32)
        return (x, src, dst, edge_type_100)
    x, src, dst, edge_type_100 = _rec_inputs()

    def _L0_gnn_setup():
        import jax, jax.numpy as jnp
        import numpy as np
        NEG_SLOPE = 0.2
        EPS = 1e-16
        N_NODES = 100000
        N_EDGES = 25000
        CHANNELS = 128
        M_LAYERS = 3

        def _gat_conv(x, src, dst, W, a_src, a_dst, b, n_nodes):
            h = x @ W
            s = h @ a_src
            d = h @ a_dst
            e = s[src] + d[dst]
            e = jnp.where(e > 0, e, NEG_SLOPE * e)
            e_max = jax.ops.segment_max(e, dst, num_segments=n_nodes)
            e_max = jnp.where(jnp.isfinite(e_max), e_max, 0.0)
            w = jnp.exp(e - e_max[dst])
            denom = jax.ops.segment_sum(w, dst, num_segments=n_nodes)
            alpha = w / (denom[dst] + EPS)
            out = jax.ops.segment_sum(alpha[:, None] * h[src], dst, num_segments=n_nodes)
            return out + b
        key = jax.random.key(seed)
        k1, k2, k3, k4, k5 = jax.random.split(key, 5)
        x = jax.random.normal(k1, (N_NODES, CHANNELS), dtype=jnp.float32)
        edge_index = jax.random.randint(k2, (2, N_EDGES), 0, N_NODES, dtype=jnp.int64)
        Ws = jax.random.normal(k3, (M_LAYERS, CHANNELS, CHANNELS), dtype=jnp.float32) / np.sqrt(CHANNELS)
        att_src = jax.random.normal(k4, (M_LAYERS, CHANNELS), dtype=jnp.float32) / np.sqrt(CHANNELS)
        att_dst = jax.random.normal(k5, (M_LAYERS, CHANNELS), dtype=jnp.float32) / np.sqrt(CHANNELS)
        bias = jnp.zeros((M_LAYERS, CHANNELS), dtype=jnp.float32)
        return {'x': x, 'edge_index': edge_index, 'Ws': Ws, 'att_src': att_src, 'att_dst': att_dst, 'bias': bias}
    _L0_gnn_all = _L0_gnn_setup()
    _L0_gnn_in = {k: v for k, v in _L0_gnn_all.items() if k in ('Ws', 'att_src', 'att_dst', 'bias')}
    del _L0_gnn_all

    def _L1_gnn_setup():
        import jax, jax.numpy as jnp
        import numpy as np
        N_NODES = 50000
        N_EDGES = 12500
        IN_DIM = 128
        OUT_DIM = 128
        NUM_RELS = 100
        NUM_BASES = 4
        key = jax.random.key(seed)
        ks = jax.random.split(key, 8)
        h = jax.random.normal(ks[0], (N_NODES, IN_DIM), dtype=jnp.float32)
        norm = jax.random.uniform(ks[1], (N_NODES, 1), dtype=jnp.float32)
        src = jax.random.randint(ks[2], (N_EDGES,), 0, N_NODES, dtype=jnp.int32)
        dst = jax.random.randint(ks[3], (N_EDGES,), 0, N_NODES, dtype=jnp.int32)
        rel_type = jax.random.randint(ks[4], (N_EDGES,), 0, NUM_RELS, dtype=jnp.int32)
        basis_weights = jax.random.normal(ks[5], (NUM_BASES, IN_DIM, OUT_DIM), dtype=jnp.float32) * (2.0 / np.sqrt(IN_DIM + OUT_DIM))
        coefficients = jax.random.normal(ks[6], (NUM_RELS, NUM_BASES), dtype=jnp.float32) * (1.0 / np.sqrt(NUM_RELS + NUM_BASES))
        loop_weight = jax.random.normal(ks[7], (IN_DIM, OUT_DIM), dtype=jnp.float32) * (2.0 / np.sqrt(IN_DIM + OUT_DIM))
        return {'h': h, 'norm': norm, 'src': src, 'dst': dst, 'rel_type': rel_type, 'basis_weights': basis_weights, 'coefficients': coefficients, 'loop_weight': loop_weight}
    _L1_gnn_all = _L1_gnn_setup()
    _L1_gnn_in = {k: v for k, v in _L1_gnn_all.items() if k in ('basis_weights', 'coefficients', 'loop_weight')}
    del _L1_gnn_all

    def _L2_gnn_setup():
        import jax, jax.numpy as jnp
        import numpy as np
        N, E, F_IN, H, C = (100000, 25000, 128, 8, 16)
        NEG_SLOPE = 0.2
        key = jax.random.key(seed)
        k1, k2, k3, k4, k5 = jax.random.split(key, 5)
        x = jax.random.normal(k1, (N, F_IN), dtype=jnp.float32)
        edge_index = jax.random.randint(k2, (2, E), 0, N, dtype=jnp.int64).astype(jnp.int32)
        scale = 1.0 / np.sqrt(F_IN)
        W_src = jax.random.normal(k3, (F_IN, H * C), dtype=jnp.float32) * scale
        attn_src = jax.random.normal(k4, (H, C), dtype=jnp.float32) * scale
        attn_dst = jax.random.normal(k5, (H, C), dtype=jnp.float32) * scale
        bias = jnp.zeros((H * C,), dtype=jnp.float32)
        return {'x': x, 'edge_index': edge_index, 'W_src': W_src, 'attn_src': attn_src, 'attn_dst': attn_dst, 'bias': bias}
    _L2_gnn_all = _L2_gnn_setup()
    _L2_gnn_in = {k: v for k, v in _L2_gnn_all.items() if k in ('W_src', 'attn_src', 'attn_dst', 'bias')}
    del _L2_gnn_all

    def _L3_gnn_setup():
        import jax, jax.numpy as jnp
        import numpy as np
        N_NODES = 50000
        N_EDGES = 9375
        D = 128
        D_OUT = 128
        key = jax.random.key(seed)
        ks = jax.random.split(key, 6)
        features = jax.random.normal(ks[0], (N_NODES, D), dtype=jnp.float32)
        edge_index = jax.random.randint(ks[1], (2, N_EDGES), 0, N_NODES, dtype=jnp.int64)

        def xavier(k, shape):
            gain = float(np.sqrt(2.0))
            fan_out, fan_in = shape
            bound = gain * float(np.sqrt(6.0 / (fan_in + fan_out)))
            return jax.random.uniform(k, shape, jnp.float32, -bound, bound)
        W_neigh = xavier(ks[2], (D, D))
        b_neigh = jnp.zeros((D,), jnp.float32)
        W_edge = xavier(ks[3], (D, 2 * D))
        b_edge = jnp.zeros((D,), jnp.float32)
        W_lin = xavier(ks[4], (D_OUT, 2 * D))
        b_lin = jnp.zeros((D_OUT,), jnp.float32)
        return {'features': features, 'edge_index': edge_index, 'W_neigh': W_neigh, 'b_neigh': b_neigh, 'W_edge': W_edge, 'b_edge': b_edge, 'W_lin': W_lin, 'b_lin': b_lin}
    _L3_gnn_all = _L3_gnn_setup()
    _L3_gnn_in = {k: v for k, v in _L3_gnn_all.items() if k in ('W_neigh', 'b_neigh', 'W_edge', 'b_edge', 'W_lin', 'b_lin')}
    del _L3_gnn_all
    return {'x': x, 'src': src, 'dst': dst, 'edge_type_100': edge_type_100, 'L0_gnn_Ws': _L0_gnn_in['Ws'], 'L0_gnn_att_src': _L0_gnn_in['att_src'], 'L0_gnn_att_dst': _L0_gnn_in['att_dst'], 'L0_gnn_bias': _L0_gnn_in['bias'], 'L1_gnn_basis_weights': _L1_gnn_in['basis_weights'], 'L1_gnn_coefficients': _L1_gnn_in['coefficients'], 'L1_gnn_loop_weight': _L1_gnn_in['loop_weight'], 'L2_gnn_W_src': _L2_gnn_in['W_src'], 'L2_gnn_attn_src': _L2_gnn_in['attn_src'], 'L2_gnn_attn_dst': _L2_gnn_in['attn_dst'], 'L2_gnn_bias': _L2_gnn_in['bias'], 'L3_gnn_W_neigh': _L3_gnn_in['W_neigh'], 'L3_gnn_b_neigh': _L3_gnn_in['b_neigh'], 'L3_gnn_W_edge': _L3_gnn_in['W_edge'], 'L3_gnn_b_edge': _L3_gnn_in['b_edge'], 'L3_gnn_W_lin': _L3_gnn_in['W_lin'], 'L3_gnn_b_lin': _L3_gnn_in['b_lin']}

def reference(x, src, dst, edge_type_100, L0_gnn_Ws, L0_gnn_att_src, L0_gnn_att_dst, L0_gnn_bias, L1_gnn_basis_weights, L1_gnn_coefficients, L1_gnn_loop_weight, L2_gnn_W_src, L2_gnn_attn_src, L2_gnn_attn_dst, L2_gnn_bias, L3_gnn_W_neigh, L3_gnn_b_neigh, L3_gnn_W_edge, L3_gnn_b_edge, L3_gnn_W_lin, L3_gnn_b_lin):
    import jax
    import jax.numpy as jnp

    def _L0_gnn_ref(x, edge_index, Ws, att_src, att_dst, bias):
        import jax, jax.numpy as jnp
        import numpy as np
        NEG_SLOPE = 0.2
        EPS = 1e-16
        N_NODES = 100000
        N_EDGES = 25000
        CHANNELS = 128
        M_LAYERS = 3

        def _gat_conv(x, src, dst, W, a_src, a_dst, b, n_nodes):
            h = x @ W
            s = h @ a_src
            d = h @ a_dst
            e = s[src] + d[dst]
            e = jnp.where(e > 0, e, NEG_SLOPE * e)
            e_max = jax.ops.segment_max(e, dst, num_segments=n_nodes)
            e_max = jnp.where(jnp.isfinite(e_max), e_max, 0.0)
            w = jnp.exp(e - e_max[dst])
            denom = jax.ops.segment_sum(w, dst, num_segments=n_nodes)
            alpha = w / (denom[dst] + EPS)
            out = jax.ops.segment_sum(alpha[:, None] * h[src], dst, num_segments=n_nodes)
            return out + b
        n = x.shape[0]
        loop = jnp.arange(n, dtype=edge_index.dtype)
        src = jnp.concatenate([edge_index[0], loop])
        dst = jnp.concatenate([edge_index[1], loop])
        for m in range(Ws.shape[0]):
            x = x + jax.nn.sigmoid(_gat_conv(x, src, dst, Ws[m], att_src[m], att_dst[m], bias[m], n))
        return x

    def _L1_gnn_ref(h, norm, src, dst, rel_type, basis_weights, coefficients, loop_weight):
        import jax, jax.numpy as jnp
        import numpy as np
        N_NODES = 50000
        N_EDGES = 12500
        IN_DIM = 128
        OUT_DIM = 128
        NUM_RELS = 100
        NUM_BASES = 4
        n_nodes = h.shape[0]
        num_bases = basis_weights.shape[0]
        loop_message = h @ loop_weight
        hb = jnp.einsum('ni,bio->bno', h, basis_weights)
        c_e = coefficients[rel_type]
        msg = c_e[:, 0, None] * hb[0][src]
        for b in range(1, num_bases):
            msg = msg + c_e[:, b, None] * hb[b][src]
        agg = jax.ops.segment_sum(msg, dst, num_segments=n_nodes)
        node_repr = agg * norm
        node_repr = node_repr + loop_message
        return jax.nn.relu(node_repr)

    def _L2_gnn_ref(x, edge_index, W_src, attn_src, attn_dst, bias):
        import jax, jax.numpy as jnp
        import numpy as np
        N, E, F_IN, H, C = (100000, 25000, 128, 8, 16)
        NEG_SLOPE = 0.2
        n = x.shape[0]
        loops = jnp.tile(jnp.arange(n, dtype=edge_index.dtype)[None, :], (2, 1))
        ei = jnp.concatenate([edge_index, loops], axis=1)
        src, dst = (ei[0], ei[1])
        h = (x @ W_src).reshape(n, H, C)
        a_src = (h * attn_src[None]).sum(-1)
        a_dst = (h * attn_dst[None]).sum(-1)
        e = a_src[src] + a_dst[dst]
        e = jnp.where(e >= 0, e, NEG_SLOPE * e)
        seg_max = jax.ops.segment_max(e, dst, num_segments=n)
        ex = jnp.exp(e - seg_max[dst])
        denom = jax.ops.segment_sum(ex, dst, num_segments=n)
        alpha = ex / denom[dst]
        msg = h[src] * alpha[..., None]
        out = jax.ops.segment_sum(msg, dst, num_segments=n)
        out = out.reshape(n, H * C) + bias
        return out

    def _L3_gnn_ref(features, edge_index, W_neigh, b_neigh, W_edge, b_edge, W_lin, b_lin):
        import jax, jax.numpy as jnp
        import numpy as np
        N_NODES = 50000
        N_EDGES = 9375
        D = 128
        D_OUT = 128
        n = features.shape[0]
        dst = edge_index[0]
        src = edge_index[1]
        h = features @ W_neigh.T + b_neigh
        h_src = h[src]
        edge_feats = jnp.abs(h[dst] - h_src)
        new_h = jnp.concatenate([h_src, edge_feats], axis=-1) @ W_edge.T + b_edge
        seg_sum = jax.ops.segment_sum(new_h, dst, num_segments=n)
        cnt = jax.ops.segment_sum(jnp.ones((dst.shape[0],), jnp.float32), dst, num_segments=n)[:, None]
        s = (h + seg_sum) / jnp.maximum(cnt, 1.0)
        z = jnp.concatenate([features, s], axis=-1) @ W_lin.T + b_lin
        return z
    edge_index = jnp.stack([src, dst])
    deg = jnp.maximum(jax.ops.segment_sum(jnp.ones(dst.shape, jnp.float32), dst, num_segments=50000), 1.0)
    deg_isqrt = deg ** (-0.5)
    h = jnp.maximum(_layernorm(x, axis=-1), 0.0)
    x = x + _L0_gnn_ref(h, edge_index, L0_gnn_Ws, L0_gnn_att_src, L0_gnn_att_dst, L0_gnn_bias)
    h = jnp.maximum(_layernorm(x, axis=-1), 0.0)
    x = x + _L1_gnn_ref(h, deg_isqrt[:, None], src, dst, edge_type_100, L1_gnn_basis_weights, L1_gnn_coefficients, L1_gnn_loop_weight)
    h = jnp.maximum(_layernorm(x, axis=-1), 0.0)
    x = x + _L2_gnn_ref(h, edge_index, L2_gnn_W_src, L2_gnn_attn_src, L2_gnn_attn_dst, L2_gnn_bias)
    h = jnp.maximum(_layernorm(x, axis=-1), 0.0)
    x = x + _L3_gnn_ref(h, edge_index, L3_gnn_W_neigh, L3_gnn_b_neigh, L3_gnn_W_edge, L3_gnn_b_edge, L3_gnn_W_lin, L3_gnn_b_lin)
    return x

_drawn_inputs = setup_inputs


def setup_inputs(seed=0):
    import zlib

    import numpy as np

    out = dict(_drawn_inputs(seed))
    spreads = {'L0_gnn_bias': (0.0, 0.506),
     'L2_gnn_bias': (0.0, 0.1),
     'L3_gnn_b_neigh': (0.0, 0.1),
     'L3_gnn_b_edge': (0.0, 0.581),
     'L3_gnn_b_lin': (0.0, 0.3)}
    factors = {'L0_gnn_att_src': 6.627,
     'L0_gnn_att_dst': 8.0,
     'L2_gnn_attn_src': 4.586,
     'L2_gnn_attn_dst': 8.0}
    for name, (base, spread) in spreads.items():
        noise = np.random.default_rng([zlib.crc32(name.encode()), seed]).standard_normal(out[name].shape)
        drawn = base * np.exp(spread * noise) if base else spread * noise
        out[name] = jnp.asarray(drawn.astype(out[name].dtype))
    for name, factor in factors.items():
        out[name] = (out[name] * factor).astype(out[name].dtype)
    return out
```

```python
import concourse.bass as bass
from concourse import mybir
from contextlib import ExitStack, contextmanager

F32 = mybir.dt.float32
I32 = mybir.dt.int32
ALU = mybir.AluOpType
ACT = mybir.ActivationFunctionType
AX = mybir.AxisListType

N = 50000
C = 128
E = 12500
P = 128
BIG = 1.0e30
LN_EPS = 1e-5
GAT_EPS = 1e-16
SLOPE = 0.2
HEADS = 8
BASES = 4


class Phase(ExitStack):

    def __init__(self, nc):
        super().__init__()
        self.nc, self.semaphores = nc, []

    def semaphore(self, name):
        self.semaphores.append(self.nc.alloc_semaphore(name))
        return self.semaphores[-1]


@contextmanager
def phase(nc):
    with Phase(nc) as ctx:
        yield ctx
    nc.clear_and_free_semaphores(ctx.semaphores)
    nc.all_engine_barrier()


def carry_waits(eng, w):
    eng.sem_inc(w["carrier"], 1)


def wait(eng, sem, value):
    if not (isinstance(value, int) and value <= 0):
        eng.wait_ge(sem, value)


def rounds(eng, n):
    yield 0
    if n > 1:
        with eng.Fori(1, n) as i:
            yield i


def local_chain(nc, x, out, w, G, rounds_n):
    J = 4
    W = J * C
    x_v = x.rearrange("(a j) c -> a (j c)", j=J)
    out_v = out.rearrange("(a j) c -> a (j c)", j=J)
    last_row = (N - P * J) // J

    with phase(nc) as ctx:
        sb = lambda n, s: ctx.enter_context(nc.sbuf_tensor(n, s, F32))
        sem = lambda n: ctx.semaphore(n)
        X = sb("a_x", [P, G, W])
        XB = sb("a_xb", [P, G, W])
        NR = sb("a_nr", [P, G, W])
        HT = sb("a_ht", [P, G, W])
        SG = sb("a_sg", [P, 3, W])
        ST = sb("a_st", [P, G, J, 6])
        MV = sb("a_mv", [P, G, J, 2])
        VE = sb("a_ve", [P, G, J])
        RS = sb("a_rs", [P, G, J])
        PT = [ctx.enter_context(nc.psum_tensor(f"a_pt{k}", [P, W], F32)) for k in range(4)]
        PM = [ctx.enter_context(nc.psum_tensor(f"a_pm{k}", [P, W], F32)) for k in range(4)]

        loaded = [sem(f"a_loaded{g}") for g in range(G)]
        stored = [sem(f"a_stored{g}") for g in range(G)]
        s_st = sem("a_stats")
        s_mv = sem("a_moments")
        s_ve = sem("a_var_eps")
        s_rs = sem("a_rstd")
        s_nr = sem("a_normed")
        s_tp = sem("a_transposed")
        s_ht = sem("a_ht_ready")
        s_mm = sem("a_product")
        s_sg = sem("a_sigmoid")
        s_h = sem("a_h_updated")
        s_bk = sem("a_back")
        s_lm = sem("a_layer_product")
        s_xb = sem("a_x_biased")
        s_x = sem("a_x_updated")

        def at(i, per_round, k, g):
            return (i * per_round + k) * G + g + 1

        block = ctx.enter_context(nc.Block())

        def row0(i, g):
            if isinstance(i, int):
                return min((i * G + g) * P, last_row)
            return None

        @block.sync
        def _(eng):
            n_chunks = rounds_n * G
            assert (n_chunks - 1) * P <= last_row + P

            def load(i, g, start):
                wait(eng, stored[g], i * 16)
                eng.dma_start(X[:, g, :], x_v[bass.ds(start, P), :]).then_inc(loaded[g], 16)

            def store(i, g, start):
                eng.wait_ge(s_x, at(i, 4, 3, g))
                eng.dma_start(out_v[bass.ds(start, P), :], X[:, g, :]).then_inc(stored[g], 16)

            for g in range(G):
                load(0, g, g * P)
            if rounds_n > 2:
                with eng.Fori(0, rounds_n - 2) as i:
                    for g in range(G):
                        store(i, g, (i * G + g) * P)
                        eng.wait_ge(stored[g], (i + 1) * 16)
                        eng.dma_start(X[:, g, :], x_v[bass.ds((i * G + G + g) * P, P), :]).then_inc(loaded[g], 16)
            i = rounds_n - 2
            for g in range(G):
                store(i, g, (i * G + g) * P)
                load(i + 1, g, row0(i + 1, g))
            for g in range(G):
                if g == G - 1:
                    eng.wait_ge(stored[g - 1], rounds_n * 16)
                store(rounds_n - 1, g, row0(rounds_n - 1, g))
            for g in range(G):
                eng.wait_ge(stored[g], rounds_n * 16)

        @block.vector
        def _(eng):
            for i in rounds(eng, rounds_n):
                def norm(k):
                    for g in range(G):
                        if k == 0:
                            eng.wait_ge(loaded[g], (i + 1) * 16)
                        else:
                            eng.wait_ge(s_x, at(i, 4, k - 1, g))
                        for j in range(J):
                            nc.vector.bn_stats(ST[:, g, j, :], X[:, g, j * C:(j + 1) * C]).then_inc(s_st, 1)
                        if g:
                            aggregate(k, g - 1)
                    aggregate(k, G - 1)
                    for g in range(G):
                        eng.wait_ge(s_rs, at(i, 4, k, g))
                        wait(eng, s_tp, at(i, 4, k, g) - G)
                        for j in range(J):
                            nc.vector.tensor_scalar(NR[:, g, j * C:(j + 1) * C], X[:, g, j * C:(j + 1) * C],
                                                    MV[:, g, j, 0:1], RS[:, g, j:j + 1],
                                                    ALU.subtract, ALU.mult).then_inc(s_nr, 1)

                def aggregate(k, g):
                    eng.wait_ge(s_st, at(i, 4, k, g) * J)
                    carry_waits(eng, w)
                    for j in range(J):
                        nc.vector.bn_aggr(MV[:, g, j, :], ST[:, g, j, :]).then_inc(s_mv, 1)

                norm(0)
                for r in range(3):
                    for g in range(G):
                        eng.wait_ge(s_sg, at(i, 3, r, g))
                        nc.vector.tensor_tensor(HT[:, g, :], HT[:, g, :], SG[:, (r * G + g) % 3, :], ALU.add).then_inc(s_h, 1)
                for g in range(G):
                    eng.wait_ge(s_bk, at(i, 1, 0, g))
                    nc.vector.tensor_tensor(X[:, g, :], PT[g % 4][:, :], X[:, g, :], ALU.add).then_inc(s_x, 1)
                norm(1)
                for g in range(G):
                    eng.wait_ge(s_lm, at(i, 3, 0, g))
                    nc.vector.scalar_tensor_tensor(X[:, g, :], PM[g % 4][:, :], 0.0, X[:, g, :],
                                                   ALU.max, ALU.add).then_inc(s_x, 1)
                for k in (2, 3):
                    norm(k)
                    for g in range(G):
                        eng.wait_ge(s_lm, at(i, 3, k - 1, g))
                        eng.wait_ge(s_xb, at(i, 2, k - 2, g))
                        nc.vector.tensor_tensor(X[:, g, :], PM[g % 4][:, :], XB[:, g, :], ALU.add).then_inc(s_x, 1)

        @block.gpsimd
        def _(eng):
            for i in rounds(eng, rounds_n):
                for k in range(4):
                    for g in range(G):
                        eng.wait_ge(s_mv, at(i, 4, k, g) * J)
                        nc.gpsimd.tensor_tensor(VE[:, g, :], MV[:, g, :, 1], w["ln_eps"][:, 0:J], ALU.add).then_inc(s_ve, 1)
                        eng.wait_ge(s_ve, at(i, 4, k, g))
                        nc.gpsimd.tensor_tensor(RS[:, g, :], VE[:, g, :], w["neg_half"][:, 0:J], ALU.pow).then_inc(s_rs, 1)
                    if k >= 2:
                        for g in range(G):
                            nc.gpsimd.tensor_tensor(XB[:, g, :].rearrange("p (j c) -> p j c", j=J),
                                                    X[:, g, :].rearrange("p (j c) -> p j c", j=J),
                                                    w["bias_rows"][k - 2][:, None, :].to_broadcast([P, J, C]), ALU.add).then_inc(s_xb, 1)

        @block.scalar
        def _(eng):
            for i in rounds(eng, rounds_n):
                def relu(k):
                    for g in range(G):
                        eng.wait_ge(s_tp, at(i, 4, k, g))
                        if k == 0:
                            wait(eng, s_lm, at(i, 3, 2, g) - 3 * G)
                        elif k == 1:
                            eng.wait_ge(s_bk, at(i, 1, 0, g))
                        else:
                            eng.wait_ge(s_lm, at(i, 3, k - 2, g))
                        nc.scalar.activation(HT[:, g, :], PT[g % 4][:, :], ACT.Relu).then_inc(s_ht, 1)

                relu(0)
                for r in range(3):
                    for g in range(G):
                        eng.wait_ge(s_mm, at(i, 3, r, g))
                        wait(eng, s_h, at(i, 3, r, g) - 3)
                        nc.scalar.activation(SG[:, (r * G + g) % 3, :], PM[g % 4][:, :], ACT.Sigmoid,
                                             bias=w["b0_cols"][:, r:r + 1]).then_inc(s_sg, 1)
                relu(1)
                relu(2)
                relu(3)

        @block.tensor
        def _(eng):
            for i in rounds(eng, rounds_n):
                def transposes(k):
                    for g in range(G):
                        eng.wait_ge(s_nr, at(i, 4, k, g) * J)
                        if g >= 4:
                            eng.wait_ge(s_ht, at(i, 4, k, g - 4))
                        elif k == 1:
                            eng.wait_ge(s_x, at(i, 4, 0, G - 1))
                        else:
                            wait(eng, s_ht, at(i, 4, k - 1, G - 1))
                        for j in range(J):
                            last = nc.tensor.transpose(PT[g % 4][:, j * C:(j + 1) * C], NR[:, g, j * C:(j + 1) * C],
                                                       w["ident"][:, :])
                        last.then_inc(s_tp, 1)

                def layer(k, rhs):
                    for g in range(G):
                        eng.wait_ge(s_ht, at(i, 4, k, g))
                        if g >= 4:
                            eng.wait_ge(s_x, at(i, 4, k, g - 4))
                        elif k == 1:
                            eng.wait_ge(s_sg, at(i, 3, 2, G - 1))
                        else:
                            eng.wait_ge(s_x, at(i, 4, k - 1, G - 1))
                        for j in range(J):
                            last = nc.tensor.matmul(PM[g % 4][:, j * C:(j + 1) * C], HT[:, g, j * C:(j + 1) * C],
                                                    rhs, start=True, stop=True)
                        last.then_inc(s_lm, 1)

                transposes(0)
                for r in range(3):
                    for g in range(G):
                        if r == 0:
                            eng.wait_ge(s_ht, at(i, 4, 0, g))
                        else:
                            eng.wait_ge(s_h, at(i, 3, r - 1, g))
                        if g >= 4:
                            eng.wait_ge(s_sg, at(i, 3, r, g - 4))
                        elif r:
                            eng.wait_ge(s_sg, at(i, 3, r - 1, G - 1))
                        else:
                            wait(eng, s_x, at(i, 4, 3, G - 1) - 4 * G)
                        nc.tensor.matmul(PM[g % 4][:, :], w["aug0"][:, r, 0:C], HT[:, g, :],
                                         start=True, stop=True).then_inc(s_mm, 1)
                for g in range(G):
                    eng.wait_ge(s_h, at(i, 3, 2, g))
                    if g >= 4:
                        eng.wait_ge(s_x, at(i, 4, 0, g - 4))
                    for j in range(J):
                        last = nc.tensor.transpose(PT[g % 4][:, j * C:(j + 1) * C], HT[:, g, j * C:(j + 1) * C],
                                                   w["ident"][:, :])
                    last.then_inc(s_bk, 1)
                transposes(1)
                layer(1, w["loop"][:, :])
                transposes(2)
                layer(2, w["aug2"][:, 0:C])
                transposes(3)
                layer(3, w["fused3"][:, :])


def setup(nc, w, ins):
    with phase(nc) as ctx:
        sb = lambda n, s: ctx.enter_context(nc.sbuf_tensor(n, s, F32))
        sem = lambda n: ctx.semaphore(n)
        W0T = sb("s_w0t", [P, 3, C])
        W2T = sb("s_w2t", [P, C])
        A0 = sb("s_a0", [P, 3, 2])
        AC = sb("s_ac", [P, 2])
        A2 = sb("s_a2", [P, 2, HEADS])
        WN = sb("s_wn", [P, C])
        BNC = sb("s_bnc", [P, 1])
        BNB = sb("s_bnb", [P, C])
        PS = ctx.enter_context(nc.psum_tensor("s_ps", [P, 512], F32))
        PB = ctx.enter_context(nc.psum_tensor("s_pb", [P, 512], F32))

        s_in = sem("s_in")
        s_pool = sem("s_pool")
        s_a2 = sem("s_a2col")
        s_heads = sem("s_heads")
        s_pe = sem("s_pe")
        s_dve = sem("s_dve")

        block = ctx.enter_context(nc.Block())
        loads = [
            (w["aug0"][:, :, 0:C], ins["L0_Ws"].rearrange("r i o -> i r o")),
            (W0T[:, :, :], ins["L0_WsT"].rearrange("r o i -> o r i")),
            (A0[:, :, 0], ins["L0_as"]), (A0[:, :, 1], ins["L0_ad"]),
            (w["b0_cols"][:, :], ins["L0_bT"]),
            (w["loop"][:, :], ins["L1_loop"]),
            (w["basis"][:, :, :], ins["L1_basis"].rearrange("b i o -> i b o")),
            (w["aug2"][:, 0:C], ins["L2_W"]), (W2T[:, :], ins["L2_WT"]),
            (AC[:, 0:1], ins["L2_as"]), (AC[:, 1:2], ins["L2_ad"]),
            (WN[:, :], ins["L3_Wn"]), (w["wnT"][:, :], ins["L3_WnT"]),
            (BNC[:, :], ins["L3_bn"]), (w["bn_col"][:, :], ins["L3_bn"]),
            (w["weT"][:, :, :], ins["L3_WeT"].rearrange("(h c) o -> c h o", h=2)),
            (w["wlT"][:, :, :], ins["L3_WlT"].rearrange("(h c) o -> c h o", h=2)),
            (w["bias_rows"][0][:, :], ins["L2_b"].to_broadcast([P, C])),
            (w["bl_row"][:, :], ins["L3_bl"].to_broadcast([P, C])),
            (w["be_row"][:, :], ins["L3_be"].to_broadcast([P, C])),
        ]
        for r in range(3):
            loads.append((w["b0_rows"][:, r, :], ins["L0_b"][r:r + 1, :].to_broadcast([P, C])))

        @block.sync
        def _(eng):
            for dst, src in loads:
                with nc.allow_non_contiguous_dma(reason="small weights"):
                    eng.dma_start(dst, src).then_inc(s_in, 16)

        @block.gpsimd
        def _(eng):
            nc.gpsimd.memset(w["ident"][:, :], 0.0).then_inc(s_pool, 1)
            nc.gpsimd.memset(w["ones"][:, :], 1.0).then_inc(s_pool, 1)
            nc.gpsimd.memset(w["ln_eps"][:, :], LN_EPS).then_inc(s_pool, 1)
            nc.gpsimd.memset(w["neg_half"][:, :], -0.5).then_inc(s_pool, 1)
            eng.wait_ge(s_pool, 4)
            nc.gpsimd.affine_select(out=w["ident"][:, :], in_=w["ident"][:, :], compare_op=ALU.not_equal, fill=1.0,
                                    base=0, pattern=[[-1, P]], channel_multiplier=1).then_inc(s_pool, 1)
            eng.wait_ge(s_a2, 3)
            nc.gpsimd.affine_select(out=A2[:, :, :], in_=A2[:, :, :], compare_op=ALU.is_ge, fill=0.0,
                                    base=0, pattern=[[0, 2], [-(C // HEADS), HEADS]], channel_multiplier=1).then_inc(s_heads, 1)
            eng.wait_ge(s_heads, 1)
            nc.gpsimd.affine_select(out=A2[:, :, :], in_=A2[:, :, :], compare_op=ALU.is_ge, fill=0.0,
                                    base=C // HEADS - 1, pattern=[[0, 2], [C // HEADS, HEADS]], channel_multiplier=-1).then_inc(s_heads, 1)

        @block.vector
        def _(eng):
            eng.wait_ge(s_in, 16 * len(loads))
            eng.wait_ge(s_pool, 5)
            nc.vector.tensor_scalar(A2[:, 0, :], w["ones"][:, 0:HEADS], AC[:, 0:1], None, ALU.mult).then_inc(s_a2, 1)
            nc.vector.tensor_scalar(A2[:, 1, :], w["ones"][:, 0:HEADS], AC[:, 1:2], None, ALU.mult).then_inc(s_a2, 1)
            nc.vector.tensor_scalar(BNB[:, :], w["ones"][:, :], BNC[:, 0:1], None, ALU.mult).then_inc(s_a2, 1)
            eng.wait_ge(s_pe, 1)
            nc.vector.tensor_copy(w["aug0"][:, :, C:C + 2], PS[:, 0:6].rearrange("p (r a) -> p r a", r=3)).then_inc(s_dve, 1)
            nc.vector.tensor_copy(w["aug2"][:, C:C + 2 * HEADS], PS[:, 16:16 + 2 * HEADS]).then_inc(s_dve, 1)
            nc.vector.tensor_tensor(w["fused3"][:, :], PB[:, 0:C], w["wlT"][:, 0, :], ALU.add).then_inc(s_dve, 1)
            nc.vector.tensor_tensor(w["bias_rows"][1][:, :], PB[:, C:2 * C], w["bl_row"][:, :], ALU.add).then_inc(s_dve, 1)

        @block.tensor
        def _(eng):
            eng.wait_ge(s_in, 16 * len(loads))
            eng.wait_ge(s_heads, 2)
            for r in range(3):
                nc.tensor.matmul(PS[:, 2 * r:2 * r + 2], W0T[:, r, :], A0[:, r, :], start=True, stop=True)
            nc.tensor.matmul(PS[:, 16:16 + 2 * HEADS], W2T[:, :], A2[:, :, :].rearrange("p a h -> p (a h)"), start=True, stop=True)
            nc.tensor.matmul(PB[:, 0:C], WN[:, :], w["wlT"][:, 1, :], start=True, stop=True)
            nc.tensor.matmul(PB[:, C:2 * C], BNB[:, :], w["wlT"][:, 1, :], start=True, stop=True).then_inc(s_pe, 1)


def alloc_weights(nc, ctx):
    sb = lambda n, s: ctx.enter_context(nc.sbuf_tensor("w_" + n, s, F32))
    w = {
        "carrier": ctx.enter_context(nc.semaphore("carrier")),
        "ident": sb("ident", [P, P]), "ones": sb("ones", [P, P]), "neg_half": sb("neg_half", [P, 8]), "ln_eps": sb("ln_eps", [P, 8]),
        "aug0": sb("aug0", [P, 3, C + 2]), "b0_cols": sb("b0_cols", [P, 3]), "b0_rows": sb("b0_rows", [P, 3, C]),
        "loop": sb("loop", [P, C]), "basis": sb("basis", [P, BASES, C]),
        "aug2": sb("aug2", [P, C + 2 * HEADS]),
        "wnT": sb("wnT", [P, C]), "bn_col": sb("bn_col", [P, 1]),
        "weT": sb("weT", [P, 2, C]), "wlT": sb("wlT", [P, 2, C]), "fused3": sb("fused3", [P, C]),
        "bl_row": sb("bl_row", [P, C]), "be_row": sb("be_row", [P, C]),
        "bias_rows": [sb("b2_row", [P, C]), sb("b3_row", [P, C])],
    }
    return w


T = 100
EP = T * P
J = 4
GE = 5
BLOCKS = T // J
ROUNDS_E = BLOCKS // GE
SKIP = 200000
DUMP = EP
FULL_ROWS = E // P
TAIL = E - FULL_ROWS * P


def alloc_keys(nc, ctx, w):
    sb = lambda n, s, d=F32: ctx.enter_context(nc.sbuf_tensor("k_" + n, s, d))
    k = {
        "dst_col": sb("dst_col", [P, T]), "src_col": sb("src_col", [P, T]), "prev_col": sb("prev_col", [P, T]),
        "src_ix": sb("src_ix", [P, T], I32), "dst_ix": sb("dst_ix", [P, T], I32),
        "map_ix": sb("map_ix", [P, T], I32),
        "hold_ix": sb("hold_ix", [P, T], I32),
        "acc_ix": sb("acc_ix", [P, T], I32),
        "out_d_ix": sb("out_d_ix", [P, T], I32), "out_s_ix": sb("out_s_ix", [P, T], I32),
        "coef": sb("coef", [P, T, BASES]),
        "is_last": sb("is_last", [T, P]), "last_pen": sb("last_pen", [T, P]),
        "pre_pen": sb("pre_pen", [T, P]), "post": sb("post", [T, P]),
        "pen0": sb("pen0", [T, HEADS, P]), "nl0": sb("nl0", [T, HEADS, P]),
        "row_pen": sb("row_pen", [HEADS, T]), "row_nl": sb("row_nl", [HEADS, T]),
    }
    return k


def alloc_tables(nc):
    d = lambda n, s, t=F32: nc.dram_tensor("t_" + n, s, t).ap()
    t = {"dst_pad": d("dst_pad", (EP + 2, 1)), "src_row": d("src_row", (1, EP)), "type_row": d("type_row", (1, EP)),
         "dst_row": d("dst_row", (1, EP)),
         "maps": d("maps", (50048 * 2, 1), I32), "dout": d("dout", (EP, C)), "sz": d("sz", (EP, C)),
         "gt": d("gt", (BLOCKS * P, J * C)),
         "xs": d("xs", (EP, C)), "xd": d("xd", (EP, C))}
    for r in range(6):
        t[f"s{r}"] = d(f"s{r}", (EP, C))
        t[f"d{r}"] = d(f"d{r}", (EP, C))
    for a in range(J):
        t[f"acc{a}"] = d(f"acc{a}", (EP + P, C + 1))
    return t


def keys(nc, w, k, t, ins):
    with phase(nc) as ctx:
        sb = lambda n, s, d=F32: ctx.enter_context(nc.sbuf_tensor("q_" + n, s, d))
        sem = lambda n: ctx.semaphore("q_" + n)
        RI = sb("ri", [T, 3, P], I32)
        RF = sb("rf", [T, 3, P])
        PN = sb("pn", [T, 2, P])
        FF = sb("ff", [T, P])
        FR = sb("fr", [T, P])
        LR = sb("lr", [T, P])
        ZERO = sb("zero", [T, P])
        ENDS = sb("ends", [2, 1])
        ENDS_I = sb("ends_i", [2, 1], I32)
        MI = sb("mi", [P, T], I32)
        LASTP = sb("lastp", [P, 1])
        s_cf_pe = sem("cf_pe")
        s_loop = sem("loop")
        ID = sb("id", [P, T], I32)
        IR = sb("ir", [T, P], I32)
        IRF = sb("irf", [T, P])
        HV = sb("hv", [T, P])
        HL = sb("hl", [T, P])
        HX = sb("hx", [T, P])
        ROW8 = sb("row8", [T, 2, HEADS])
        HC = sb("hc", [1, T])
        HS = sb("hs", [1, T])
        HO = sb("ho", [T, 1])
        LC = sb("lc", [P, T])
        TL = sb("tl", [P, T])
        OWN = sb("own", [P, T])
        TMP = sb("tmp", [P, T])
        DUP = sb("dup", [P, J])
        TMQ = sb("tmq", [P, T])
        IDF = sb("idf", [P, T])
        DUMPC = sb("dumpc", [P, 1], I32)
        DUMPF = sb("dumpf", [P, 1])
        M1 = sb("m1", [P, T], I32)
        M2 = sb("m2", [P, T], I32)
        MG = sb("mg", [P, T, 2], I32)
        MGF = sb("mgf", [P, T, 2])
        KEEP = sb("keep", [P, 50048 * 2 // P], I32)
        UPPER = sb("upper", [P, P])
        SB_ = sb("sbc", [P, 2, J * P])
        EQ = sb("eq", [P, J, P])
        TB = sb("tb", [P, 2, J * P])
        OH = sb("oh", [P, 2, J * P])
        RELI = sb("reli", [P, 1], I32)
        RELF = sb("relf", [P, 1])
        COEF = sb("coefs", [100, BASES])
        ZT = sb("zt", [P, (EP + P) * (C + 1) // P // 3])
        PS = ctx.enter_context(nc.psum_tensor("q_ps", [P, 512], F32))
        PQ = ctx.enter_context(nc.psum_tensor("q_pq", [P, 512], F32))
        PC = ctx.enter_context(nc.psum_tensor("q_pc", [P, 512], F32))

        s_fill, s_in, s_rf, s_pad, s_pn, s_v, s_pe, s_pool = (sem(n) for n in "fill in rf pad pn v pe pool".split())
        s_map1, s_map2, s_mg, s_zero, s_ix, s_coef_in = (sem(n) for n in "map1 map2 mg zero ix coef_in".split())
        s_tb = [sem(f"tb{b}") for b in range(2)]
        s_eq, s_tl, s_oh, s_cf, s_keep, s_shape = (sem(n) for n in "eq tl oh cf keep shape".split())
        block = ctx.enter_context(nc.Block())
        ident_t = w["ident"][0:T, 0:T]
        ZN = 3

        @block.sync
        def _(eng):
            eng.wait_ge(s_fill, 3)
            for n, name in enumerate(("dst", "src", "etype")):
                v = ins[name]
                eng.dma_start(RI[0:FULL_ROWS, n, :], v[0:FULL_ROWS * P].rearrange("(t p) -> t p", p=P)).then_inc(s_in, 16)
                eng.dma_start(RI[FULL_ROWS:FULL_ROWS + 1, n, 0:TAIL], v[FULL_ROWS * P:E].rearrange("(o p) -> o p", o=1)).then_inc(s_in, 16)
            eng.dma_start(COEF[:, :], ins["L1_coef"]).then_inc(s_coef_in, 16)
            eng.dma_start(t["maps"].rearrange("(p n) o -> p (n o)", p=P), KEEP[:, :]).then_inc(s_keep, 16)
            eng.wait_ge(s_rf, 1)
            rows = lambda x: x.rearrange("o (t p) -> (o t) p", p=P)
            eng.dma_start(rows(t["dst_row"]), RF[:, 0, :]).then_inc(s_pad, 16)
            eng.dma_start(rows(t["src_row"]), RF[:, 1, :]).then_inc(s_pad, 16)
            eng.dma_start(rows(t["type_row"]), RF[:, 2, :]).then_inc(s_pad, 16)
            eng.dma_start(t["dst_pad"][1:EP + 1, :].rearrange("(t p) o -> t (p o)", p=P), RF[:, 0, :]).then_inc(s_pad, 16)
            with nc.allow_non_contiguous_dma(reason="two words"):
                eng.dma_start(t["dst_pad"][0:EP + 2:EP + 1, :], ENDS[:, :]).then_inc(s_pad, 16)
            eng.wait_ge(s_pad, 80)
            eng.dma_start(PN[:, 0, :], t["dst_pad"][0:EP, :].rearrange("(t p) o -> t (p o)", p=P)).then_inc(s_pn, 16)
            eng.dma_start(PN[:, 1, :], t["dst_pad"][2:EP + 2, :].rearrange("(t p) o -> t (p o)", p=P)).then_inc(s_pn, 16)

            def rows_in(b, buf):
                eng.dma_start(SB_[:, buf, :], t["src_row"][0:1, bass.ds(b * J * P, J * P)].to_broadcast([P, J * P])).then_inc(s_tb[buf], 16)
                eng.dma_start(TB[:, buf, :], t["type_row"][0:1, bass.ds(b * J * P, J * P)].to_broadcast([P, J * P])).then_inc(s_tb[buf], 16)

            rows_in(0, 0)
            for i in rounds(eng, (BLOCKS - 1) // 2):
                for h in range(2):
                    b = i * 2 + h
                    wait(eng, s_tl, b)
                    rows_in(b + 1, 1 - h)
            for a in range(J):
                flat = t[f"acc{a}"].rearrange("(p n) c -> p (n c)", p=P)
                n = flat.shape[1] // ZN
                for z in range(ZN):
                    eng.dma_start(flat[:, z * n:(z + 1) * n], ZT[:, 0:n]).then_inc(s_zero, 16)
            eng.wait_ge(s_zero, 16 * ZN * J)

        @block.gpsimd
        def _(eng):
            nc.gpsimd.memset(RI[:, 0:2, :], N).then_inc(s_fill, 1)
            nc.gpsimd.memset(RI[:, 2:3, :], 0).then_inc(s_fill, 1)
            nc.gpsimd.memset(KEEP[:, :], SKIP).then_inc(s_fill, 1)
            nc.gpsimd.iota(ID[:, :], [[P, T]], base=0, channel_multiplier=1).then_inc(s_pool, 1)
            nc.gpsimd.iota(IR[:, :], [[1, P]], base=0, channel_multiplier=P).then_inc(s_pool, 1)
            nc.gpsimd.iota(DUMPC[:, :], [[1, 1]], base=DUMP, channel_multiplier=1).then_inc(s_pool, 1)
            nc.gpsimd.iota(RELI[:, :], [[1, 1]], base=0, channel_multiplier=1).then_inc(s_pool, 1)
            nc.gpsimd.affine_select(out=UPPER[:, :], in_=w["ones"][:, :], compare_op=ALU.is_gt, fill=0.0, base=0,
                                    pattern=[[1, P]], channel_multiplier=-1).then_inc(s_pool, 1)
            nc.gpsimd.iota(ENDS_I[:, :], [[1, 1]], base=-2, channel_multiplier=1).then_inc(s_pool, 1)
            eng.wait_ge(s_keep, 16)
            eng.wait_ge(s_ix, 1)
            for c in range(T):
                eng.indirect_dma_start(out=t["maps"], out_offset=bass.IndirectOffsetOnAxis(ap=M1[:, c:c + 1], axis=0),
                                       in_=ID[:, c:c + 1], in_offset=None, bounds_check=50048 * 2 - 1, oob_is_err=False).then_inc(s_map1, 16)
            eng.wait_ge(s_ix, 2)
            for c in range(T):
                if c:
                    eng.wait_ge(s_map2, 16 * c)
                eng.indirect_dma_start(out=t["maps"], out_offset=bass.IndirectOffsetOnAxis(ap=M2[:, c:c + 1], axis=0),
                                       in_=ID[:, c:c + 1], in_offset=None, bounds_check=50048 * 2 - 1, oob_is_err=False).then_inc(s_map2, 16)
            eng.wait_ge(s_map1, 16 * T)
            eng.wait_ge(s_map2, 16 * T)
            pairs = t["maps"].rearrange("(n a) o -> n (a o)", a=2)
            for c in range(T):
                eng.indirect_dma_start(out=MG[:, c, :], out_offset=None, in_=pairs,
                                       in_offset=bass.IndirectOffsetOnAxis(ap=MI[:, c:c + 1], axis=0),
                                       bounds_check=50047, oob_is_err=False).then_inc(s_mg, 16)

        @block.tensor
        def _(eng):
            eng.wait_ge(s_rf, 1)
            nc.tensor.transpose(PS[:, 0:T], RF[:, 0, :], ident_t).then_inc(s_pe, 1)
            nc.tensor.transpose(PS[:, 128:128 + T], RF[:, 1, :], ident_t).then_inc(s_pe, 1)
            eng.wait_ge(s_shape, 1)
            nc.tensor.transpose(PS[:, 256:256 + T], k["is_last"][:, :], ident_t).then_inc(s_pe, 1)
            nc.tensor.transpose(PQ[0:HEADS, 0:T], ROW8[:, 0, :], ident_t).then_inc(s_pe, 1)
            nc.tensor.transpose(PQ[0:HEADS, 128:128 + T], ROW8[:, 1, :], ident_t).then_inc(s_pe, 1)
            nc.tensor.transpose(PQ[0:1, 256:256 + T], HL[:, 0:1], ident_t).then_inc(s_pe, 1)
            eng.wait_ge(s_shape, 2)
            nc.tensor.transpose(PQ[0:T, 400:401], HS[0:1, :], w["ident"][0:1, 0:1]).then_inc(s_pe, 1)
            eng.wait_ge(s_shape, 3)
            nc.tensor.transpose(PS[:, 384:384 + T], HX[:, :], ident_t).then_inc(s_pe, 1)
            eng.wait_ge(s_coef_in, 16)
            for i in rounds(eng, BLOCKS):
                wait(eng, s_tl, i)
                eng.wait_ge(s_oh, i + 1)
                for j in range(J):
                    last = nc.tensor.matmul(PC[:, 4 * j:4 * j + 4], OH[0:100, 0, j * P:(j + 1) * P], COEF[:, :], start=True, stop=True)
                last.then_inc(s_cf_pe, 1)

        @block.vector
        def _(eng):
            n = [0]

            def done(ins_):
                n[0] += 1
                ins_.then_inc(s_v, 1)
                eng.wait_ge(s_v, n[0])

            v = nc.vector
            done(v.memset(ZERO[:, :], 0.0))
            done(v.memset(ZT[:, :], 0.0))
            eng.wait_ge(s_pool, 6)
            done(v.tensor_copy(ENDS[:, :], ENDS_I[:, :]))
            done(v.tensor_copy(IDF[:, :], ID[:, :]))
            done(v.tensor_copy(IRF[:, :], IR[:, :]))
            done(v.tensor_copy(DUMPF[:, :], DUMPC[:, :]))
            done(v.tensor_copy(RELF[:, :], RELI[:, :]))
            eng.wait_ge(s_in, 96)
            v.tensor_copy(RF[:, :, :], RI[:, :, :]).then_inc(s_rf, 1)
            eng.wait_ge(s_pn, 32)
            done(v.tensor_tensor(FF[:, :], RF[:, 0, :], PN[:, 0, :], ALU.not_equal))
            done(v.tensor_tensor(k["is_last"][:, :], RF[:, 0, :], PN[:, 1, :], ALU.not_equal))
            done(v.tensor_scalar(k["last_pen"][:, :], k["is_last"][:, :], -1.0, BIG, ALU.add, ALU.mult))
            done(v.tensor_tensor_scan(FR[:, :], ZERO[:, :], FF[:, :], 0.0, ALU.add, ALU.max))
            done(v.tensor_tensor_scan(LR[:, ::-1], ZERO[:, :], k["is_last"][:, ::-1], 0.0, ALU.add, ALU.max))
            done(v.tensor_scalar(k["pre_pen"][:, :], FR[:, :], -BIG, None, ALU.mult))
            done(v.tensor_scalar(k["post"][:, :], LR[:, :], -1.0, 1.0, ALU.mult, ALU.add))
            for h in range(HEADS):
                done(v.tensor_scalar(k["pen0"][:, h, :], FF[:, :], -BIG, None, ALU.mult))
                done(v.tensor_scalar(k["nl0"][:, h, :], k["is_last"][:, :], -1.0, 1.0, ALU.mult, ALU.add))
            done(v.memset(k["pen0"][:, :, 0:1], -BIG))
            done(v.memset(k["nl0"][:, :, P - 1:P], 0.0))
            for h in range(HEADS):
                done(v.tensor_scalar(ROW8[:, 0, h:h + 1], FR[:, P - 1:P], -BIG, None, ALU.mult))
                done(v.tensor_scalar(ROW8[:, 1, h:h + 1], LR[:, 0:1], -1.0, 1.0, ALU.mult, ALU.add))
            done(v.tensor_tensor(HV[:, :], IRF[:, :], k["is_last"][:, :], ALU.mult))
            done(v.tensor_tensor_scan(HL[:, ::-1], k["nl0"][:, 0, ::-1], HV[:, ::-1], 0.0, ALU.mult, ALU.add))
            v.memset(HS[:, :], 0.0).then_inc(s_shape, 1)
            eng.wait_ge(s_pe, 6)
            done(v.tensor_copy(k["dst_col"][:, :], PS[:, 0:T]))
            done(v.tensor_copy(k["src_col"][:, :], PS[:, 128:128 + T]))
            done(v.tensor_copy(LC[:, :], PS[:, 256:256 + T]))
            done(v.tensor_copy(k["row_pen"][:, :], PQ[0:HEADS, 0:T]))
            done(v.tensor_copy(k["row_nl"][:, :], PQ[0:HEADS, 128:128 + T]))
            eng.wait_ge(s_shape, 1)
            done(v.tensor_tensor_scan(HC[:, ::-1], k["row_nl"][0:1, ::-1], PQ[0:1, 256:256 + T][:, ::-1], 0.0, ALU.mult, ALU.add))
            v.tensor_copy(HS[:, 0:T - 1], HC[:, 1:T]).then_inc(s_shape, 1)
            eng.wait_ge(s_pe, 7)
            done(v.tensor_copy(HO[:, :], PQ[0:T, 400:401]))
            done(v.tensor_scalar(HV[:, :], k["post"][:, :], HO[:, 0:1], None, ALU.mult))
            v.tensor_tensor(HX[:, :], HV[:, :], HL[:, :], ALU.add).then_inc(s_shape, 1)
            eng.wait_ge(s_pe, 8)
            done(v.tensor_copy(k["hold_ix"][:, :], PS[:, 384:384 + T]))
            done(v.tensor_copy(k["dst_ix"][:, :], k["dst_col"][:, :]))
            done(v.tensor_scalar(k["dst_ix"][:, :], k["dst_col"][:, :], float(N - 1), None, ALU.min))
            done(v.tensor_scalar(k["src_ix"][:, :], k["src_col"][:, :], float(N - 1), None, ALU.min))
            done(v.tensor_copy(MI[:, :], k["src_col"][:, :]))

            def where(out, cond, value, scale, add, other):
                done(v.tensor_scalar(TMP[:, :], value, scale, add - other, ALU.mult, ALU.add))
                done(v.tensor_tensor(TMQ[:, :], TMP[:, :], cond, ALU.mult))
                done(v.tensor_scalar(out, TMQ[:, :], float(other), None, ALU.add))

            where(M1[:, :], LC[:, :], k["dst_col"][:, :], 2.0, 0.0, float(SKIP))
            v.memset(ZERO[:, 0:1], 0.0).then_inc(s_ix, 1)
            where(k["out_d_ix"][:, :], LC[:, :], k["dst_col"][:, :], 1.0, 0.0, float(SKIP))
            done(v.tensor_scalar(LASTP[:, :], RELF[:, :], float(P - 1), None, ALU.is_equal))
            done(v.memset(k["prev_col"][:, :], -5.0))
            done(v.tensor_scalar(TMP[:, 0:T - 1], k["dst_col"][:, 0:T - 1], 5.0, LASTP[:, 0:1], ALU.add, ALU.mult))
            done(v.tensor_scalar(k["prev_col"][:, 1:T], TMP[:, 0:T - 1], -5.0, None, ALU.add))
            STEPS = 5

            def block_of(b, buf, loads):
                eng.wait_ge(s_tb[buf], loads * 32)
                carry_waits(eng, w)
                cols = lambda x: x[:, bass.ds(b * J, J)]
                rows = lambda x: x.rearrange("p (j q) -> p j q", j=J)
                v.tensor_tensor(EQ[:, :, :], rows(SB_[:, buf, :]), cols(k["src_col"])[:, :, None].to_broadcast([P, J, P]), ALU.is_equal).then_inc(s_loop, 1)
                v.tensor_scalar(OH[:, 0, :], TB[:, buf, :], RELF[:, 0:1], None, ALU.is_equal).then_inc(s_oh, 1)
                eng.wait_ge(s_loop, b * STEPS + 1)
                v.tensor_tensor(EQ[:, :, :], EQ[:, :, :], UPPER[:, None, :].to_broadcast([P, J, P]), ALU.mult).then_inc(s_loop, 1)
                eng.wait_ge(s_loop, b * STEPS + 2)
                v.tensor_reduce(DUP[:, :], EQ[:, :, :], AX.X, ALU.max).then_inc(s_loop, 1)
                eng.wait_ge(s_loop, b * STEPS + 3)
                v.tensor_scalar(cols(TL), DUP[:, :], -1.0, 1.0, ALU.mult, ALU.add).then_inc(s_loop, 1)
                eng.wait_ge(s_cf_pe, b + 1)
                carry_waits(eng, w)
                v.tensor_scalar(k["coef"][:, bass.ds(b * J, J), :], PC[:, 0:J * BASES].rearrange("p (j b) -> p j b", j=J), 1.0, None, ALU.mult).then_inc(s_loop, 1)
                eng.wait_ge(s_loop, (b + 1) * STEPS)
                v.memset(DUP[:, :], 0.0).then_inc(s_tl, 1)

            block_of(0, 0, 1)
            with eng.Fori(0, (BLOCKS - 1) // 2) as i:
                block_of(i * 2 + 1, 1, i + 1)
                block_of(i * 2 + 2, 0, i + 2)
            eng.wait_ge(s_tl, BLOCKS)
            where(M2[:, :], TL[:, :], k["src_col"][:, :], 2.0, 1.0, float(SKIP))
            v.memset(ZERO[:, 0:1], 0.0).then_inc(s_ix, 1)
            eng.wait_ge(s_mg, 16 * T)
            done(v.tensor_copy(MGF[:, :, :], MG[:, :, :]))
            done(v.tensor_copy(k["map_ix"][:, :], MGF[:, :, 0]))
            done(v.tensor_tensor(OWN[:, :], MGF[:, :, 1], IDF[:, :], ALU.is_equal))
            where(k["out_s_ix"][:, :], OWN[:, :], k["src_col"][:, :], 1.0, 0.0, float(SKIP))
            done(v.tensor_scalar(TMP[:, :], MGF[:, :, 1], DUMPF[:, 0:1], None, ALU.subtract))
            done(v.tensor_tensor(TMQ[:, :], TMP[:, :], TL[:, :], ALU.mult))
            done(v.tensor_scalar(k["acc_ix"][:, :], TMQ[:, :], DUMPF[:, 0:1], None, ALU.add))


def block_rows(table, b):
    return table[bass.ds(b * J * P, J * P), :].rearrange("(j p) c -> p j c", p=P)


class NormBuffers:

    def __init__(self, nc, ctx, name, n):
        sb = lambda x, s: ctx.enter_context(nc.sbuf_tensor(name + x, s, F32))
        sem = lambda x: ctx.semaphore(name + x)
        self.n = n
        self.stats, self.moments = sb("_st", [P, n, J, 6]), sb("_mv", [P, n, J, 2])
        self.var_eps, self.rstd = sb("_ve", [P, n, J]), sb("_rs", [P, n, J])
        self.s_stats, self.s_moments = sem("_stats"), sem("_moments")
        self.s_var_eps, self.s_rstd, self.s_normed = sem("_var_eps"), sem("_rstd"), sem("_normed")


def norm_stats(nc, eng, nb, w, rows, u, count):
    for j in range(J):
        nc.vector.bn_stats(nb.stats[:, u, j, :], rows[:, j, :]).then_inc(nb.s_stats, 1)
    eng.wait_ge(nb.s_stats, count * J)
    carry_waits(eng, w)
    for j in range(J):
        nc.vector.bn_aggr(nb.moments[:, u, j, :], nb.stats[:, u, j, :]).then_inc(nb.s_moments, 1)


def norm_rstd(nc, eng, nb, w, u, count):
    eng.wait_ge(nb.s_moments, count * J)
    nc.gpsimd.tensor_tensor(nb.var_eps[:, u, :], nb.moments[:, u, :, 1], w["ln_eps"][:, 0:J], ALU.add).then_inc(nb.s_var_eps, 1)
    eng.wait_ge(nb.s_var_eps, count)
    nc.gpsimd.tensor_tensor(nb.rstd[:, u, :], nb.var_eps[:, u, :], w["neg_half"][:, 0:J], ALU.pow).then_inc(nb.s_rstd, 1)


def norm_apply(nc, eng, nb, out, rows, u, count):
    eng.wait_ge(nb.s_rstd, count)
    for j in range(J):
        nc.vector.tensor_scalar(out[:, j, :], rows[:, j, :], nb.moments[:, u, j, 0:1], nb.rstd[:, u, j:j + 1],
                                ALU.subtract, ALU.mult).then_inc(nb.s_normed, 1)


def gather_inputs(nc, w, k, t, x):
    U = 2 * GE
    with phase(nc) as ctx:
        sb = lambda n, s, d=F32: ctx.enter_context(nc.sbuf_tensor("g_" + n, s, d))
        sem = lambda n: ctx.semaphore("g_" + n)
        IX = sb("ix", [P, U, J], I32)
        X = sb("x", [P, U, J, C])
        H = sb("h", [P, U, J, C])
        nb = NormBuffers(nc, ctx, "g_nb", U)
        s_ix, s_relu = sem("ix"), sem("relu")
        s_x = [sem(f"x{u}") for u in range(U)]
        s_out = [sem(f"out{u}") for u in range(U)]
        block = ctx.enter_context(nc.Block())

        @block.gpsimd
        def _(eng):
            for i in rounds(eng, ROUNDS_E):
                for u in range(U):
                    wait(eng, s_out[u], i * 32)
                    eng.wait_ge(s_ix, i * U + u + 1)
                    carry_waits(eng, w)
                    for j in range(J):
                        eng.indirect_dma_start(out=X[:, u, j, :], out_offset=None, in_=x,
                                               in_offset=bass.IndirectOffsetOnAxis(ap=IX[:, u, j:j + 1], axis=0),
                                               bounds_check=N - 1, oob_is_err=False).then_inc(s_x[u], 16)
                for u in range(U):
                    norm_rstd(nc, eng, nb, w, u, i * U + u + 1)

        @block.vector
        def _(eng):
            for i in rounds(eng, ROUNDS_E):
                for u in range(U):
                    wait(eng, s_x[u], i * (16 * J))
                    carry_waits(eng, w)
                    source = k["src_ix"] if u % 2 == 0 else k["dst_ix"]
                    nc.vector.tensor_scalar(IX[:, u, :], source[:, bass.ds((i * GE + u // 2) * J, J)], 0.0, None, ALU.add).then_inc(s_ix, 1)
                for u in range(U):
                    eng.wait_ge(s_x[u], (i + 1) * (16 * J))
                    norm_stats(nc, eng, nb, w, X[:, u, :, :], u, i * U + u + 1)
                for u in range(U):
                    norm_apply(nc, eng, nb, H[:, u, :, :], X[:, u, :, :], u, i * U + u + 1)
                    eng.wait_ge(nb.s_normed, (i * U + u + 1) * J)
                    nc.vector.tensor_scalar(H[:, u, :, :], H[:, u, :, :], 0.0, None, ALU.max).then_inc(s_relu, 1)

        @block.sync
        def _(eng):
            for i in rounds(eng, ROUNDS_E):
                for u in range(U):
                    b = i * GE + u // 2
                    eng.wait_ge(s_x[u], (i + 1) * (16 * J))
                    eng.dma_start(block_rows(t["xs" if u % 2 == 0 else "xd"], b), X[:, u, :, :]).then_inc(s_out[u], 16)
                    eng.wait_ge(s_relu, i * U + u + 1)
                    eng.dma_start(block_rows(t["s0" if u % 2 == 0 else "d0"], b), H[:, u, :, :]).then_inc(s_out[u], 16)
            for u in range(U):
                eng.wait_ge(s_out[u], 32 * ROUNDS_E)


def project(nc, w, k, t, r, heads, rhs, bias_row, norm, sigmoid, overlay, plus_x, keep):
    U = 2 * GE
    CW = C + 2 * heads
    with phase(nc) as ctx:
        pre = f"p{r}_"
        sb = lambda n, s, d=F32: ctx.enter_context(nc.sbuf_tensor(pre + n, s, d))
        sem = lambda n: ctx.semaphore(pre + n)
        IX = sb("ix", [P, GE, J], I32)
        A = sb("a", [P, U, J, C])
        HT = sb("ht", [P, U, J * C])
        NR = HT[:, :, :].rearrange("p u (j c) -> p u j c", j=J)
        UP = sb("up", [P, GE, J, C])
        XS = sb("xs", [P, GE, J, C]) if plus_x else None
        nb = NormBuffers(nc, ctx, pre + "nb", U) if norm else None
        PT = [ctx.enter_context(nc.psum_tensor(f"{pre}pt{n}", [P, J, C], F32)) for n in range(2)]
        PM = [ctx.enter_context(nc.psum_tensor(f"{pre}pm{n}", [P, J, 256], F32)) for n in range(2)]
        s_ix, s_tp, s_ht, s_mm, s_keep, s_biased, s_sig, s_next, s_plus = (
            sem(n) for n in "ix tp ht mm keep biased sig next plus".split())
        s_load = [sem(f"load{u}") for u in range(U)]
        s_over = [sem(f"over{g}") for g in range(GE)]
        s_xs = [sem(f"xs{g}") for g in range(GE)]
        s_out = [sem(f"out{g}") for g in range(GE)]
        block = ctx.enter_context(nc.Block())

        def state_there(eng, i, u):
            if u % 2 == 0 and overlay:
                eng.wait_ge(s_over[u // 2], (i + 1) * (16 * J))
            else:
                eng.wait_ge(s_load[u], (i + 1) * 16)

        @block.sync
        def _(eng):
            for i in rounds(eng, ROUNDS_E):
                for u in range(U):
                    g = u // 2
                    if u % 2 == 0:
                        wait(eng, s_out[g], i * 16)
                    else:
                        wait(eng, s_tp, (i - 1) * U + u + 1)
                    eng.dma_start(A[:, u, :, :], block_rows(t[f"s{r}" if u % 2 == 0 else f"d{r}"], i * GE + g)).then_inc(s_load[u], 16)
                    if plus_x and u % 2 == 0:
                        wait(eng, s_next, (i - 1) * GE + g + 1)
                        eng.dma_start(XS[:, g, :, :], block_rows(t["xs"], i * GE + g)).then_inc(s_xs[g], 16)
                for g in range(GE):
                    eng.wait_ge(s_next, i * GE + g + 1)
                    eng.dma_start(block_rows(t[f"s{r + 1}"], i * GE + g), A[:, 2 * g, :, :]).then_inc(s_out[g], 16)
            for g in range(GE):
                eng.wait_ge(s_out[g], 16 * ROUNDS_E)

        @block.gpsimd
        def _(eng):
            for i in rounds(eng, ROUNDS_E):
                if overlay:
                    for g in range(GE):
                        eng.wait_ge(s_ix, i * GE + g + 1)
                        eng.wait_ge(s_load[2 * g], (i + 1) * 16)
                        carry_waits(eng, w)
                        for j in range(J):
                            eng.indirect_dma_start(out=A[:, 2 * g, j, :], out_offset=None, in_=t[f"d{r}"],
                                                   in_offset=bass.IndirectOffsetOnAxis(ap=IX[:, g, j:j + 1], axis=0),
                                                   bounds_check=EP - 1, oob_is_err=False).then_inc(s_over[g], 16)
                if norm:
                    for u in range(U):
                        norm_rstd(nc, eng, nb, w, u, i * U + u + 1)

        @block.vector
        def _(eng):
            for i in rounds(eng, ROUNDS_E):
                if overlay:
                    for g in range(GE):
                        wait(eng, s_over[g], i * (16 * J))
                        carry_waits(eng, w)
                        nc.vector.tensor_scalar(IX[:, g, :], k["map_ix"][:, bass.ds((i * GE + g) * J, J)], 0.0, None, ALU.add).then_inc(s_ix, 1)
                if norm:
                    for u in range(U):
                        state_there(eng, i, u)
                        norm_stats(nc, eng, nb, w, A[:, u, :, :], u, i * U + u + 1)
                    for u in range(U):
                        wait(eng, s_mm, (i - 1) * U + u + 1)
                        norm_apply(nc, eng, nb, NR[:, u, :, :], A[:, u, :, :], u, i * U + u + 1)
                for u in range(U):
                    g = u // 2
                    eng.wait_ge(s_mm, i * U + u + 1)
                    if u % 2 == 0:
                        wait(eng, s_next, (i - 1) * GE + g + 1)
                        nc.vector.tensor_tensor(UP[:, g, :, :], PM[u % 2][:, :, 0:C], bias_row[:, None, :].to_broadcast([P, J, C]),
                                                ALU.add).then_inc(s_biased, 1)
                        eng.wait_ge(s_biased, i * GE + g + 1)
                    keep_to = keep["src" if u % 2 == 0 else "dst"]
                    carry_waits(eng, w)
                    nc.vector.tensor_scalar(keep_to[:, bass.ds((i * GE + g) * J, J), 0:CW], PM[u % 2][:, :, 0:CW], 0.0, None, ALU.add).then_inc(s_keep, 1)
                for g in range(GE):
                    eng.wait_ge(s_sig if sigmoid else s_biased, i * GE + g + 1)
                    if plus_x:
                        eng.wait_ge(s_xs[g], (i + 1) * 16)
                        nc.vector.tensor_tensor(UP[:, g, :, :], UP[:, g, :, :], XS[:, g, :, :], ALU.add).then_inc(s_plus, 1)
                        eng.wait_ge(s_plus, i * GE + g + 1)
                    state_there(eng, i, 2 * g)
                    eng.wait_ge(s_tp, i * U + 2 * g + 1)
                    nc.vector.tensor_tensor(A[:, 2 * g, :, :], A[:, 2 * g, :, :], UP[:, g, :, :], ALU.add).then_inc(s_next, 1)

        @block.scalar
        def _(eng):
            for i in rounds(eng, ROUNDS_E):
                for u in range(U):
                    eng.wait_ge(s_tp, i * U + u + 1)
                    wait(eng, s_mm, (i - 1) * U + u + 1)
                    nc.scalar.activation(HT[:, u, :], PT[u % 2][:, :, :].rearrange("p j c -> p (j c)"),
                                         ACT.Relu if norm else ACT.Copy).then_inc(s_ht, 1)
                    if sigmoid and u % 2:
                        g = u // 2
                        eng.wait_ge(s_biased, i * GE + g + 1)
                        nc.scalar.activation(UP[:, g, :, :], UP[:, g, :, :], ACT.Sigmoid).then_inc(s_sig, 1)

        @block.tensor
        def _(eng):
            for i in rounds(eng, ROUNDS_E):
                def product(u):
                    eng.wait_ge(s_ht, i * U + u + 1)
                    wait(eng, s_keep, i * U + u + 1 - 2)
                    for j in range(J):
                        last = nc.tensor.matmul(PM[u % 2][:, j, 0:CW], HT[:, u, j * C:(j + 1) * C], rhs, start=True, stop=True)
                    last.then_inc(s_mm, 1)

                for u in range(U):
                    if norm:
                        eng.wait_ge(nb.s_normed, (i * U + u + 1) * J)
                    else:
                        state_there(eng, i, u)
                    wait(eng, s_ht, i * U + u + 1 - 2)
                    for j in range(J):
                        last = nc.tensor.transpose(PT[u % 2][:, j, :], (NR if norm else A)[:, u, j, :], w["ident"][:, :])
                    last.then_inc(s_tp, 1)
                    if u:
                        product(u - 1)
                product(U - 1)


def attend(nc, w, k, r, heads, keep, wm, ws):
    H = heads
    with phase(nc) as ctx:
        pre = f"t{r}_"
        sb = lambda n, s, d=F32: ctx.enter_context(nc.sbuf_tensor(pre + n, s, d))
        sem = lambda n: ctx.semaphore(pre + n)
        row = lambda n: sb(n, [T, H, P])
        SR, DS, DD, HD, T1, SC, ES, MX = (row(n) for n in "sr ds dd hd t1 sc es mx".split())
        EDGE = sb("edge", [T, H])
        RC, RS = sb("rc", [H, T]), sb("rs", [H, T])
        CI = sb("ci", [T, H])
        PA = ctx.enter_context(nc.psum_tensor(pre + "pa", [P, HEADS, P], F32))
        PB = ctx.enter_context(nc.psum_tensor(pre + "pb", [P, HEADS, P], F32))
        PC = ctx.enter_context(nc.psum_tensor(pre + "pc", [P, HEADS, P], F32))
        PX = ctx.enter_context(nc.psum_tensor(pre + "px", [P, 512], F32))
        s_v, s_rows, s_edge, s_edge_t, s_carry, s_carry_t, s_exp_in, s_exp, s_cols = (
            sem(n) for n in "v rows edge edge_t carry carry_t exp_in exp cols".split())
        block = ctx.enter_context(nc.Block())
        idp, idt, idh = w["ident"][:, :], w["ident"][0:T, 0:T], w["ident"][0:H, 0:H]
        flat = lambda x: x.rearrange("t h p -> t (h p)")
        wide = lambda x: x[:, None, :].to_broadcast([T, H, P])

        @block.tensor
        def _(eng):
            for h in range(H):
                nc.tensor.transpose(PA[0:T, h, :], keep["src"][:, :, C + h], idp)
                nc.tensor.transpose(PB[0:T, h, :], keep["dst"][:, :, C + h], idp)
                last = nc.tensor.transpose(PC[0:T, h, :], keep["dst"][:, :, C + H + h], idp)
            last.then_inc(s_rows, 1)
            for n in range(3):
                eng.wait_ge(s_edge, n + 1)
                nc.tensor.transpose(PX[0:H, 0:T], EDGE[:, :], idt).then_inc(s_edge_t, 1)
                eng.wait_ge(s_carry, n + 1)
                nc.tensor.transpose(PX[0:T, 256:256 + H], RS[:, :], idh).then_inc(s_carry_t, 1)
            eng.wait_ge(s_exp, 2)
            for h in range(H):
                nc.tensor.transpose(PA[:, h, 0:T], SC[:, h, :], idt)
                last = nc.tensor.transpose(PB[:, h, 0:T], ES[:, h, :], idt)
            last.then_inc(s_cols, 1)

        @block.scalar
        def _(eng):
            eng.wait_ge(s_exp_in, 1)
            nc.scalar.activation(flat(SC[:, :, :]), flat(SC[:, :, :]), ACT.Exp).then_inc(s_exp, 1)
            nc.scalar.activation(flat(ES[:, :, :]), flat(ES[:, :, :]), ACT.Exp).then_inc(s_exp, 1)

        @block.vector
        def _(eng):
            v = nc.vector
            n = [0]
            m = [0]

            def done(ins_):
                n[0] += 1
                ins_.then_inc(s_v, 1)
                eng.wait_ge(s_v, n[0])

            def over_rows(scan):
                m[0] += 1
                v.tensor_scalar(EDGE[:, :], EDGE[:, :], 0.0, None, ALU.add).then_inc(s_edge, 1)
                eng.wait_ge(s_edge_t, m[0])
                scan(PX[0:H, 0:T])
                eng.wait_ge(s_carry_t, m[0])
                done(v.tensor_copy(CI[:, :], PX[0:T, 256:256 + H]))

            def hold(out, values):
                done(v.tensor_tensor(T1[:, :, :], values, wide(k["is_last"]), ALU.mult))
                done(v.tensor_tensor_scan(flat(out)[:, ::-1], flat(k["nl0"][:, 0:H, :])[:, ::-1], flat(T1[:, :, :])[:, ::-1],
                                          0.0, ALU.mult, ALU.add))
                done(v.tensor_copy(EDGE[:, :], out[:, :, 0]))

                def scan(edge):
                    done(v.tensor_tensor_scan(RC[:, ::-1], k["row_nl"][0:H, ::-1], edge[:, ::-1], 0.0, ALU.mult, ALU.add))
                    done(v.memset(RS[:, T - 1:T], 0.0))
                    v.tensor_copy(RS[:, 0:T - 1], RC[:, 1:T]).then_inc(s_carry, 1)

                over_rows(scan)
                done(v.tensor_tensor(T1[:, :, :], wide(k["post"]), CI[:, :, None].to_broadcast([T, H, P]), ALU.mult))
                done(v.tensor_tensor(out, out, T1[:, :, :], ALU.add))

            eng.wait_ge(s_rows, 1)
            done(v.tensor_copy(SR[:, :, :], PA[0:T, 0:H, :]))
            done(v.tensor_copy(DS[:, :, :], PB[0:T, 0:H, :]))
            done(v.tensor_copy(DD[:, :, :], PC[0:T, 0:H, :]))
            hold(HD[:, :, :], DD[:, :, :])
            for out, a in ((SC, SR), (ES, DS)):
                done(v.tensor_tensor(T1[:, :, :], a[:, :, :], HD[:, :, :], ALU.add))
                done(v.scalar_tensor_tensor(out[:, :, :], T1[:, :, :], SLOPE, T1[:, :, :], ALU.mult, ALU.max))
            done(v.tensor_tensor(T1[:, :, :], ES[:, :, :], wide(k["last_pen"]), ALU.add))
            done(v.tensor_tensor(T1[:, :, :], T1[:, :, :], SC[:, :, :], ALU.max))
            done(v.tensor_tensor_scan(flat(MX[:, :, :]), flat(k["pen0"][:, 0:H, :]), flat(T1[:, :, :]), 0.0, ALU.add, ALU.max))
            done(v.tensor_copy(EDGE[:, :], MX[:, :, P - 1]))

            def scan_max(edge):
                done(v.tensor_tensor_scan(RC[:, :], k["row_pen"][0:H, :], edge, -BIG, ALU.add, ALU.max))
                done(v.memset(RS[:, 0:1], -BIG))
                v.tensor_copy(RS[:, 1:T], RC[:, 0:T - 1]).then_inc(s_carry, 1)

            over_rows(scan_max)
            done(v.tensor_tensor(T1[:, :, :], wide(k["pre_pen"]), CI[:, :, None].to_broadcast([T, H, P]), ALU.add))
            done(v.tensor_tensor(MX[:, :, :], MX[:, :, :], T1[:, :, :], ALU.max))
            hold(SR[:, :, :], MX[:, :, :])
            done(v.tensor_tensor(SC[:, :, :], SC[:, :, :], SR[:, :, :], ALU.subtract))
            done(v.tensor_tensor(ES[:, :, :], ES[:, :, :], SR[:, :, :], ALU.subtract))
            v.tensor_scalar(ES[:, :, :], ES[:, :, :], 0.0, None, ALU.min).then_inc(s_exp_in, 1)
            eng.wait_ge(s_cols, 1)
            done(v.tensor_copy(wm[:, :, 0:H], PA[:, 0:H, 0:T].rearrange("p h t -> p t h")))
            done(v.tensor_copy(ws[:, :, 0:H], PB[:, 0:H, 0:T].rearrange("p h t -> p t h")))


def aggregate(nc, w, k, t, r, kind, heads, keep, wm, ws, bias_row, plus_x):
    H = heads
    M = C + H
    with phase(nc) as ctx:
        pre = f"c{r}_"
        sb = lambda n, s, d=F32: ctx.enter_context(nc.sbuf_tensor(pre + n, s, d))
        sem = lambda n: ctx.semaphore(pre + n)
        KB = sb("kb", [P, GE, J * P])
        SEL = sb("sel", [P, GE, J, P])
        CAR = sb("car", [P, GE, J, P])
        MS = sb("ms", [P, GE, J, M])
        SUM = sb("sum", [P, GE, J, M])
        U = MS[:, :, :, 0:C]
        DN = sb("dn", [P, GE, J, H])
        XD = KB[:, :, :].rearrange("p g (j c) -> p g j c", j=J)
        A = sb("a", [P, GE, J, C]) if plus_x else XD
        PS = [ctx.enter_context(nc.psum_tensor(f"{pre}ps{n}", [P, 512], F32)) for n in range(J)]
        s_v, s_sel, s_pe, s_sum, s_num, s_den, s_sig, s_next, s_pow_in = (
            sem(n) for n in "v sel pe sum num den sig next pow_in".split())
        s_kb = [sem(f"kb{g}") for g in range(GE)]
        s_load = [sem(f"load{g}") for g in range(GE)]
        s_out = [sem(f"out{g}") for g in range(GE)]
        s_zero = sem("zero")
        block = ctx.enter_context(nc.Block())
        heads_of = lambda x: x.rearrange("p j (h c) -> p j h c", h=H)
        over = lambda x: x[:, :, :, None].to_broadcast([P, J, H, C // H])

        @block.sync
        def _(eng):
            for i in rounds(eng, ROUNDS_E):
                for g in range(GE):
                    b = i * GE + g
                    if plus_x:
                        wait(eng, s_pow_in, (i - 1) * GE + g + 1)
                    else:
                        wait(eng, s_out[g], i * 16)
                    eng.dma_start(KB[:, g, :], t["dst_row"][0:1, bass.ds(b * J * P, J * P)].to_broadcast([P, J * P])).then_inc(s_kb[g], 16)
                    if plus_x:
                        wait(eng, s_out[g], i * 16)
                        eng.dma_start(A[:, g, :, :], block_rows(t[f"d{r}"], b)).then_inc(s_load[g], 16)
                for g in range(GE):
                    eng.wait_ge(s_sel, i * GE + g + 1)
                    eng.dma_start(XD[:, g, :, :], block_rows(t["xd" if plus_x else f"d{r}"], i * GE + g)).then_inc(s_load[g], 16)
                for g in range(GE):
                    eng.wait_ge(s_next, i * GE + g + 1)
                    eng.dma_start(block_rows(t[f"d{r + 1}"], i * GE + g), A[:, g, :, :]).then_inc(s_out[g], 16)
            for g in range(GE):
                eng.wait_ge(s_out[g], 16 * ROUNDS_E)

        @block.gpsimd
        def _(eng):
            if kind == "relu":
                for i in rounds(eng, ROUNDS_E):
                    for g in range(GE):
                        eng.wait_ge(s_pow_in, i * GE + g + 1)
                        nc.gpsimd.tensor_tensor(DN[:, g, :, 0], DN[:, g, :, 0], w["neg_half"][:, 0:J], ALU.pow).then_inc(s_den, 1)

        @block.vector
        def _(eng):
            v = nc.vector
            v.memset(SUM[:, GE - 1, J - 1, :], 0.0).then_inc(s_zero, 1)
            for i in rounds(eng, ROUNDS_E):
                tiles = lambda x, g: x[:, bass.ds((i * GE + g) * J, J)]
                for g in range(GE):
                    c = i * GE + g + 1
                    wait(eng, s_pe, (c - GE) * J)
                    wait(eng, s_next, c - GE)
                    eng.wait_ge(s_kb[g], (i + 1) * 16)
                    carry_waits(eng, w)
                    key = KB[:, g, :].rearrange("p (j q) -> p j q", j=J)
                    v.tensor_tensor(SEL[:, g, :, :], key, tiles(k["dst_col"], g)[:, :, None].to_broadcast([P, J, P]), ALU.is_equal).then_inc(s_v, 1)
                    v.tensor_tensor(CAR[:, g, :, :], key, tiles(k["prev_col"], g)[:, :, None].to_broadcast([P, J, P]), ALU.is_equal).then_inc(s_sel, 1)
                    if kind == "relu":
                        v.tensor_scalar(MS[:, g, :, 0:C], keep["src"][:, bass.ds((i * GE + g) * J, J), 0:C], 0.0, None, ALU.add).then_inc(s_v, 1)
                        v.memset(MS[:, g, :, C:M], 1.0).then_inc(s_v, 1)
                    else:
                        wt = wm[:, bass.ds((i * GE + g) * J, J), 0:H]
                        v.tensor_tensor(heads_of(MS[:, g, :, 0:C]), heads_of(keep["src"][:, bass.ds((i * GE + g) * J, J), 0:C]), over(wt), ALU.mult).then_inc(s_v, 1)
                        v.tensor_scalar(MS[:, g, :, C:M], wt, 0.0, None, ALU.add).then_inc(s_v, 1)
                for g in range(GE):
                    c = i * GE + g + 1
                    kept = keep["dst"][:, bass.ds((i * GE + g) * J, J), 0:C]
                    if kind == "relu":
                        eng.wait_ge(s_sum, c * J)
                        v.tensor_scalar(DN[:, g, :, :], SUM[:, g, :, C:M], 1.0, None, ALU.max).then_inc(s_pow_in, 1)
                        eng.wait_ge(s_den, c)
                        v.tensor_tensor(U[:, g, :, :], SUM[:, g, :, 0:C], DN[:, g, :, :].to_broadcast([P, J, C]), ALU.mult).then_inc(s_num, 1)
                        eng.wait_ge(s_num, c * 2 - 1)
                        v.tensor_tensor(U[:, g, :, :], U[:, g, :, :], kept, ALU.add).then_inc(s_num, 1)
                        eng.wait_ge(s_num, c * 2)
                        eng.wait_ge(s_load[g], (i + 1) * 16)
                        v.scalar_tensor_tensor(A[:, g, :, :], U[:, g, :, :], 0.0, A[:, g, :, :], ALU.max, ALU.add).then_inc(s_next, 1)
                        continue
                    self_w = ws[:, bass.ds((i * GE + g) * J, J), 0:H]
                    eng.wait_ge(s_pe, c * J)
                    carry_waits(eng, w)
                    v.tensor_tensor(heads_of(U[:, g, :, :]), heads_of(kept), over(self_w), ALU.mult).then_inc(s_num, 1)
                    eng.wait_ge(s_sum, c * J)
                    carry_waits(eng, w)
                    v.tensor_tensor(DN[:, g, :, :], SUM[:, g, :, C:M], self_w, ALU.add).then_inc(s_den, 1)
                    eng.wait_ge(s_num, c * 4 - 3)
                    v.tensor_tensor(U[:, g, :, :], U[:, g, :, :], SUM[:, g, :, 0:C], ALU.add).then_inc(s_num, 1)
                    eng.wait_ge(s_den, c * 3 - 2)
                    v.tensor_scalar(DN[:, g, :, :], DN[:, g, :, :], GAT_EPS if kind == "sigmoid" else 0.0, None, ALU.add).then_inc(s_den, 1)
                    eng.wait_ge(s_den, c * 3 - 1)
                    v.reciprocal(DN[:, g, :, :], DN[:, g, :, :]).then_inc(s_den, 1)
                    eng.wait_ge(s_num, c * 4 - 2)
                    eng.wait_ge(s_den, c * 3)
                    v.tensor_tensor(heads_of(U[:, g, :, :]), heads_of(U[:, g, :, :]), over(DN[:, g, :, :]), ALU.mult).then_inc(s_num, 1)
                    eng.wait_ge(s_num, c * 4 - 1)
                    v.tensor_tensor(U[:, g, :, :], U[:, g, :, :], bias_row[:, None, :].to_broadcast([P, J, C]), ALU.add).then_inc(s_num, 1)
                if kind != "relu":
                    for g in range(GE):
                        c = i * GE + g + 1
                        eng.wait_ge(s_load[g], (i + 1) * (32 if plus_x else 16))
                        if plus_x:
                            v.tensor_tensor(A[:, g, :, :], A[:, g, :, :], XD[:, g, :, :], ALU.add).then_inc(s_pow_in, 1)
                            eng.wait_ge(s_pow_in, c)
                        if kind == "sigmoid":
                            eng.wait_ge(s_sig, c)
                        else:
                            eng.wait_ge(s_num, c * 4)
                        v.tensor_tensor(A[:, g, :, :], A[:, g, :, :], U[:, g, :, :], ALU.add).then_inc(s_next, 1)

        @block.scalar
        def _(eng):
            for i in rounds(eng, ROUNDS_E):
                for g in range(GE):
                    c = i * GE + g + 1
                    wait(eng, s_next, c - GE)
                    for j in range(J):
                        eng.wait_ge(s_pe, (c - 1) * J + j + 1)
                        nc.scalar.activation(SUM[:, g, j, :], PS[j][:, 0:M], ACT.Copy).then_inc(s_sum, 1)
                if kind == "sigmoid":
                    for g in range(GE):
                        eng.wait_ge(s_num, (i * GE + g + 1) * 4)
                        nc.scalar.activation(U[:, g, :, :], U[:, g, :, :], ACT.Sigmoid).then_inc(s_sig, 1)

        @block.tensor
        def _(eng):
            eng.wait_ge(s_zero, 1)
            for i in rounds(eng, ROUNDS_E):
                for g in range(GE):
                    c = i * GE + g + 1
                    eng.wait_ge(s_v, c * 3)
                    eng.wait_ge(s_sel, c)
                    for j in range(J):
                        wait(eng, s_sum, (c - 2) * J + j + 1)
                        nc.tensor.matmul(PS[j][:, 0:M], SEL[:, g, j, :], MS[:, g, j, :], start=True, stop=False)
                        wait(eng, s_sum, (c - 1) * J + j)
                        before = SUM[:, g, j - 1, :] if j else SUM[:, (g - 1) % GE, J - 1, :]
                        nc.tensor.matmul(PS[j][:, 0:M], CAR[:, g, j, :], before, start=False, stop=True).then_inc(s_pe, 1)


def relate(nc, w, k, t, r, keep):
    U = 2 * GE
    with phase(nc) as ctx:
        pre = f"r{r}_"
        sb = lambda n, s, d=F32: ctx.enter_context(nc.sbuf_tensor(pre + n, s, d))
        sem = lambda n: ctx.semaphore(pre + n)
        IX = sb("ix", [P, GE, J], I32)
        A = sb("a", [P, U, J, C])
        HT = sb("ht", [P, U, J * C])
        NR = HT[:, :, :].rearrange("p u (j c) -> p u j c", j=J)
        nb = NormBuffers(nc, ctx, pre + "nb", U)
        PT = [ctx.enter_context(nc.psum_tensor(f"{pre}pt{n}", [P, J, C], F32)) for n in range(2)]
        PM = [ctx.enter_context(nc.psum_tensor(f"{pre}pm{n}", [P, J, C], F32)) for n in range(2)]
        PB = [ctx.enter_context(nc.psum_tensor(f"{pre}pb{n}", [P, BASES, C], F32)) for n in range(4)]
        s_ix, s_tp, s_ht, s_mm, s_loop, s_next, s_basis, s_mix = (sem(n) for n in "ix tp ht mm loop next basis mix".split())
        s_load = [sem(f"load{u}") for u in range(U)]
        s_over = [sem(f"over{g}") for g in range(GE)]
        s_out = [sem(f"out{g}") for g in range(GE)]
        block = ctx.enter_context(nc.Block())

        def state_there(eng, i, u):
            if u % 2 == 0:
                eng.wait_ge(s_over[u // 2], (i + 1) * (16 * J))
            else:
                eng.wait_ge(s_load[u], (i + 1) * 16)

        @block.sync
        def _(eng):
            for i in rounds(eng, ROUNDS_E):
                for u in range(U):
                    g = u // 2
                    if u % 2 == 0:
                        wait(eng, s_out[g], i * 16)
                    else:
                        wait(eng, s_tp, (i - 1) * U + u + 1)
                    eng.dma_start(A[:, u, :, :], block_rows(t[f"s{r}" if u % 2 == 0 else f"d{r}"], i * GE + g)).then_inc(s_load[u], 16)
                for g in range(GE):
                    eng.wait_ge(s_next, i * GE + g + 1)
                    eng.dma_start(block_rows(t[f"s{r + 1}"], i * GE + g), A[:, 2 * g, :, :]).then_inc(s_out[g], 16)
            for g in range(GE):
                eng.wait_ge(s_out[g], 16 * ROUNDS_E)

        @block.gpsimd
        def _(eng):
            for i in rounds(eng, ROUNDS_E):
                for g in range(GE):
                    eng.wait_ge(s_ix, i * GE + g + 1)
                    eng.wait_ge(s_load[2 * g], (i + 1) * 16)
                    carry_waits(eng, w)
                    for j in range(J):
                        eng.indirect_dma_start(out=A[:, 2 * g, j, :], out_offset=None, in_=t[f"d{r}"],
                                               in_offset=bass.IndirectOffsetOnAxis(ap=IX[:, g, j:j + 1], axis=0),
                                               bounds_check=EP - 1, oob_is_err=False).then_inc(s_over[g], 16)
                for u in range(U):
                    norm_rstd(nc, eng, nb, w, u, i * U + u + 1)

        @block.vector
        def _(eng):
            v = nc.vector
            for i in rounds(eng, ROUNDS_E):
                for g in range(GE):
                    wait(eng, s_over[g], i * (16 * J))
                    carry_waits(eng, w)
                    v.tensor_scalar(IX[:, g, :], k["map_ix"][:, bass.ds((i * GE + g) * J, J)], 0.0, None, ALU.add).then_inc(s_ix, 1)
                for u in range(U):
                    state_there(eng, i, u)
                    norm_stats(nc, eng, nb, w, A[:, u, :, :], u, i * U + u + 1)
                for u in range(U):
                    wait(eng, s_mm, (i - 1) * U + u + 1)
                    if u % 2 == 0:
                        wait(eng, s_basis, ((i - 1) * GE + u // 2 + 1) * J)
                    norm_apply(nc, eng, nb, NR[:, u, :, :], A[:, u, :, :], u, i * U + u + 1)
                for u in range(U):
                    g = u // 2
                    b = i * GE + g
                    eng.wait_ge(s_mm, i * U + u + 1)
                    if u % 2:
                        carry_waits(eng, w)
                        v.tensor_scalar(keep["dst"][:, bass.ds(b * J, J), 0:C], PM[1][:, :, :], 0.0, None, ALU.add).then_inc(s_loop, 1)
                        continue
                    eng.wait_ge(s_tp, i * U + u + 1)
                    v.scalar_tensor_tensor(A[:, u, :, :], PM[0][:, :, :], 0.0, A[:, u, :, :], ALU.max, ALU.add).then_inc(s_next, 1)
                    for j in range(J):
                        q = b * J + j
                        tile = keep["src"][:, bass.ds(q, 1), 0:C].rearrange("p o c -> p (o c)")
                        coef = lambda base: k["coef"][:, bass.ds(q, 1), base:base + 1].rearrange("p o b -> p (o b)")
                        eng.wait_ge(s_basis, q + 1)
                        v.tensor_scalar(tile, PB[j][:, 0, :], coef(0), None, ALU.mult).then_inc(s_mix, 1)
                        for base in range(1, BASES):
                            eng.wait_ge(s_mix, q * BASES + base)
                            v.scalar_tensor_tensor(tile, PB[j][:, base, :], coef(base), tile, ALU.mult, ALU.add).then_inc(s_mix, 1)

        @block.scalar
        def _(eng):
            for i in rounds(eng, ROUNDS_E):
                for u in range(U):
                    eng.wait_ge(s_tp, i * U + u + 1)
                    wait(eng, s_mm, (i - 1) * U + u + 1)
                    if u % 2 == 0:
                        wait(eng, s_basis, ((i - 1) * GE + u // 2 + 1) * J)
                    nc.scalar.activation(HT[:, u, :], PT[u % 2][:, :, :].rearrange("p j c -> p (j c)"), ACT.Relu).then_inc(s_ht, 1)

        @block.tensor
        def _(eng):
            for i in rounds(eng, ROUNDS_E):
                def product(u):
                    g = u // 2
                    c = i * GE + g + 1
                    eng.wait_ge(s_ht, i * U + u + 1)
                    wait(eng, s_loop if u % 2 else s_next, c - 1)
                    for j in range(J):
                        last = nc.tensor.matmul(PM[u % 2][:, j, :], HT[:, u, j * C:(j + 1) * C], w["loop"][:, :], start=True, stop=True)
                    last.then_inc(s_mm, 1)
                    if u % 2 == 0:
                        for j in range(J):
                            wait(eng, s_mix, ((c - 2) * J + j + 1) * BASES)
                            nc.tensor.matmul(PB[j][:, :, :].rearrange("p b c -> p (b c)"), HT[:, u, j * C:(j + 1) * C],
                                             w["basis"][:, :, :].rearrange("p b c -> p (b c)"), start=True, stop=True).then_inc(s_basis, 1)

                for u in range(U):
                    eng.wait_ge(nb.s_normed, (i * U + u + 1) * J)
                    wait(eng, s_ht, i * U + u + 1 - 2)
                    for j in range(J):
                        last = nc.tensor.transpose(PT[u % 2][:, j, :], NR[:, u, j, :], w["ident"][:, :])
                    last.then_inc(s_tp, 1)
                    if u:
                        product(u - 1)
                product(U - 1)


def edge_messages(nc, w, k, t, r, out):
    U = 2 * GE
    M = C + 1
    MAP, HOLD, ACC, OUT = range(4)
    with phase(nc) as ctx:
        sb = lambda n, s, d=F32: ctx.enter_context(nc.sbuf_tensor("e_" + n, s, d))
        sem = lambda n: ctx.semaphore("e_" + n)
        IX = sb("ix", [P, GE, 4, J], I32)
        A = sb("a", [P, U, J, C])
        HT = sb("ht", [P, U, J * C])
        NR = HT[:, :, :].rearrange("p u (j c) -> p u j c", j=J)
        GT = sb("gt", [P, U, J * C])
        AD = sb("ad", [P, GE, J * C])
        KB = sb("kb", [P, GE, J, P])
        SEL = sb("sel", [P, GE, J, P])
        MS = sb("ms", [P, GE, J, M])
        TOT = sb("tot", [P, GE, J, M])
        nb = NormBuffers(nc, ctx, "e_nb", U)
        ps = lambda n, s: ctx.enter_context(nc.psum_tensor("e_" + n, s, F32))
        PT = [ps(f"pt{n}", [P, J, C]) for n in range(2)]
        PG, PM, PZ, PD = (ps(n, [P, J, C]) for n in "pg pm pz pd".split())
        PO = [ps(f"po{n}", [P, 2, 256]) for n in range(2)]
        s_ix, s_tp, s_ht, s_pg, s_nm, s_gt, s_sel, s_diff, s_abs, s_nh, s_ms, s_po, s_tot, s_z, s_d, s_one = (
            sem(n) for n in "ix tp ht pg nm gt sel diff abs nh ms po tot z d one".split())
        s_kb = [sem(f"kb{g}") for g in range(GE)]
        s_load = [sem(f"load{g}") for g in range(GE)]
        s_over = [sem(f"over{g}") for g in range(GE)]
        s_hold = [sem(f"hold{g}") for g in range(GE)]
        s_acc = [sem(f"acc{j}") for j in range(J)]
        s_out = [sem(f"out{g}") for g in range(GE)]
        s_gt_out = [sem(f"gt_out{g}") for g in range(GE)]
        s_sz_out = [sem(f"sz_out{g}") for g in range(GE)]
        block = ctx.enter_context(nc.Block())

        @block.sync
        def _(eng):
            for i in rounds(eng, ROUNDS_E):
                for g in range(GE):
                    b = i * GE + g
                    wait(eng, s_sz_out[g], i * 16)
                    eng.dma_start(A[:, 2 * g, :, :], block_rows(t[f"s{r}"], b)).then_inc(s_load[g], 16)
                    wait(eng, s_sel, (i - 1) * GE + g + 1)
                    carry_waits(eng, w)
                    eng.dma_start(KB[:, g, :, :].rearrange("p j q -> p (j q)"),
                                  t["src_row"][0:1, bass.ds(b * J * P, J * P)].to_broadcast([P, J * P])).then_inc(s_kb[g], 16)
                for g in range(GE):
                    b = i * GE + g
                    eng.wait_ge(s_gt, i * U + 2 * g + 1)
                    eng.dma_start(t["gt"][bass.ds(b * P, P), :], GT[:, 2 * g, :]).then_inc(s_gt_out[g], 16)
                    eng.wait_ge(s_z, (b + 1) * 2)
                    eng.dma_start(block_rows(t["sz"], b), A[:, 2 * g, :, :]).then_inc(s_sz_out[g], 16)
            for g in range(GE):
                eng.wait_ge(s_gt_out[g], 16 * ROUNDS_E)
                eng.wait_ge(s_sz_out[g], 16 * ROUNDS_E)

        @block.gpsimd
        def _(eng):
            gather = lambda out_, g, what, j, sem_: eng.indirect_dma_start(
                out=out_, out_offset=None, in_=t[f"d{r}"],
                in_offset=bass.IndirectOffsetOnAxis(ap=IX[:, g, what, j:j + 1], axis=0),
                bounds_check=EP - 1, oob_is_err=False).then_inc(sem_, 16)
            for i in rounds(eng, ROUNDS_E):
                for g in range(GE):
                    eng.wait_ge(s_ix, i * GE + g + 1)
                    eng.wait_ge(s_load[g], (i + 1) * 16)
                    carry_waits(eng, w)
                    for j in range(J):
                        gather(A[:, 2 * g, j, :], g, MAP, j, s_over[g])
                    wait(eng, s_out[g], i * (16 * J))
                    carry_waits(eng, w)
                    for j in range(J):
                        gather(A[:, 2 * g + 1, j, :], g, HOLD, j, s_hold[g])
                for u in range(U):
                    norm_rstd(nc, eng, nb, w, u, i * U + u + 1)
                for g in range(GE):
                    c = i * GE + g + 1
                    eng.wait_ge(s_tot, c * 2)
                    for j in range(J):
                        wait(eng, s_acc[j], (c - 1) * 16)
                        carry_waits(eng, w)
                        eng.indirect_dma_start(out=t[f"acc{j}"], out_offset=bass.IndirectOffsetOnAxis(ap=IX[:, g, ACC, j:j + 1], axis=0),
                                               in_=TOT[:, g, j, :], in_offset=None, compute_op=ALU.add).then_inc(s_acc[j], 16)
                    eng.wait_ge(s_d, c * 2)
                    carry_waits(eng, w)
                    for j in range(J):
                        eng.indirect_dma_start(out=out, out_offset=bass.IndirectOffsetOnAxis(ap=IX[:, g, OUT, j:j + 1], axis=0),
                                               in_=A[:, 2 * g + 1, j, :], in_offset=None,
                                               bounds_check=N - 1, oob_is_err=False).then_inc(s_out[g], 16)
            for j in range(J):
                eng.wait_ge(s_acc[j], 16 * BLOCKS)
            for g in range(GE):
                eng.wait_ge(s_out[g], 16 * J * ROUNDS_E)

        @block.vector
        def _(eng):
            v = nc.vector
            v.memset(MS[:, :, :, C:M], 1.0).then_inc(s_one, 1)
            for i in rounds(eng, ROUNDS_E):
                tiles = lambda x, g: x[:, bass.ds((i * GE + g) * J, J)]
                for g in range(GE):
                    wait(eng, s_out[g], i * (16 * J))
                    wait(eng, s_over[g], i * (16 * J))
                    wait(eng, s_hold[g], i * (16 * J))
                    for j in range(J):
                        wait(eng, s_acc[j], ((i - 1) * GE + g + 1) * 16)
                    carry_waits(eng, w)
                    for n, name in enumerate(("map_ix", "hold_ix", "acc_ix", "out_d_ix")):
                        last = v.tensor_scalar(IX[:, g, n, :], tiles(k[name], g), 0.0, None, ALU.add)
                    last.then_inc(s_ix, 1)
                for u in range(U):
                    eng.wait_ge((s_hold if u % 2 else s_over)[u // 2], (i + 1) * (16 * J))
                    norm_stats(nc, eng, nb, w, A[:, u, :, :], u, i * U + u + 1)
                for u in range(U):
                    wait(eng, s_nm, (i - 1) * U + u + 1)
                    norm_apply(nc, eng, nb, NR[:, u, :, :], A[:, u, :, :], u, i * U + u + 1)

                def messages(g):
                    c = i * GE + g + 1
                    eng.wait_ge(s_nh, c)
                    wait(eng, s_po, (c - GE) * 2)
                    v.tensor_tensor(MS[:, g, :, 0:C], PM[:, :, :], w["be_row"][:, None, :].to_broadcast([P, J, C]), ALU.add).then_inc(s_ms, 1)

                for g in range(GE):
                    c = i * GE + g + 1
                    eng.wait_ge(s_kb[g], (i + 1) * 16)
                    wait(eng, s_po, (c - GE) * 2)
                    carry_waits(eng, w)
                    v.tensor_tensor(SEL[:, g, :, :], KB[:, g, :, :], tiles(k["src_col"], g)[:, :, None].to_broadcast([P, J, P]), ALU.is_equal).then_inc(s_sel, 1)
                    eng.wait_ge(s_gt, c * 2)
                    wait(eng, s_nh, c - GE)
                    v.tensor_tensor(AD[:, g, :], GT[:, 2 * g, :], GT[:, 2 * g + 1, :], ALU.subtract).then_inc(s_diff, 1)
                    for u, ps_, row, s in ((2 * g, PZ, w["bl_row"], s_z), (2 * g + 1, PD, w["bias_rows"][1], s_d)):
                        eng.wait_ge(s_nm, i * U + u + 1)
                        v.tensor_tensor(A[:, u, :, :], A[:, u, :, :], ps_[:, :, :], ALU.add).then_inc(s, 1)
                        eng.wait_ge(s, c * 2 - 1)
                        v.tensor_tensor(A[:, u, :, :], A[:, u, :, :], row[:, None, :].to_broadcast([P, J, C]), ALU.add).then_inc(s, 1)
                    if g:
                        messages(g - 1)
                messages(GE - 1)

        @block.scalar
        def _(eng):
            for i in rounds(eng, ROUNDS_E):
                def features(u):
                    g = u // 2
                    eng.wait_ge(s_pg, i * U + u + 1)
                    wait(eng, s_diff, (i - 1) * GE + g + 1)
                    if u % 2:
                        wait(eng, s_nh, (i - 1) * GE + g + 1)
                    else:
                        wait(eng, s_gt_out[g], i * 16)
                    carry_waits(eng, w)
                    nc.scalar.activation(GT[:, u, :], PG[:, :, :].rearrange("p j c -> p (j c)"), ACT.Identity,
                                         bias=w["bn_col"][:, 0:1]).then_inc(s_gt, 1)

                def totals(g):
                    c = i * GE + g + 1
                    for j in range(J):
                        wait(eng, s_acc[j], (c - GE) * 16)
                    for q in range(2):
                        eng.wait_ge(s_po, (c - 1) * 2 + q + 1)
                        nc.scalar.activation(TOT[:, g, 2 * q:2 * q + 2, :], PO[q][:, :, 0:M], ACT.Copy).then_inc(s_tot, 1)

                for u in range(U + 1):
                    if u < U:
                        eng.wait_ge(s_tp, i * U + u + 1)
                        nc.scalar.activation(HT[:, u, :], PT[u % 2][:, :, :].rearrange("p j c -> p (j c)"), ACT.Relu).then_inc(s_ht, 1)
                    if u:
                        features(u - 1)
                    if u and u % 2 == 0:
                        g = u // 2 - 1
                        eng.wait_ge(s_diff, i * GE + g + 1)
                        nc.scalar.activation(AD[:, g, :], AD[:, g, :], ACT.Abs).then_inc(s_abs, 1)
                        if g:
                            totals(g - 1)
                totals(GE - 1)

        @block.tensor
        def _(eng):
            eng.wait_ge(s_one, 1)
            for i in rounds(eng, ROUNDS_E):
                def product(u):
                    c = i * GE + u // 2 + 1
                    eng.wait_ge(s_ht, i * U + u + 1)
                    wait(eng, s_gt, i * U + u)
                    nc.tensor.matmul(PG[:, :, :].rearrange("p j c -> p (j c)"), w["wnT"][:, :], HT[:, u, :], start=True, stop=True).then_inc(s_pg, 1)
                    wait(eng, s_d if u % 2 else s_z, (c - 1) * 2)
                    for j in range(J):
                        last = nc.tensor.matmul((PD if u % 2 else PZ)[:, j, :], HT[:, u, j * C:(j + 1) * C],
                                                w["fused3"][:, :] if u % 2 else w["wlT"][:, 0, :], start=True, stop=True)
                    last.then_inc(s_nm, 1)

                def edges(g):
                    c = i * GE + g + 1
                    eng.wait_ge(s_abs, c)
                    wait(eng, s_ms, c - 1)
                    for j in range(J):
                        nc.tensor.matmul(PM[:, j, :], GT[:, 2 * g + 1, j * C:(j + 1) * C], w["weT"][:, 0, :], start=True, stop=False)
                        last = nc.tensor.matmul(PM[:, j, :], AD[:, g, j * C:(j + 1) * C], w["weT"][:, 1, :], start=False, stop=True)
                    last.then_inc(s_nh, 1)
                    eng.wait_ge(s_ms, c)
                    eng.wait_ge(s_sel, c)
                    for q in range(2):
                        wait(eng, s_tot, (c - 2) * 2 + q + 1)
                        for n in range(2):
                            last = nc.tensor.matmul(PO[q][:, n, 0:M], SEL[:, g, 2 * q + n, :], MS[:, g, 2 * q + n, :], start=True, stop=True)
                        last.then_inc(s_po, 1)

                for u in range(U + 1):
                    if u < U:
                        eng.wait_ge(nb.s_normed, (i * U + u + 1) * J)
                        wait(eng, s_ht, i * U + u + 1 - 2)
                        for j in range(J):
                            last = nc.tensor.transpose(PT[u % 2][:, j, :], NR[:, u, j, :], w["ident"][:, :])
                        last.then_inc(s_tp, 1)
                    if u:
                        product(u - 1)
                    if u >= 4 and u % 2 == 0:
                        edges(u // 2 - 2)
                edges(GE - 1)


def edge_outputs(nc, w, k, t, out):
    M = C + 1
    with phase(nc) as ctx:
        sb = lambda n, s, d=F32: ctx.enter_context(nc.sbuf_tensor("o_" + n, s, d))
        sem = lambda n: ctx.semaphore("o_" + n)
        IX = sb("ix", [P, GE, J], I32)
        ACC = sb("acc", [P, GE, J, J, M])
        GT = sb("gt", [P, GE, J * C])
        SZ = sb("sz", [P, GE, J, C])
        UP = sb("up", [P, GE, J, C])
        CN = sb("cn", [P, GE, J, 1])
        PT = [ctx.enter_context(nc.psum_tensor(f"o_pt{n}", [P, J, C], F32)) for n in range(2)]
        PM = [ctx.enter_context(nc.psum_tensor(f"o_pm{n}", [P, J, C], F32)) for n in range(2)]
        s_ix, s_sum, s_cnt, s_tp, s_s, s_mm, s_up, s_out_in = (sem(n) for n in "ix sum cnt tp s mm up out_in".split())
        s_load = [sem(f"load{g}") for g in range(GE)]
        s_out = [sem(f"out{g}") for g in range(GE)]
        LOADS = 16 * (J + 2)
        block = ctx.enter_context(nc.Block())

        @block.sync
        def _(eng):
            for i in rounds(eng, ROUNDS_E):
                for g in range(GE):
                    b = i * GE + g
                    wait(eng, s_out[g], i * (16 * J))
                    carry_waits(eng, w)
                    for a in range(J):
                        eng.dma_start(ACC[:, g, a, :, :], block_rows(t[f"acc{a}"], b)).then_inc(s_load[g], 16)
                    eng.dma_start(GT[:, g, :], t["gt"][bass.ds(b * P, P), :]).then_inc(s_load[g], 16)
                    eng.dma_start(SZ[:, g, :, :], block_rows(t["sz"], b)).then_inc(s_load[g], 16)

        @block.gpsimd
        def _(eng):
            for i in rounds(eng, ROUNDS_E):
                for g in range(GE):
                    eng.wait_ge(s_ix, i * GE + g + 1)
                    eng.wait_ge(s_out_in, i * GE + g + 1)
                    carry_waits(eng, w)
                    for j in range(J):
                        eng.indirect_dma_start(out=out, out_offset=bass.IndirectOffsetOnAxis(ap=IX[:, g, j:j + 1], axis=0),
                                               in_=SZ[:, g, j, :], in_offset=None,
                                               bounds_check=N - 1, oob_is_err=False).then_inc(s_out[g], 16)
            for g in range(GE):
                eng.wait_ge(s_out[g], 16 * J * ROUNDS_E)

        @block.vector
        def _(eng):
            v = nc.vector
            for i in rounds(eng, ROUNDS_E):
                for g in range(GE):
                    c = i * GE + g + 1
                    wait(eng, s_out[g], i * (16 * J))
                    carry_waits(eng, w)
                    v.tensor_scalar(IX[:, g, :], k["out_s_ix"][:, bass.ds((i * GE + g) * J, J)], 0.0, None, ALU.add).then_inc(s_ix, 1)
                    eng.wait_ge(s_load[g], (i + 1) * LOADS)
                    carry_waits(eng, w)
                    v.tensor_tensor(ACC[:, g, 0, :, :], ACC[:, g, 0, :, :], ACC[:, g, 1, :, :], ALU.add).then_inc(s_sum, 1)
                    v.tensor_tensor(ACC[:, g, 2, :, :], ACC[:, g, 2, :, :], ACC[:, g, 3, :, :], ALU.add).then_inc(s_sum, 1)
                    eng.wait_ge(s_sum, c * 3 - 1)
                    v.tensor_tensor(ACC[:, g, 0, :, :], ACC[:, g, 0, :, :], ACC[:, g, 2, :, :], ALU.add).then_inc(s_sum, 1)
                    eng.wait_ge(s_sum, c * 3)
                    v.tensor_scalar(CN[:, g, :, :], ACC[:, g, 0, :, C:M], 1.0, None, ALU.max).then_inc(s_cnt, 1)
                    eng.wait_ge(s_cnt, c * 2 - 1)
                    v.reciprocal(CN[:, g, :, :], CN[:, g, :, :]).then_inc(s_cnt, 1)
                for g in range(GE):
                    c = i * GE + g + 1
                    eng.wait_ge(s_tp, c)
                    v.tensor_tensor(GT[:, g, :], PT[g % 2][:, :, :].rearrange("p j c -> p (j c)"), GT[:, g, :], ALU.add).then_inc(s_s, 1)
                for g in range(GE):
                    c = i * GE + g + 1
                    eng.wait_ge(s_mm, c)
                    eng.wait_ge(s_cnt, c * 2)
                    v.tensor_tensor(UP[:, g, :, :], PM[g % 2][:, :, :], CN[:, g, :, :].to_broadcast([P, J, C]), ALU.mult).then_inc(s_up, 1)
                    eng.wait_ge(s_up, c)
                    v.tensor_tensor(SZ[:, g, :, :], SZ[:, g, :, :], UP[:, g, :, :], ALU.add).then_inc(s_out_in, 1)

        @block.tensor
        def _(eng):
            for i in rounds(eng, ROUNDS_E):
                for g in range(GE):
                    c = i * GE + g + 1
                    eng.wait_ge(s_sum, c * 3)
                    wait(eng, s_s, (i * GE + g - 1) if g >= 2 else (i - 1) * GE + GE)
                    for j in range(J):
                        last = nc.tensor.transpose(PT[g % 2][:, j, :], ACC[:, g, 0, j, 0:C], w["ident"][:, :])
                    last.then_inc(s_tp, 1)
                for g in range(GE):
                    c = i * GE + g + 1
                    eng.wait_ge(s_s, c)
                    wait(eng, s_up, (i * GE + g - 1) if g >= 2 else (i - 1) * GE + GE)
                    for j in range(J):
                        last = nc.tensor.matmul(PM[g % 2][:, j, :], GT[:, g, j * C:(j + 1) * C], w["wlT"][:, 1, :], start=True, stop=True)
                    last.then_inc(s_mm, 1)


def edge_layers(nc, w, k, t):
    held = lambda ctx, name, width: {s: ctx.enter_context(nc.sbuf_tensor(f"{name}_{s}", [P, T, width], F32)) for s in ("src", "dst")}
    weights = lambda ctx, name, heads: [ctx.enter_context(nc.sbuf_tensor(f"{name}_{s}_weight", [P, T, heads], F32)) for s in ("edge", "self")]
    with ExitStack() as ctx:
        keep, (wm, ws) = held(ctx, "layer0", C + 2), weights(ctx, "layer0", 1)
        for r in range(3):
            project(nc, w, k, t, r, 1, w["aug0"][:, r, :], w["b0_rows"][:, r, :], False, True, r > 0, r == 2, keep)
            attend(nc, w, k, r, 1, keep, wm, ws)
            aggregate(nc, w, k, t, r, "sigmoid", 1, keep, wm, ws, w["b0_rows"][:, r, :], r == 2)
    with ExitStack() as ctx:
        keep = held(ctx, "layer1", C)
        relate(nc, w, k, t, 3, keep)
        aggregate(nc, w, k, t, 3, "relu", 1, keep, None, None, None, False)
    with ExitStack() as ctx:
        keep, (wm, ws) = held(ctx, "layer2", C + 2 * HEADS), weights(ctx, "layer2", HEADS)
        project(nc, w, k, t, 4, HEADS, w["aug2"][:, :], w["bias_rows"][0][:, :], True, False, True, False, keep)
        attend(nc, w, k, 4, HEADS, keep, wm, ws)
        aggregate(nc, w, k, t, 4, "linear", HEADS, keep, wm, ws, w["bias_rows"][0][:, :], False)


def program(nc, ins, out):
    with ExitStack() as ctx:
        w = alloc_weights(nc, ctx)
        setup(nc, w, ins)
        local_chain(nc, ins["x"], out, w, G=7, rounds_n=14)
        t = alloc_tables(nc)
        k = alloc_keys(nc, ctx, w)
        keys(nc, w, k, t, ins)
        gather_inputs(nc, w, k, t, ins["x"])
        edge_layers(nc, w, k, t)
        edge_messages(nc, w, k, t, 5, out)
        edge_outputs(nc, w, k, t, out)


def kernel(**a):
    import numpy as np
    import concourse.bacc as bacc
    from concourse.bass_utils import run_bass_kernel_spmd

    a = {k: np.asarray(v) for k, v in a.items()}
    t = lambda v, *axes: np.ascontiguousarray(np.transpose(v, axes or None))
    arrays = {
        "x": a["x"], "src": a["src"], "dst": a["dst"], "etype": a["edge_type_100"],
        "L0_Ws": a["L0_gnn_Ws"], "L0_WsT": t(a["L0_gnn_Ws"], 0, 2, 1),
        "L0_as": t(a["L0_gnn_att_src"]), "L0_ad": t(a["L0_gnn_att_dst"]),
        "L0_b": a["L0_gnn_bias"], "L0_bT": t(a["L0_gnn_bias"]),
        "L1_basis": a["L1_gnn_basis_weights"], "L1_coef": a["L1_gnn_coefficients"], "L1_loop": a["L1_gnn_loop_weight"],
        "L2_W": a["L2_gnn_W_src"], "L2_WT": t(a["L2_gnn_W_src"]),
        "L2_as": a["L2_gnn_attn_src"].reshape(128, 1), "L2_ad": a["L2_gnn_attn_dst"].reshape(128, 1),
        "L2_b": a["L2_gnn_bias"].reshape(1, 128),
        "L3_Wn": a["L3_gnn_W_neigh"], "L3_WnT": t(a["L3_gnn_W_neigh"]), "L3_bn": a["L3_gnn_b_neigh"].reshape(128, 1),
        "L3_WeT": t(a["L3_gnn_W_edge"]), "L3_be": a["L3_gnn_b_edge"].reshape(1, 128),
        "L3_WlT": t(a["L3_gnn_W_lin"]), "L3_bl": a["L3_gnn_b_lin"].reshape(1, 128),
    }
    nc = bacc.Bacc("TRN2", target_bir_lowering=False, num_devices=1)
    ins = {k: nc.dram_tensor("in_" + k, v.shape, mybir.dt.from_np(v.dtype), kind="ExternalInput").ap() for k, v in arrays.items()}
    out = nc.dram_tensor("out", (N, C), F32, kind="ExternalOutput").ap()
    program(nc, ins, out)
    r = run_bass_kernel_spmd(nc, [{"in_" + k: v for k, v in arrays.items()}], core_ids=[0])
    return r.results[0]["out"]
```

```python
import concourse.bass as bass
from concourse import mybir
from contextlib import ExitStack, contextmanager
from itertools import count

F32 = mybir.dt.float32
I32 = mybir.dt.int32
ALU = mybir.AluOpType
ACT = mybir.ActivationFunctionType
AX = mybir.AxisListType

N = 50000
C = 128
E = 12500
P = 128
BIG = 1.0e30
LN_EPS = 1e-5
REGISTERS = count()
GAT_EPS = 1e-16
SLOPE = 0.2
HEADS = 8
BASES = 4


class Phase(ExitStack):

    def __init__(self, nc):
        super().__init__()
        self.nc, self.semaphores = nc, []

    def semaphore(self, name):
        self.semaphores.append(self.nc.alloc_semaphore(name))
        return self.semaphores[-1]


@contextmanager
def phase(nc):
    with Phase(nc) as ctx:
        yield ctx
    nc.clear_and_free_semaphores(ctx.semaphores)
    nc.all_engine_barrier()


def carry_waits(eng, w):
    eng.sem_inc(w["carrier"], 1)


class Affine:

    def __init__(self, register, a, b, first=1):
        self.register, self.a, self.b, self.first = register, a, b, first

    def __mul__(self, n):
        return Affine(self.register, self.a * n, self.b * n, self.first)

    def __add__(self, n):
        return Affine(self.register, self.a, self.b + n, self.first)

    def __sub__(self, n):
        return self + -n

    def __floordiv__(self, n):
        assert self.a % n == 0
        return Affine(self.register, self.a // n, self.b // n, self.first)

    def value(self):
        return self.register * self.a + self.b


def number(v):
    return v.value() if isinstance(v, Affine) else v


def wait(eng, sem, value):
    if isinstance(value, Affine):
        assert value.first * value.a + value.b > 0
        value = value.value()
    if not (isinstance(value, int) and value <= 0):
        eng.wait_ge(sem, value)


def rounds(eng, n):
    yield 0
    if n > 1:
        with eng.Fori(1, n) as i:
            yield i


def stream(eng, *steps):
    deepest = max(lag for _, lag in steps)
    assert deepest <= GE
    with eng.register(f"stream_round_{next(REGISTERS)}") as own:
        def turn(n, round_=None):
            for step, lag in steps:
                if round_ is not None:
                    step(Affine(round_, GE, n - lag, 2), (n - lag) % GE)
                elif 0 <= n - lag < BLOCKS:
                    step(n - lag, (n - lag) % GE)

        for n in range(2 * GE):
            turn(n)
        with eng.Fori(2, ROUNDS_E) as i:
            for n in range(GE):
                eng.reg_mov(own, i)
                turn(n, eng.snap(own))
        for n in range(BLOCKS, BLOCKS + deepest):
            turn(n)


T = 100
EP = T * P
J = 4
GE = 5
BLOCKS = T // J
ROUNDS_E = BLOCKS // GE
NODES = 50048
WORDS = 1 + J
CHAIN_ROUNDS = 7
PER = -(-T // (CHAIN_ROUNDS - 1))
TX = PER * CHAIN_ROUNDS
SKIP = 300000
DUMP = EP
FULL_ROWS = E // P
TAIL = E - FULL_ROWS * P


def alloc_keys(nc, ctx, w):
    sb = lambda n, s, d=F32: ctx.enter_context(nc.sbuf_tensor("k_" + n, s, d))
    k = {
        "dst_col": sb("dst_col", [P, T]), "src_col": sb("src_col", [P, T]), "prev_col": sb("prev_col", [P, T]),
        "map_ix": sb("map_ix", [P, T], I32),
        "hold_ix": sb("hold_ix", [P, T], I32),
        "acc_ix": sb("acc_ix", [P, T], I32),
        "out_d_ix": sb("out_d_ix", [P, T], I32), "out_s_ix": sb("out_s_ix", [P, T], I32),
        "coef": sb("coef", [P, T, BASES]),
        "is_last": sb("is_last", [T, P]), "last_pen": sb("last_pen", [T, P]),
        "pre_pen": sb("pre_pen", [T, P]), "post": sb("post", [T, P]),
        "pen0": sb("pen0", [T, HEADS, P]), "nl0": sb("nl0", [T, HEADS, P]),
        "row_pen": sb("row_pen", [HEADS, T]), "row_nl": sb("row_nl", [HEADS, T]),
    }
    return k


def alloc_search(nc, ctx):
    sb = lambda n, s, d=F32: ctx.enter_context(nc.sbuf_tensor("f_" + n, s, d))
    return {
        "src_ix": sb("src_ix", [P, TX], I32), "dst_ix": sb("dst_ix", [P, TX], I32),
        "number": sb("number", [P, T], I32), "number_f": sb("number_f", [P, T]),
        "own_at": sb("own_at", [P, T], I32),
        "map_at": sb("map_at", [P, TX], I32),
        "found": sb("found", [P, TX, WORDS]),
        "tile_last": sb("tile_last", [P, T]),
        "dump": sb("dump", [P, 1]),
    }


def alloc_tables(nc):
    d = lambda n, s, t=F32: nc.dram_tensor("t_" + n, s, t).ap()
    t = {"dst_pad": d("dst_pad", (EP + 2, 1)), "src_row": d("src_row", (1, EP)), "type_row": d("type_row", (1, EP)),
         "dst_row": d("dst_row", (1, EP)),
         "maps": d("maps", (NODES * WORDS, 1), I32), "dout": d("dout", (EP, C)), "sz": d("sz", (EP, C)),
         "gt": d("gt", (BLOCKS * P, J * C)),
         "xs": d("xs", (TX * P, C)), "xd": d("xd", (TX * P, C))}
    for r in range(6):
        t[f"s{r}"] = d(f"s{r}", (EP, C))
        t[f"d{r}"] = d(f"d{r}", (EP, C))
    t["acc"] = d("acc", (EP + P, C + 1))
    return t


def keys(nc, w, k, f, t, ins):
    with phase(nc) as ctx:
        sb = lambda n, s, d=F32: ctx.enter_context(nc.sbuf_tensor("q_" + n, s, d))
        sem = lambda n: ctx.semaphore("q_" + n)
        RI = sb("ri", [T, 3, P], I32)
        RF = sb("rf", [T, 3, P])
        PN = sb("pn", [T, 2, P])
        FF = sb("ff", [T, P])
        FR = sb("fr", [T, P])
        LR = sb("lr", [T, P])
        ZERO = sb("zero", [T, P])
        ENDS = sb("ends", [2, 1])
        ENDS_I = sb("ends_i", [2, 1], I32)
        LASTP = sb("lastp", [P, 1])
        s_cf_pe = sem("cf_pe")
        s_loop = sem("loop")
        IR = sb("ir", [T, P], I32)
        IRF = sb("irf", [T, P])
        HV = sb("hv", [T, P])
        HL = sb("hl", [T, P])
        HX = sb("hx", [T, P])
        ROW8 = sb("row8", [T, 2, HEADS])
        HC = sb("hc", [1, T])
        HS = sb("hs", [1, T])
        HO = sb("ho", [T, 1])
        ID, IDF, TL, DUMPF, M2, MI = (f[n] for n in "number number_f tile_last dump own_at map_at".split())
        LC = sb("lc", [P, T])
        TMP = sb("tmp", [P, T])
        DUP = sb("dup", [P, J])
        TMQ = sb("tmq", [P, T])
        DUMPC = sb("dumpc", [P, 1], I32)
        M1 = sb("m1", [P, T], I32)
        KEEP = sb("keep", [P, NODES * WORDS // P], I32)
        UPPER = sb("upper", [P, P])
        SB_ = sb("sbc", [P, 2, J * P])
        EQ = sb("eq", [P, J, P])
        TB = sb("tb", [P, 2, J * P])
        OH = sb("oh", [P, 2, J * P])
        RELI = sb("reli", [P, 1], I32)
        RELF = sb("relf", [P, 1])
        COEF = sb("coefs", [100, BASES])
        ZT = sb("zt", [P, (EP + P) * (C + 1) // P // 3])
        PS = ctx.enter_context(nc.psum_tensor("q_ps", [P, 512], F32))
        PQ = ctx.enter_context(nc.psum_tensor("q_pq", [P, 512], F32))
        PC = ctx.enter_context(nc.psum_tensor("q_pc", [P, 512], F32))

        s_fill, s_in, s_rf, s_pad, s_pn, s_v, s_pe, s_pool = (sem(n) for n in "fill in rf pad pn v pe pool".split())
        s_map1, s_zero, s_ix, s_coef_in = (sem(n) for n in "map1 zero ix coef_in".split())
        s_tb = [sem(f"tb{b}") for b in range(2)]
        s_eq, s_tl, s_oh, s_cf, s_keep, s_shape = (sem(n) for n in "eq tl oh cf keep shape".split())
        block = ctx.enter_context(nc.Block())
        ident_t = w["ident"][0:T, 0:T]
        ZN = 3

        @block.sync
        def _(eng):
            eng.wait_ge(s_fill, 3)
            for n, name in enumerate(("dst", "src", "etype")):
                v = ins[name]
                eng.dma_start(RI[0:FULL_ROWS, n, :], v[0:FULL_ROWS * P].rearrange("(t p) -> t p", p=P)).then_inc(s_in, 16)
                eng.dma_start(RI[FULL_ROWS:FULL_ROWS + 1, n, 0:TAIL], v[FULL_ROWS * P:E].rearrange("(o p) -> o p", o=1)).then_inc(s_in, 16)
            eng.dma_start(COEF[:, :], ins["L1_coef"]).then_inc(s_coef_in, 16)
            eng.dma_start(t["maps"].rearrange("(p n) o -> p (n o)", p=P), KEEP[:, :]).then_inc(s_keep, 16)
            eng.wait_ge(s_rf, 1)
            rows = lambda x: x.rearrange("o (t p) -> (o t) p", p=P)
            eng.dma_start(rows(t["dst_row"]), RF[:, 0, :]).then_inc(s_pad, 16)
            eng.dma_start(rows(t["src_row"]), RF[:, 1, :]).then_inc(s_pad, 16)
            eng.dma_start(rows(t["type_row"]), RF[:, 2, :]).then_inc(s_pad, 16)
            eng.dma_start(t["dst_pad"][1:EP + 1, :].rearrange("(t p) o -> t (p o)", p=P), RF[:, 0, :]).then_inc(s_pad, 16)
            with nc.allow_non_contiguous_dma(reason="two words"):
                eng.dma_start(t["dst_pad"][0:EP + 2:EP + 1, :], ENDS[:, :]).then_inc(s_pad, 16)
            eng.wait_ge(s_pad, 80)
            eng.dma_start(PN[:, 0, :], t["dst_pad"][0:EP, :].rearrange("(t p) o -> t (p o)", p=P)).then_inc(s_pn, 16)
            eng.dma_start(PN[:, 1, :], t["dst_pad"][2:EP + 2, :].rearrange("(t p) o -> t (p o)", p=P)).then_inc(s_pn, 16)

            def rows_in(b, buf):
                eng.dma_start(SB_[:, buf, :], t["src_row"][0:1, bass.ds(b * J * P, J * P)].to_broadcast([P, J * P])).then_inc(s_tb[buf], 16)
                eng.dma_start(TB[:, buf, :], t["type_row"][0:1, bass.ds(b * J * P, J * P)].to_broadcast([P, J * P])).then_inc(s_tb[buf], 16)

            rows_in(0, 0)
            for i in rounds(eng, (BLOCKS - 1) // 2):
                for h in range(2):
                    b = i * 2 + h
                    wait(eng, s_tl, b)
                    rows_in(b + 1, 1 - h)
            flat = t["acc"].rearrange("(p n) c -> p (n c)", p=P)
            n = flat.shape[1] // ZN
            for z in range(ZN):
                eng.dma_start(flat[:, z * n:(z + 1) * n], ZT[:, 0:n]).then_inc(s_zero, 16)
            eng.wait_ge(s_zero, 16 * ZN)

        @block.gpsimd
        def _(eng):
            nc.gpsimd.memset(RI[:, 0:2, :], N).then_inc(s_fill, 1)
            nc.gpsimd.memset(RI[:, 2:3, :], 0).then_inc(s_fill, 1)
            nc.gpsimd.memset(KEEP[:, :], SKIP).then_inc(s_fill, 1)
            nc.gpsimd.iota(ID[:, :], [[P, T]], base=0, channel_multiplier=1).then_inc(s_pool, 1)
            nc.gpsimd.iota(IR[:, :], [[1, P]], base=0, channel_multiplier=P).then_inc(s_pool, 1)
            nc.gpsimd.iota(DUMPC[:, :], [[1, 1]], base=DUMP, channel_multiplier=1).then_inc(s_pool, 1)
            nc.gpsimd.iota(RELI[:, :], [[1, 1]], base=0, channel_multiplier=1).then_inc(s_pool, 1)
            nc.gpsimd.affine_select(out=UPPER[:, :], in_=w["ones"][:, :], compare_op=ALU.is_gt, fill=0.0, base=0,
                                    pattern=[[1, P]], channel_multiplier=-1).then_inc(s_pool, 1)
            nc.gpsimd.iota(ENDS_I[:, :], [[1, 1]], base=-2, channel_multiplier=1).then_inc(s_pool, 1)
            eng.wait_ge(s_keep, 16)
            eng.wait_ge(s_ix, 1)
            for c in range(T):
                eng.indirect_dma_start(out=t["maps"], out_offset=bass.IndirectOffsetOnAxis(ap=M1[:, c:c + 1], axis=0),
                                       in_=ID[:, c:c + 1], in_offset=None, bounds_check=NODES * WORDS - 1, oob_is_err=False).then_inc(s_map1, 16)
            eng.wait_ge(s_map1, 16 * T)

        @block.tensor
        def _(eng):
            eng.wait_ge(s_rf, 1)
            nc.tensor.transpose(PS[:, 0:T], RF[:, 0, :], ident_t).then_inc(s_pe, 1)
            nc.tensor.transpose(PS[:, 128:128 + T], RF[:, 1, :], ident_t).then_inc(s_pe, 1)
            eng.wait_ge(s_shape, 1)
            nc.tensor.transpose(PS[:, 256:256 + T], k["is_last"][:, :], ident_t).then_inc(s_pe, 1)
            nc.tensor.transpose(PQ[0:HEADS, 0:T], ROW8[:, 0, :], ident_t).then_inc(s_pe, 1)
            nc.tensor.transpose(PQ[0:HEADS, 128:128 + T], ROW8[:, 1, :], ident_t).then_inc(s_pe, 1)
            nc.tensor.transpose(PQ[0:1, 256:256 + T], HL[:, 0:1], ident_t).then_inc(s_pe, 1)
            eng.wait_ge(s_shape, 2)
            nc.tensor.transpose(PQ[0:T, 400:401], HS[0:1, :], w["ident"][0:1, 0:1]).then_inc(s_pe, 1)
            eng.wait_ge(s_shape, 3)
            nc.tensor.transpose(PS[:, 384:384 + T], HX[:, :], ident_t).then_inc(s_pe, 1)
            eng.wait_ge(s_coef_in, 16)
            for i in rounds(eng, BLOCKS):
                wait(eng, s_tl, i)
                eng.wait_ge(s_oh, i + 1)
                for j in range(J):
                    last = nc.tensor.matmul(PC[:, 4 * j:4 * j + 4], OH[0:100, 0, j * P:(j + 1) * P], COEF[:, :], start=True, stop=True)
                last.then_inc(s_cf_pe, 1)

        @block.vector
        def _(eng):
            n = [0]

            def done(ins_):
                n[0] += 1
                ins_.then_inc(s_v, 1)
                eng.wait_ge(s_v, n[0])

            v = nc.vector
            done(v.memset(ZERO[:, :], 0.0))
            done(v.memset(ZT[:, :], 0.0))
            eng.wait_ge(s_pool, 6)
            done(v.tensor_copy(ENDS[:, :], ENDS_I[:, :]))
            done(v.tensor_copy(IDF[:, :], ID[:, :]))
            done(v.tensor_copy(IRF[:, :], IR[:, :]))
            done(v.tensor_copy(DUMPF[:, :], DUMPC[:, :]))
            done(v.tensor_copy(RELF[:, :], RELI[:, :]))
            eng.wait_ge(s_in, 96)
            v.tensor_copy(RF[:, :, :], RI[:, :, :]).then_inc(s_rf, 1)
            eng.wait_ge(s_pn, 32)
            done(v.tensor_tensor(FF[:, :], RF[:, 0, :], PN[:, 0, :], ALU.not_equal))
            done(v.tensor_tensor(k["is_last"][:, :], RF[:, 0, :], PN[:, 1, :], ALU.not_equal))
            done(v.tensor_scalar(k["last_pen"][:, :], k["is_last"][:, :], -1.0, BIG, ALU.add, ALU.mult))
            done(v.tensor_tensor_scan(FR[:, :], ZERO[:, :], FF[:, :], 0.0, ALU.add, ALU.max))
            done(v.tensor_tensor_scan(LR[:, ::-1], ZERO[:, :], k["is_last"][:, ::-1], 0.0, ALU.add, ALU.max))
            done(v.tensor_scalar(k["pre_pen"][:, :], FR[:, :], -BIG, None, ALU.mult))
            done(v.tensor_scalar(k["post"][:, :], LR[:, :], -1.0, 1.0, ALU.mult, ALU.add))
            for h in range(HEADS):
                done(v.tensor_scalar(k["pen0"][:, h, :], FF[:, :], -BIG, None, ALU.mult))
                done(v.tensor_scalar(k["nl0"][:, h, :], k["is_last"][:, :], -1.0, 1.0, ALU.mult, ALU.add))
            done(v.memset(k["pen0"][:, :, 0:1], -BIG))
            done(v.memset(k["nl0"][:, :, P - 1:P], 0.0))
            for h in range(HEADS):
                done(v.tensor_scalar(ROW8[:, 0, h:h + 1], FR[:, P - 1:P], -BIG, None, ALU.mult))
                done(v.tensor_scalar(ROW8[:, 1, h:h + 1], LR[:, 0:1], -1.0, 1.0, ALU.mult, ALU.add))
            done(v.tensor_tensor(HV[:, :], IRF[:, :], k["is_last"][:, :], ALU.mult))
            done(v.tensor_tensor_scan(HL[:, ::-1], k["nl0"][:, 0, ::-1], HV[:, ::-1], 0.0, ALU.mult, ALU.add))
            v.memset(HS[:, :], 0.0).then_inc(s_shape, 1)
            eng.wait_ge(s_pe, 6)
            done(v.tensor_copy(k["dst_col"][:, :], PS[:, 0:T]))
            done(v.tensor_copy(k["src_col"][:, :], PS[:, 128:128 + T]))
            done(v.tensor_copy(LC[:, :], PS[:, 256:256 + T]))
            done(v.tensor_copy(k["row_pen"][:, :], PQ[0:HEADS, 0:T]))
            done(v.tensor_copy(k["row_nl"][:, :], PQ[0:HEADS, 128:128 + T]))
            eng.wait_ge(s_shape, 1)
            done(v.tensor_tensor_scan(HC[:, ::-1], k["row_nl"][0:1, ::-1], PQ[0:1, 256:256 + T][:, ::-1], 0.0, ALU.mult, ALU.add))
            v.tensor_copy(HS[:, 0:T - 1], HC[:, 1:T]).then_inc(s_shape, 1)
            eng.wait_ge(s_pe, 7)
            done(v.tensor_copy(HO[:, :], PQ[0:T, 400:401]))
            done(v.tensor_scalar(HV[:, :], k["post"][:, :], HO[:, 0:1], None, ALU.mult))
            v.tensor_tensor(HX[:, :], HV[:, :], HL[:, :], ALU.add).then_inc(s_shape, 1)
            eng.wait_ge(s_pe, 8)
            done(v.tensor_copy(k["hold_ix"][:, :], PS[:, 384:384 + T]))
            for name in ("src_ix", "dst_ix", "map_at"):
                done(v.memset(f[name][:, T:TX], 0))
            done(v.tensor_scalar(f["dst_ix"][:, 0:T], k["dst_col"][:, :], float(N - 1), None, ALU.min))
            done(v.tensor_scalar(f["src_ix"][:, 0:T], k["src_col"][:, :], float(N - 1), None, ALU.min))
            done(v.tensor_copy(MI[:, 0:T], k["src_col"][:, :]))

            def where(out, cond, value, scale, add, other):
                done(v.tensor_scalar(TMP[:, :], value, scale, add - other, ALU.mult, ALU.add))
                done(v.tensor_tensor(TMQ[:, :], TMP[:, :], cond, ALU.mult))
                done(v.tensor_scalar(out, TMQ[:, :], float(other), None, ALU.add))

            where(M1[:, :], LC[:, :], k["dst_col"][:, :], float(WORDS), 0.0, float(SKIP))
            v.memset(ZERO[:, 0:1], 0.0).then_inc(s_ix, 1)
            where(k["out_d_ix"][:, :], LC[:, :], k["dst_col"][:, :], 1.0, 0.0, float(SKIP))
            done(v.tensor_scalar(LASTP[:, :], RELF[:, :], float(P - 1), None, ALU.is_equal))
            done(v.memset(k["prev_col"][:, :], -5.0))
            done(v.tensor_scalar(TMP[:, 0:T - 1], k["dst_col"][:, 0:T - 1], 5.0, LASTP[:, 0:1], ALU.add, ALU.mult))
            done(v.tensor_scalar(k["prev_col"][:, 1:T], TMP[:, 0:T - 1], -5.0, None, ALU.add))
            STEPS = 5

            def block_of(b, buf, loads):
                eng.wait_ge(s_tb[buf], loads * 32)
                carry_waits(eng, w)
                cols = lambda x: x[:, bass.ds(b * J, J)]
                rows = lambda x: x.rearrange("p (j q) -> p j q", j=J)
                v.tensor_tensor(EQ[:, :, :], rows(SB_[:, buf, :]), cols(k["src_col"])[:, :, None].to_broadcast([P, J, P]), ALU.is_equal).then_inc(s_loop, 1)
                v.tensor_scalar(OH[:, 0, :], TB[:, buf, :], RELF[:, 0:1], None, ALU.is_equal).then_inc(s_oh, 1)
                eng.wait_ge(s_loop, b * STEPS + 1)
                v.tensor_tensor(EQ[:, :, :], EQ[:, :, :], UPPER[:, None, :].to_broadcast([P, J, P]), ALU.mult).then_inc(s_loop, 1)
                eng.wait_ge(s_loop, b * STEPS + 2)
                v.tensor_reduce(DUP[:, :], EQ[:, :, :], AX.X, ALU.max).then_inc(s_loop, 1)
                eng.wait_ge(s_loop, b * STEPS + 3)
                v.tensor_scalar(cols(TL), DUP[:, :], -1.0, 1.0, ALU.mult, ALU.add).then_inc(s_loop, 1)
                eng.wait_ge(s_cf_pe, b + 1)
                carry_waits(eng, w)
                v.tensor_scalar(k["coef"][:, bass.ds(b * J, J), :], PC[:, 0:J * BASES].rearrange("p (j b) -> p j b", j=J), 1.0, None, ALU.mult).then_inc(s_loop, 1)
                eng.wait_ge(s_loop, (b + 1) * STEPS)
                v.memset(DUP[:, :], 0.0).then_inc(s_tl, 1)

            block_of(0, 0, 1)
            with eng.Fori(0, (BLOCKS - 1) // 2) as i:
                block_of(i * 2 + 1, 1, i + 1)
                block_of(i * 2 + 2, 0, i + 2)
            eng.wait_ge(s_tl, BLOCKS)
            where(M2[:, :], TL[:, :], k["src_col"][:, :], float(WORDS), 1.0, float(SKIP))
            for j in range(1, J):
                done(v.tensor_scalar(M2[:, j::J], M2[:, j::J], float(j), None, ALU.add))


def rows_found(nc, k, f):
    with phase(nc) as ctx:
        sb = lambda n, s, d=F32: ctx.enter_context(nc.sbuf_tensor("n_" + n, s, d))
        OWNER, OWN, TMP, TMQ = (sb(n, [P, T]) for n in "owner own tmp tmq".split())
        s_v = ctx.semaphore("n_v")
        block = ctx.enter_context(nc.Block())

        @block.vector
        def _(eng):
            v = nc.vector
            n = [0]

            def done(ins_):
                n[0] += 1
                ins_.then_inc(s_v, 1)
                eng.wait_ge(s_v, n[0])

            done(v.tensor_copy(k["map_ix"][:, :], f["found"][:, 0:T, 0]))
            done(v.tensor_copy(OWNER[:, :], f["found"][:, 0:T, 1]))
            for j in range(1, J):
                done(v.tensor_tensor(OWNER[:, :], OWNER[:, :], f["found"][:, 0:T, 1 + j], ALU.min))
            done(v.tensor_tensor(OWN[:, :], OWNER[:, :], f["number_f"][:, :], ALU.is_equal))
            done(v.tensor_scalar(TMP[:, :], k["src_col"][:, :], float(-SKIP), None, ALU.add))
            done(v.tensor_tensor(TMQ[:, :], TMP[:, :], OWN[:, :], ALU.mult))
            done(v.tensor_scalar(k["out_s_ix"][:, :], TMQ[:, :], float(SKIP), None, ALU.add))
            done(v.tensor_scalar(TMP[:, :], OWNER[:, :], f["dump"][:, 0:1], None, ALU.subtract))
            done(v.tensor_tensor(TMQ[:, :], TMP[:, :], f["tile_last"][:, :], ALU.mult))
            done(v.tensor_scalar(k["acc_ix"][:, :], TMQ[:, :], f["dump"][:, 0:1], None, ALU.add))


def local_chain(nc, x, out, w, f, t, G, rounds_n):
    J = 4
    W = J * C
    SIGMOIDS = 4
    BANKS = 4
    LEAD = 4
    BATCHES = ((0, LEAD), (LEAD, G))
    batch_of = lambda g: 0 if g < LEAD else 1
    x_v = x.rearrange("(a j) c -> a (j c)", j=J)
    out_v = out.rearrange("(a j) c -> a (j c)", j=J)
    last_row = (N - P * J) // J

    with phase(nc) as ctx:
        sb = lambda n, s: ctx.enter_context(nc.sbuf_tensor(n, s, F32))
        sb_i = lambda n, s: ctx.enter_context(nc.sbuf_tensor(n, s, I32))
        sem = lambda n: ctx.semaphore(n)

        class Group:

            def __init__(self, h):
                self.h = h
                self.X = sb(f"a{h}_x", [P, G, W])
                self.HT = sb(f"a{h}_ht", [P, G, W])
                self.SG = sb(f"a{h}_sg", [P, SIGMOIDS, W])
                self.ST = sb(f"a{h}_st", [P, G, J, 6])
                self.MV = sb(f"a{h}_mv", [P, G, J, 2])
                self.VE = sb(f"a{h}_ve", [P, G, J])
                self.RS = sb(f"a{h}_rs", [P, G, J])
                self.NM = sb(f"a{h}_nm", [P, G, J])
                self.PS = [ctx.enter_context(nc.psum_tensor(f"a{h}_ps{n}", [P, W], F32)) for n in range(BANKS)]
                self.loaded = [sem(f"a{h}_loaded{g}") for g in range(G)]
                self.stored = [sem(f"a{h}_stored{g}") for g in range(G)]
                (self.s_st, self.s_mv, self.s_ve, self.s_rs, self.s_nm, self.s_nr, self.s_tp, self.s_ht, self.s_mm,
                 self.s_sg, self.s_h, self.s_bk, self.s_lm, self.s_xb, self.s_x, self.s_na) = (
                    sem(f"a{h}_{n}") for n in ("stats moments var_eps rstd neg_mean_rstd normed_dve transposed ht_ready "
                                               "product sigmoid h_updated back layer_product x_biased x_updated normed_act").split())

        groups = [Group(h) for h in range(2)]

        GI = sb_i("a_gi", [P, 2, PER])
        GX = sb("a_gx", [P, 2, PER, C])
        s_owner = [sem(f"a_owner{j}") for j in range(J)]
        s_index, s_ends, s_ends_out = (sem(n) for n in "a_index a_ends a_ends_out".split())

        ACT_NORMS = {0: (1, 2, 3, 5, 6), 1: (1, 2, 3, 5, 6), 2: (), 3: ()}
        act_side = lambda k, g: g in ACT_NORMS[k]
        ACT_ALL = sum(len(v) for v in ACT_NORMS.values())
        act_before = lambda k, g: sum(len(ACT_NORMS[q]) for q in range(k)) + sum(x < g for x in ACT_NORMS.get(k, ()))

        def at(i, per_round, k, g):
            return (i * per_round + k) * G + g + 1

        def normed(q, i, k, g):
            if act_side(k, g):
                return q.s_na, (i * ACT_ALL + act_before(k, g) + 1) * J
            return q.s_nr, (i * (4 * G - ACT_ALL) + k * G + g - act_before(k, g) + 1) * J

        def free(eng, q, i, k, g):
            if k == 0:
                wait(eng, q.s_lm, at(i, 3, 2, g) - 3 * G)
            elif k == 1:
                wait(eng, q.s_bk, at(i, 1, 0, g))
            else:
                wait(eng, q.s_lm, at(i, 3, k - 2, g))

        TICKS = (("stats0",), ("norm0",), ("round0",), ("round1",), ("round2",), ("back", "stats1"),
                 ("norm1",), ("layer1", "stats2"), ("norm2",), ("layer2", "stats3"), ("norm3",), ("layer3",))
        HALF = len(TICKS) // 2

        def schedule(eng, body, lags, between=None, before_last=None):
            base = eng.alloc_register("base")

            def tick(parts, place=None):
                todo = [(q, i, step[:-1], int(step[-1]) if step[-1].isdigit() else 0)
                        for q, i, steps in parts for step in (s if s[-1].isdigit() else s + "0" for s in steps)]
                todo = [(q, i, name, k, lags.get(name, 0) if not (name == "stats" and k == 0) else 0) for q, i, name, k in todo]
                for n in range(G + max(lag for *_, lag in todo)):
                    for q, i, name, k, lag in todo:
                        if 0 <= n - lag < G:
                            body(q, i, name, k, n - lag)
                    if between and place is not None and n < G:
                        between(parts[0][1], place * G + n)

            def full(i, in_loop):
                def at_round():
                    if not in_loop:
                        return i
                    eng.reg_mov(base, i)
                    return Affine(eng.snap(base), 1, 0)

                a, b = groups
                for s in range(HALF):
                    i_ = at_round()
                    tick([(a, i_, TICKS[s])] + ([(b, i_ - 1, TICKS[s + HALF])] if in_loop else []), s)
                for s in range(HALF):
                    i_ = at_round()
                    if before_last and s == HALF - 1:
                        before_last(i_)
                    tick([(a, i_, TICKS[s + HALF]), (b, i_, TICKS[s])], HALF + s)

            full(0, False)
            with eng.Fori(1, rounds_n) as i:
                full(i, True)
            for s in range(HALF, len(TICKS)):
                tick([(groups[1], rounds_n - 1, TICKS[s])])

        block = ctx.enter_context(nc.Block())
        last_group = groups[1]
        assert (rounds_n * 2 * G - 2) * P <= last_row < (rounds_n * 2 * G - 1) * P

        def rows_of(q, i, g, last=False):
            return last_row if last else ((i * 2 + q.h) * G + g) * P

        @block.sync
        def _(eng):
            def load(q, i, g, last=False):
                if not (isinstance(i, int) and i == 0):
                    wait(eng, q.stored[g], i * 16)
                eng.dma_start(q.X[:, g, :], x_v[bass.ds(rows_of(q, i, g, last), P), :]).then_inc(q.loaded[g], 16)

            def store(q, i, g, last=False):
                wait(eng, q.s_x, at(i, 4, 3, g))
                eng.dma_start(out_v[bass.ds(rows_of(q, i, g, last), P), :], q.X[:, g, :]).then_inc(q.stored[g], 16)

            a, b = groups
            for q in groups:
                for g in range(G):
                    load(q, 0, g)
            def ends(i):
                eng.wait_ge(s_ends, i * (2 * PER * 16))
                for side, name in enumerate(("xs", "xd")):
                    table = t[name][bass.ds((i - 1) * (PER * P), PER * P), :].rearrange("(c p) n -> p c n", p=P)
                    eng.dma_start(table, GX[:, side, :, :]).then_inc(s_ends_out, 16)

            def turn(i, to_last=False):
                for q in groups:
                    for g in range(G):
                        store(q, i, g)
                        load(q, i + 1, g, to_last and q is b and g == G - 1)

            turn(0)
            with eng.Fori(1, rounds_n - 2) as i:
                ends(i)
                turn(i)
            ends(rounds_n - 2)
            turn(rounds_n - 2, True)
            ends(rounds_n - 1)
            i = rounds_n - 1
            for q in groups:
                for g in range(G):
                    if q is b and g == G - 1:
                        eng.wait_ge(b.stored[g - 1], rounds_n * 16)
                    store(q, i, g, q is b and g == G - 1)
            eng.wait_ge(s_ends_out, (rounds_n - 1) * 32)
            for q in groups:
                for g in range(G):
                    wait(eng, q.stored[g], rounds_n * 16)

        @block.vector
        def _(eng):
            def aggregate(q, i, k, g):
                wait(eng, q.s_st, at(i, 4, k, g) * J)
                carry_waits(eng, w)
                for j in range(J):
                    nc.vector.bn_aggr(q.MV[:, g, j, :], q.ST[:, g, j, :]).then_inc(q.s_mv, 1)

            def body(q, i, step, k, g):
                if step == "stats":
                    if k == 0:
                        wait(eng, q.loaded[g], (i + 1) * 16)
                    else:
                        wait(eng, q.s_x, at(i, 4, k - 1, g))
                    for j in range(J):
                        nc.vector.bn_stats(q.ST[:, g, j, :], q.X[:, g, j * C:(j + 1) * C]).then_inc(q.s_st, 1)
                    if g:
                        aggregate(q, i, k, g - 1)
                    if g == G - 1:
                        aggregate(q, i, k, g)
                elif step == "norm":
                    for n, (lo, hi) in enumerate(BATCHES):
                        if g == lo:
                            wait(eng, q.s_rs, (i * 4 + k) * 2 + n + 1)
                            carry_waits(eng, w)
                            nc.vector.scalar_tensor_tensor(q.NM[:, lo:hi, :], q.MV[:, lo:hi, :, 0], -1.0, q.RS[:, lo:hi, :],
                                                           ALU.mult, ALU.mult).then_inc(q.s_nm, 1)
                    if not act_side(k, g):
                        free(eng, q, i, k, g)
                        for j in range(J):
                            nc.vector.tensor_scalar(q.HT[:, g, j * C:(j + 1) * C], q.X[:, g, j * C:(j + 1) * C],
                                                    q.MV[:, g, j, 0:1], q.RS[:, g, j:j + 1],
                                                    ALU.subtract, ALU.mult).then_inc(q.s_nr, 1)
                elif step == "round":
                    wait(eng, q.s_sg, at(i, 3, k, g))
                    nc.vector.tensor_tensor(q.HT[:, g, :], q.HT[:, g, :], q.SG[:, (k * G + g) % SIGMOIDS, :], ALU.add).then_inc(q.s_h, 1)
                elif step == "back":
                    wait(eng, q.s_bk, at(i, 1, 0, g))
                    nc.vector.tensor_tensor(q.X[:, g, :], q.PS[g % BANKS][:, :], q.X[:, g, :], ALU.add).then_inc(q.s_x, 1)
                elif k == 1:
                    wait(eng, q.s_lm, at(i, 3, 0, g))
                    wait(eng, *normed(q, i, 1, g))
                    nc.vector.scalar_tensor_tensor(q.X[:, g, :], q.PS[g % BANKS][:, :], 0.0, q.X[:, g, :],
                                                   ALU.max, ALU.add).then_inc(q.s_x, 1)
                else:
                    wait(eng, q.s_lm, at(i, 3, k - 1, g))
                    wait(eng, q.s_xb, at(i, 2, k - 2, g))
                    nc.vector.tensor_tensor(q.X[:, g, :], q.PS[g % BANKS][:, :], q.X[:, g, :], ALU.add).then_inc(q.s_x, 1)

            def gathers_turn(i):
                if isinstance(i, int):
                    column = 0
                else:
                    column = i.register * PER
                    wait(eng, s_ends_out, i * 32)
                    carry_waits(eng, w)
                for n, name in enumerate(("src_ix", "dst_ix")):
                    nc.vector.tensor_scalar(GI[:, n, :], f[name][:, bass.ds(column, PER)], 0.0, None, ALU.add).then_inc(s_index, 1)

            schedule(eng, body, {"round": 2, "back": 1, "layer": 1, "stats": 2}, before_last=gathers_turn)

        @block.gpsimd
        def _(eng):
            def body(q, i, step, k, g):
                if step == "stats":
                    for n, (lo, hi) in enumerate(BATCHES):
                        if g != hi - 1:
                            continue
                        wait(eng, q.s_mv, at(i, 4, k, g) * J)
                        wait(eng, q.s_nr, (i * (4 * G - ACT_ALL) + k * G - act_before(k, 0)) * J)
                        wait(eng, q.s_na, (i * ACT_ALL + act_before(k, 0)) * J)
                        nc.gpsimd.tensor_tensor(q.VE[:, lo:hi, :], q.MV[:, lo:hi, :, 1],
                                                w["ln_eps"][:, None, 0:J].to_broadcast([P, hi - lo, J]), ALU.add).then_inc(q.s_ve, 1)
                        wait(eng, q.s_ve, (i * 4 + k) * 2 + n + 1)
                        nc.gpsimd.tensor_tensor(q.RS[:, lo:hi, :], q.VE[:, lo:hi, :],
                                                w["neg_half"][:, None, 0:J].to_broadcast([P, hi - lo, J]), ALU.pow).then_inc(q.s_rs, 1)
                elif step == "norm" and k >= 2:
                    wait(eng, *normed(q, i, k, g))
                    nc.gpsimd.tensor_tensor(q.X[:, g, :].rearrange("p (j c) -> p j c", j=J),
                                            q.X[:, g, :].rearrange("p (j c) -> p j c", j=J),
                                            w["bias_rows"][k - 2][:, None, :].to_broadcast([P, J, C]), ALU.add).then_inc(q.s_xb, 1)

            def between(i, place):
                if isinstance(i, int):
                    for c in range(place * T // (2 * HALF * G), (place + 1) * T // (2 * HALF * G)):
                        wait(eng, s_owner[c % J], 16 * (c // J))
                        eng.indirect_dma_start(out=t["maps"], out_offset=bass.IndirectOffsetOnAxis(ap=f["own_at"][:, c:c + 1], axis=0),
                                               in_=f["number"][:, c:c + 1], in_offset=None, bounds_check=NODES * WORDS - 1,
                                               oob_is_err=False).then_inc(s_owner[c % J], 16)
                    return
                if place == 0:
                    wait(eng, s_index, i * 2)
                    carry_waits(eng, w)
                c, side = place // 2, place % 2
                if c < PER:
                    eng.indirect_dma_start(out=GX[:, side, c, :], out_offset=None, in_=x,
                                           in_offset=bass.IndirectOffsetOnAxis(ap=GI[:, side, c:c + 1], axis=0),
                                           bounds_check=N - 1, oob_is_err=False).then_inc(s_ends, 16)

            schedule(eng, body, {"norm": 1, "stats": 3}, between=between)
            for j in range(J):
                eng.wait_ge(s_owner[j], 16 * (T // J))

        @block.scalar
        def _(eng):
            def body(q, i, step, k, g):
                if step == "norm":
                    def norm(g):
                        wait(eng, q.s_nm, (i * 4 + k) * 2 + batch_of(g) + 1)
                        free(eng, q, i, k, g)
                        carry_waits(eng, w)
                        for j in range(J):
                            nc.scalar.activation(q.HT[:, g, j * C:(j + 1) * C], q.X[:, g, j * C:(j + 1) * C], ACT.Identity,
                                                 bias=q.NM[:, g, j:j + 1], scale=q.RS[:, g, j:j + 1]).then_inc(q.s_na, 1)

                    if g == 0 and act_side(k, 0):
                        norm(0)
                    if act_side(k, g + 1):
                        norm(g + 1)
                    wait(eng, q.s_tp, at(i, 4, k, g))
                    nc.scalar.activation(q.HT[:, g, :], q.PS[g % BANKS][:, :], ACT.Relu).then_inc(q.s_ht, 1)
                elif step == "round":
                    wait(eng, q.s_mm, at(i, 3, k, g))
                    wait(eng, q.s_h, at(i, 3, k, g) - SIGMOIDS)
                    nc.scalar.activation(q.SG[:, (k * G + g) % SIGMOIDS, :], q.PS[g % BANKS][:, :], ACT.Sigmoid,
                                         bias=w["b0_cols"][:, k:k + 1]).then_inc(q.s_sg, 1)

            schedule(eng, body, {})

        @block.tensor
        def _(eng):
            USES = [("norm", 0), ("round", 0), ("round", 1), ("round", 2), ("back", 0), ("norm", 1),
                    ("layer", 1), ("norm", 2), ("layer", 2), ("norm", 3), ("layer", 3)]

            def read(q, i, step, k, g):
                if step == "norm":
                    return q.s_ht, at(i, 4, k, g)
                if step == "round":
                    return q.s_sg, at(i, 3, k, g)
                return q.s_x, at(i, 4, k, g)

            def bank_free(q, i, step, k, g):
                if g >= BANKS:
                    wait(eng, *read(q, i, step, k, g - BANKS))
                    return
                before = max(x for x in range(G) if x % BANKS == g)
                n = USES.index((step, k))
                if n:
                    wait(eng, *read(q, i, *USES[n - 1], before))
                else:
                    wait(eng, q.s_x, at(i, 4, 3, before) - 4 * G)

            def body(q, i, step, k, g):
                if step == "norm":
                    wait(eng, *normed(q, i, k, g))
                    bank_free(q, i, step, k, g)
                    for j in range(J):
                        last = nc.tensor.transpose(q.PS[g % BANKS][:, j * C:(j + 1) * C], q.HT[:, g, j * C:(j + 1) * C],
                                                   w["ident"][:, :])
                    last.then_inc(q.s_tp, 1)
                elif step == "round":
                    if k == 0:
                        wait(eng, q.s_ht, at(i, 4, 0, g))
                    else:
                        wait(eng, q.s_h, at(i, 3, k - 1, g))
                    bank_free(q, i, step, k, g)
                    nc.tensor.matmul(q.PS[g % BANKS][:, :], w["aug0"][:, k, 0:C], q.HT[:, g, :],
                                     start=True, stop=True).then_inc(q.s_mm, 1)
                elif step == "back":
                    wait(eng, q.s_h, at(i, 3, 2, g))
                    bank_free(q, i, step, k, g)
                    for j in range(J):
                        last = nc.tensor.transpose(q.PS[g % BANKS][:, j * C:(j + 1) * C], q.HT[:, g, j * C:(j + 1) * C],
                                                   w["ident"][:, :])
                    last.then_inc(q.s_bk, 1)
                elif step == "layer":
                    rhs = {1: w["loop"][:, :], 2: w["aug2"][:, 0:C], 3: w["fused3"][:, :]}[k]
                    wait(eng, q.s_ht, at(i, 4, k, g))
                    bank_free(q, i, step, k, g)
                    for j in range(J):
                        last = nc.tensor.matmul(q.PS[g % BANKS][:, j * C:(j + 1) * C], q.HT[:, g, j * C:(j + 1) * C],
                                                rhs, start=True, stop=True)
                    last.then_inc(q.s_lm, 1)

            schedule(eng, body, {})


def setup(nc, w, ins):
    with phase(nc) as ctx:
        sb = lambda n, s: ctx.enter_context(nc.sbuf_tensor(n, s, F32))
        sem = lambda n: ctx.semaphore(n)
        W0T = sb("s_w0t", [P, 3, C])
        W2T = sb("s_w2t", [P, C])
        A0 = sb("s_a0", [P, 3, 2])
        AC = sb("s_ac", [P, 2])
        A2 = sb("s_a2", [P, 2, HEADS])
        WN = sb("s_wn", [P, C])
        BNC = sb("s_bnc", [P, 1])
        BNB = sb("s_bnb", [P, C])
        PS = ctx.enter_context(nc.psum_tensor("s_ps", [P, 512], F32))
        PB = ctx.enter_context(nc.psum_tensor("s_pb", [P, 512], F32))

        s_in = sem("s_in")
        s_pool = sem("s_pool")
        s_a2 = sem("s_a2col")
        s_heads = sem("s_heads")
        s_pe = sem("s_pe")
        s_dve = sem("s_dve")

        block = ctx.enter_context(nc.Block())
        loads = [
            (w["aug0"][:, :, 0:C], ins["L0_Ws"].rearrange("r i o -> i r o")),
            (W0T[:, :, :], ins["L0_WsT"].rearrange("r o i -> o r i")),
            (A0[:, :, 0], ins["L0_as"]), (A0[:, :, 1], ins["L0_ad"]),
            (w["b0_cols"][:, :], ins["L0_bT"]),
            (w["loop"][:, :], ins["L1_loop"]),
            (w["basis"][:, :, :], ins["L1_basis"].rearrange("b i o -> i b o")),
            (w["aug2"][:, 0:C], ins["L2_W"]), (W2T[:, :], ins["L2_WT"]),
            (AC[:, 0:1], ins["L2_as"]), (AC[:, 1:2], ins["L2_ad"]),
            (WN[:, :], ins["L3_Wn"]), (w["wnT"][:, :], ins["L3_WnT"]),
            (BNC[:, :], ins["L3_bn"]), (w["bn_col"][:, :], ins["L3_bn"]),
            (w["weT"][:, :, :], ins["L3_WeT"].rearrange("(h c) o -> c h o", h=2)),
            (w["wlT"][:, :, :], ins["L3_WlT"].rearrange("(h c) o -> c h o", h=2)),
            (w["bias_rows"][0][:, :], ins["L2_b"].to_broadcast([P, C])),
            (w["bl_row"][:, :], ins["L3_bl"].to_broadcast([P, C])),
            (w["be_row"][:, :], ins["L3_be"].to_broadcast([P, C])),
        ]
        for r in range(3):
            loads.append((w["b0_rows"][:, r, :], ins["L0_b"][r:r + 1, :].to_broadcast([P, C])))

        @block.sync
        def _(eng):
            for dst, src in loads:
                with nc.allow_non_contiguous_dma(reason="small weights"):
                    eng.dma_start(dst, src).then_inc(s_in, 16)

        @block.gpsimd
        def _(eng):
            nc.gpsimd.memset(w["ident"][:, :], 0.0).then_inc(s_pool, 1)
            nc.gpsimd.memset(w["ones"][:, :], 1.0).then_inc(s_pool, 1)
            nc.gpsimd.memset(w["ln_eps"][:, :], LN_EPS).then_inc(s_pool, 1)
            nc.gpsimd.memset(w["neg_half"][:, :], -0.5).then_inc(s_pool, 1)
            eng.wait_ge(s_pool, 4)
            nc.gpsimd.affine_select(out=w["ident"][:, :], in_=w["ident"][:, :], compare_op=ALU.not_equal, fill=1.0,
                                    base=0, pattern=[[-1, P]], channel_multiplier=1).then_inc(s_pool, 1)
            eng.wait_ge(s_a2, 3)
            nc.gpsimd.affine_select(out=A2[:, :, :], in_=A2[:, :, :], compare_op=ALU.is_ge, fill=0.0,
                                    base=0, pattern=[[0, 2], [-(C // HEADS), HEADS]], channel_multiplier=1).then_inc(s_heads, 1)
            eng.wait_ge(s_heads, 1)
            nc.gpsimd.affine_select(out=A2[:, :, :], in_=A2[:, :, :], compare_op=ALU.is_ge, fill=0.0,
                                    base=C // HEADS - 1, pattern=[[0, 2], [C // HEADS, HEADS]], channel_multiplier=-1).then_inc(s_heads, 1)

        @block.vector
        def _(eng):
            eng.wait_ge(s_in, 16 * len(loads))
            eng.wait_ge(s_pool, 5)
            nc.vector.tensor_scalar(A2[:, 0, :], w["ones"][:, 0:HEADS], AC[:, 0:1], None, ALU.mult).then_inc(s_a2, 1)
            nc.vector.tensor_scalar(A2[:, 1, :], w["ones"][:, 0:HEADS], AC[:, 1:2], None, ALU.mult).then_inc(s_a2, 1)
            nc.vector.tensor_scalar(BNB[:, :], w["ones"][:, :], BNC[:, 0:1], None, ALU.mult).then_inc(s_a2, 1)
            eng.wait_ge(s_pe, 1)
            nc.vector.tensor_copy(w["aug0"][:, :, C:C + 2], PS[:, 0:6].rearrange("p (r a) -> p r a", r=3)).then_inc(s_dve, 1)
            nc.vector.tensor_copy(w["aug2"][:, C:C + 2 * HEADS], PS[:, 16:16 + 2 * HEADS]).then_inc(s_dve, 1)
            nc.vector.tensor_tensor(w["fused3"][:, :], PB[:, 0:C], w["wlT"][:, 0, :], ALU.add).then_inc(s_dve, 1)
            nc.vector.tensor_tensor(w["bias_rows"][1][:, :], PB[:, C:2 * C], w["bl_row"][:, :], ALU.add).then_inc(s_dve, 1)

        @block.tensor
        def _(eng):
            eng.wait_ge(s_in, 16 * len(loads))
            eng.wait_ge(s_heads, 2)
            for r in range(3):
                nc.tensor.matmul(PS[:, 2 * r:2 * r + 2], W0T[:, r, :], A0[:, r, :], start=True, stop=True)
            nc.tensor.matmul(PS[:, 16:16 + 2 * HEADS], W2T[:, :], A2[:, :, :].rearrange("p a h -> p (a h)"), start=True, stop=True)
            nc.tensor.matmul(PB[:, 0:C], WN[:, :], w["wlT"][:, 1, :], start=True, stop=True)
            nc.tensor.matmul(PB[:, C:2 * C], BNB[:, :], w["wlT"][:, 1, :], start=True, stop=True).then_inc(s_pe, 1)


def alloc_weights(nc, ctx):
    sb = lambda n, s: ctx.enter_context(nc.sbuf_tensor("w_" + n, s, F32))
    w = {
        "carrier": ctx.enter_context(nc.semaphore("carrier")),
        "ident": sb("ident", [P, P]), "ones": sb("ones", [P, P]), "neg_half": sb("neg_half", [P, 8]), "ln_eps": sb("ln_eps", [P, 8]),
        "aug0": sb("aug0", [P, 3, C + 2]), "b0_cols": sb("b0_cols", [P, 3]), "b0_rows": sb("b0_rows", [P, 3, C]),
        "loop": sb("loop", [P, C]), "basis": sb("basis", [P, BASES, C]),
        "aug2": sb("aug2", [P, C + 2 * HEADS]),
        "wnT": sb("wnT", [P, C]), "bn_col": sb("bn_col", [P, 1]),
        "weT": sb("weT", [P, 2, C]), "wlT": sb("wlT", [P, 2, C]), "fused3": sb("fused3", [P, C]),
        "bl_row": sb("bl_row", [P, C]), "be_row": sb("be_row", [P, C]),
        "bias_rows": [sb("b2_row", [P, C]), sb("b3_row", [P, C])],
    }
    return w


def block_rows(table, b):
    return table[bass.ds(number(b) * (J * P), J * P), :].rearrange("(j p) c -> p j c", p=P)


def tiles_of(x, b):
    return x[:, bass.ds(number(b) * J, J)]


SRC, DST = 0, 1


class Norms:

    def __init__(self, nc, ctx, name, w):
        sb = lambda x, s: ctx.enter_context(nc.sbuf_tensor(name + x, s, F32))
        sem = lambda x: ctx.semaphore(name + x)
        self.nc, self.w = nc, w
        self.stats, self.moments = sb("_st", [P, GE, 2 * J, 6]), sb("_mv", [P, GE, 2 * J, 2])
        self.var_eps, self.rstd, self.shift = (sb(n, [P, GE, 2 * J]) for n in ("_ve", "_rs", "_sh"))
        self.s_stats, self.s_moments = sem("_stats"), sem("_moments")
        self.s_var_eps, self.s_rstd, self.s_shift = sem("_var_eps"), sem("_rstd"), sem("_shift")
        self.s_normed = [sem("_normed_src"), sem("_normed_dst")]

    def take(self, eng, rows, b, g):
        for n in range(2 * J):
            self.nc.vector.bn_stats(self.stats[:, g, n, :], rows[:, n // J, n % J, :]).then_inc(self.s_stats, 1)
        wait(eng, self.s_stats, (b + 1) * (2 * J))
        carry_waits(eng, self.w)
        for n in range(2 * J):
            self.nc.vector.bn_aggr(self.moments[:, g, n, :], self.stats[:, g, n, :]).then_inc(self.s_moments, 1)

    def invert(self, eng, b, g):
        wait(eng, self.s_moments, (b + 1) * (2 * J))
        self.nc.gpsimd.tensor_tensor(self.var_eps[:, g, :], self.moments[:, g, :, 1], self.w["ln_eps"][:, :], ALU.add).then_inc(self.s_var_eps, 1)
        wait(eng, self.s_var_eps, b + 1)
        self.nc.gpsimd.tensor_tensor(self.rstd[:, g, :], self.var_eps[:, g, :], self.w["neg_half"][:, :], ALU.pow).then_inc(self.s_rstd, 1)

    def shifts(self, eng, b, g):
        wait(eng, self.s_rstd, b + 1)
        carry_waits(eng, self.w)
        self.nc.vector.scalar_tensor_tensor(self.shift[:, g, :], self.moments[:, g, :, 0], -1.0, self.rstd[:, g, :],
                                            ALU.mult, ALU.mult).then_inc(self.s_shift, 1)

    def apply(self, eng, out, rows, side, b, g):
        wait(eng, self.s_rstd, b + 1)
        for j in range(J):
            n = side * J + j
            self.nc.vector.tensor_scalar(out[:, j, :], rows[:, j, :], self.moments[:, g, n, 0:1], self.rstd[:, g, n:n + 1],
                                         ALU.subtract, ALU.mult).then_inc(self.s_normed[side], 1)

    def apply_scalar(self, eng, out, rows, side, b, g):
        wait(eng, self.s_shift, b + 1)
        carry_waits(eng, self.w)
        for j in range(J):
            n = side * J + j
            self.nc.scalar.activation(out[:, j, :], rows[:, j, :], ACT.Identity, bias=self.shift[:, g, n:n + 1],
                                      scale=self.rstd[:, g, n:n + 1]).then_inc(self.s_normed[side], 1)


class Ends:

    def __init__(self, nc, ctx, name, w, k, t, src_table, dst_table, overlay):
        sem = lambda x: ctx.semaphore(name + x)
        self.nc, self.w, self.k, self.t, self.overlay = nc, w, k, t, overlay
        self.src_table, self.dst_table = src_table, dst_table
        self.A = ctx.enter_context(nc.sbuf_tensor(name + "_state", [P, GE, 2, J, C], F32))
        self.IX = ctx.enter_context(nc.sbuf_tensor(name + "_ix", [P, GE, J], I32))
        self.s_index = sem("_index")
        self.s_load = [sem(f"_load{g}") for g in range(GE)]
        self.s_over = [sem(f"_over{g}") for g in range(GE)]

    def load(self, eng, b, g):
        eng.dma_start(self.A[:, g, SRC, :, :], block_rows(self.t[self.src_table], b)).then_inc(self.s_load[g], 16)
        eng.dma_start(self.A[:, g, DST, :, :], block_rows(self.t[self.dst_table], b)).then_inc(self.s_load[g], 16)

    def index(self, eng, b, g):
        wait(eng, self.s_over[g], (b // GE) * (16 * J))
        carry_waits(eng, self.w)
        self.nc.vector.tensor_scalar(self.IX[:, g, :], tiles_of(self.k["map_ix"], b), 0.0, None, ALU.add).then_inc(self.s_index, 1)

    def gather(self, eng, b, g):
        wait(eng, self.s_index, b + 1)
        wait(eng, self.s_load[g], (b // GE + 1) * 32)
        carry_waits(eng, self.w)
        for j in range(J):
            eng.indirect_dma_start(out=self.A[:, g, SRC, j, :], out_offset=None, in_=self.t[self.dst_table],
                                   in_offset=bass.IndirectOffsetOnAxis(ap=self.IX[:, g, j:j + 1], axis=0),
                                   bounds_check=EP - 1, oob_is_err=False).then_inc(self.s_over[g], 16)

    def there(self, eng, b, g, sides=(SRC, DST)):
        if self.overlay and SRC in sides:
            wait(eng, self.s_over[g], (b // GE + 1) * (16 * J))
        wait(eng, self.s_load[g], (b // GE + 1) * 32)


def project(nc, w, k, t, r, heads, rhs, bias_row, kind, plus_x, keep, f=None):
    CW = C + 2 * heads
    sigmoid = kind != "normed"
    norm = kind != "plain"
    with phase(nc) as ctx:
        pre = f"p{r}_"
        sb = lambda n, s, d=F32: ctx.enter_context(nc.sbuf_tensor(pre + n, s, d))
        sem = lambda n: ctx.semaphore(pre + n)
        tables = ("xs", "xd") if kind == "first" else (f"s{r}", f"d{r}")
        ends = Ends(nc, ctx, pre + "ends", w, k, t, *tables, kind != "first")
        A = ends.A
        HT = sb("ht", [P, GE, 2, J * C])
        NR = HT[:, :, :, :].rearrange("p g s (j c) -> p g s j c", j=J) if kind == "normed" else A
        UP = sb("up", [P, GE, J, C])
        XS = sb("xs", [P, GE, J, C]) if plus_x else None
        nb = Norms(nc, ctx, pre + "nb", w) if norm else None
        PT = [ctx.enter_context(nc.psum_tensor(f"{pre}pt{n}", [P, J, C], F32)) for n in range(4)]
        PM = [ctx.enter_context(nc.psum_tensor(f"{pre}pm{n}", [P, J, 256], F32)) for n in range(2)]
        s_relu, s_tp, s_ht, s_mm, s_biased, s_sig, s_next, s_plus = (
            sem(n) for n in "relu tp ht mm biased sig next plus".split())
        s_keep = [sem("keep_src"), sem("keep_dst")]
        s_xs = [sem(f"xs{g}") for g in range(GE)]
        s_out = [sem(f"out{g}") for g in range(GE)]
        OUTS = 32 if kind == "first" else 16
        if kind == "first":
            ROWS = ctx.enter_context(nc.sbuf_tensor(pre + "map_rows", [P, GE, J, WORDS], I32))
            s_map = [sem(f"map{g}") for g in range(GE)]
            s_found = sem("found")
        block = ctx.enter_context(nc.Block())

        @block.sync
        def _(eng):
            def load(b, g):
                wait(eng, s_out[g], (b // GE) * OUTS)
                carry_waits(eng, w)
                if kind == "normed":
                    wait(eng, nb.s_normed[DST], (b - GE + 1) * J)
                elif kind == "plain":
                    wait(eng, s_tp, (b - GE + 1) * 2)
                carry_waits(eng, w)
                ends.load(eng, b, g)
                if plus_x:
                    eng.dma_start(XS[:, g, :, :], block_rows(t["xs"], b)).then_inc(s_xs[g], 16)

            def store(b, g):
                if kind == "first":
                    wait(eng, s_relu, (b + 1) * 2)
                    carry_waits(eng, w)
                    eng.dma_start(block_rows(t["d0"], b), A[:, g, DST, :, :]).then_inc(s_out[g], 16)
                wait(eng, s_next, b + 1)
                carry_waits(eng, w)
                eng.dma_start(block_rows(t[f"s{r + 1}"], b), A[:, g, SRC, :, :]).then_inc(s_out[g], 16)

            stream(eng, (load, 0), (store, 4))
            for g in range(GE):
                eng.wait_ge(s_out[g], OUTS * ROUNDS_E)

        @block.gpsimd
        def _(eng):
            def map_rows(b, g):
                wait(eng, ends.s_index, b + 1)
                wait(eng, s_found, b - GE + 1)
                carry_waits(eng, w)
                for j in range(J):
                    eng.indirect_dma_start(out=ROWS[:, g, j, :], out_offset=None, in_=t["maps"].rearrange("(n a) o -> n (a o)", a=WORDS),
                                           in_offset=bass.IndirectOffsetOnAxis(ap=ends.IX[:, g, j:j + 1], axis=0),
                                           bounds_check=NODES - 1, oob_is_err=False).then_inc(s_map[g], 16)

            steps = [(map_rows, 2)] if kind == "first" else []
            if ends.overlay:
                steps.append((lambda b, g: ends.gather(eng, b, g), 0))
            if norm:
                steps.append((lambda b, g: nb.invert(eng, b, g), 1))
            stream(eng, *steps)

        @block.vector
        def _(eng):
            v = nc.vector

            def map_index(b, g):
                wait(eng, s_map[g], (b // GE) * (16 * J))
                carry_waits(eng, w)
                v.tensor_scalar(ends.IX[:, g, :], tiles_of(f["map_at"], b), 0.0, None, ALU.add).then_inc(ends.s_index, 1)

            def found(b, g):
                wait(eng, s_map[g], (b // GE + 1) * (16 * J))
                carry_waits(eng, w)
                v.tensor_scalar(tiles_of(f["found"], b), ROWS[:, g, :, :], 0.0, None, ALU.add).then_inc(s_found, 1)

            def stats(b, g):
                ends.there(eng, b, g)
                nb.take(eng, A[:, g, :, :, :], b, g)

            def apply(b, g):
                nb.shifts(eng, b, g)
                wait(eng, s_mm, (b - GE) * 2 + 1)
                nb.apply(eng, NR[:, g, SRC, :, :], A[:, g, SRC, :, :], SRC, b, g)

            def product(b, g):
                wait(eng, s_mm, b * 2 + 1)
                wait(eng, s_next, b - GE + 1)
                v.tensor_tensor(UP[:, g, :, :], PM[SRC][:, :, 0:C], bias_row[:, None, :].to_broadcast([P, J, C]), ALU.add).then_inc(s_biased, 1)
                v.tensor_scalar(tiles_of(keep["src"], b)[:, :, 0:CW], PM[SRC][:, :, 0:CW], 0.0, None, ALU.add).then_inc(s_keep[SRC], 1)

            def residual(b, g):
                wait(eng, s_sig if sigmoid else s_biased, b + 1)
                if plus_x:
                    wait(eng, s_xs[g], (b // GE + 1) * 16)
                    v.tensor_tensor(UP[:, g, :, :], UP[:, g, :, :], XS[:, g, :, :], ALU.add).then_inc(s_plus, 1)
                    wait(eng, s_plus, b + 1)
                ends.there(eng, b, g, (SRC,))
                wait(eng, s_tp, b * 2 + 1)
                if kind == "normed":
                    wait(eng, nb.s_normed[SRC], (b + 1) * J)
                v.tensor_tensor(A[:, g, SRC, :, :], A[:, g, SRC, :, :], UP[:, g, :, :], ALU.add).then_inc(s_next, 1)

            steps = []
            if ends.overlay:
                steps.append((lambda b, g: ends.index(eng, b, g), 0))
            if kind == "first":
                steps += [(map_index, 0), (found, 5)]
            if norm:
                lag = 2 if kind == "first" else 3
                steps += [(stats, lag), (product, 4), (apply, lag), (residual, 4)]
            else:
                steps += [(residual, 3), (product, 2)]
            stream(eng, *steps)

        @block.scalar
        def _(eng):
            def apply(b, g):
                wait(eng, s_mm, (b - GE + 1) * 2)
                nb.apply_scalar(eng, NR[:, g, DST, :, :], A[:, g, DST, :, :], DST, b, g)

            def relu(b, g):
                for side in (SRC, DST):
                    wait(eng, nb.s_normed[side], (b + 1) * J)
                    nc.scalar.activation(A[:, g, side, :, :], A[:, g, side, :, :], ACT.Relu).then_inc(s_relu, 1)

            def copy(b, g):
                for side in (SRC, DST):
                    wait(eng, s_tp, b * 2 + side + 1)
                    wait(eng, s_mm, (b - GE) * 2 + side + 1)
                    nc.scalar.activation(HT[:, g, side, :], PT[g % 2 * 2 + side][:, :, :].rearrange("p j c -> p (j c)"),
                                         ACT.Relu if kind == "normed" else ACT.Copy).then_inc(s_ht, 1)

            def keep_dst(b, g):
                wait(eng, s_mm, b * 2 + 2)
                carry_waits(eng, w)
                nc.scalar.activation(tiles_of(keep["dst"], b)[:, :, 0:CW], PM[DST][:, :, 0:CW], ACT.Copy).then_inc(s_keep[DST], 1)

            def squash(b, g):
                wait(eng, s_biased, b + 1)
                nc.scalar.activation(UP[:, g, :, :], UP[:, g, :, :], ACT.Sigmoid).then_inc(s_sig, 1)

            if kind == "first":
                stream(eng, (keep_dst, 2), (squash, 2), (apply, 0), (relu, 0), (copy, 0))
            elif kind == "plain":
                stream(eng, (copy, 0), (keep_dst, 0), (squash, 0))
            else:
                stream(eng, (keep_dst, 1), (apply, 0), (copy, 0))

        @block.tensor
        def _(eng):
            def turn(b, g):
                for side in (SRC, DST):
                    if kind == "first":
                        wait(eng, s_relu, b * 2 + side + 1)
                    elif kind == "normed":
                        wait(eng, nb.s_normed[side], (b + 1) * J)
                    else:
                        ends.there(eng, b, g, (side,))
                    before = 1 if g == 0 else 2
                    wait(eng, s_ht, (b - before) * 2 + side + 1)
                    for j in range(J):
                        last = nc.tensor.transpose(PT[g % 2 * 2 + side][:, j, :], NR[:, g, side, j, :], w["ident"][:, :])
                    last.then_inc(s_tp, 1)

            def product(b, g):
                for side in (SRC, DST):
                    wait(eng, s_ht, b * 2 + side + 1)
                    wait(eng, s_keep[side], b)
                    for j in range(J):
                        last = nc.tensor.matmul(PM[side][:, j, 0:CW], HT[:, g, side, j * C:(j + 1) * C], rhs, start=True, stop=True)
                    last.then_inc(s_mm, 1)

            stream(eng, (turn, 0), (product, 0))


def attend(nc, w, k, r, heads, keep, wm, ws):
    H = heads
    with phase(nc) as ctx:
        pre = f"t{r}_"
        sb = lambda n, s, d=F32: ctx.enter_context(nc.sbuf_tensor(pre + n, s, d))
        sem = lambda n: ctx.semaphore(pre + n)
        row = lambda n: sb(n, [T, H, P])
        SR, DS, DD, HD, T1, SC, ES, MX = (row(n) for n in "sr ds dd hd t1 sc es mx".split())
        EDGE = sb("edge", [T, H])
        RC, RS = sb("rc", [H, T]), sb("rs", [H, T])
        CI = sb("ci", [T, H])
        PA = ctx.enter_context(nc.psum_tensor(pre + "pa", [P, HEADS, P], F32))
        PB = ctx.enter_context(nc.psum_tensor(pre + "pb", [P, HEADS, P], F32))
        PC = ctx.enter_context(nc.psum_tensor(pre + "pc", [P, HEADS, P], F32))
        PX = ctx.enter_context(nc.psum_tensor(pre + "px", [P, 512], F32))
        s_v, s_rows, s_edge, s_edge_t, s_carry, s_carry_t, s_exp_in, s_exp, s_cols = (
            sem(n) for n in "v rows edge edge_t carry carry_t exp_in exp cols".split())
        block = ctx.enter_context(nc.Block())
        idp, idt, idh = w["ident"][:, :], w["ident"][0:T, 0:T], w["ident"][0:H, 0:H]
        flat = lambda x: x.rearrange("t h p -> t (h p)")
        wide = lambda x: x[:, None, :].to_broadcast([T, H, P])

        @block.tensor
        def _(eng):
            for h in range(H):
                nc.tensor.transpose(PA[0:T, h, :], keep["src"][:, :, C + h], idp)
                nc.tensor.transpose(PB[0:T, h, :], keep["dst"][:, :, C + h], idp)
                last = nc.tensor.transpose(PC[0:T, h, :], keep["dst"][:, :, C + H + h], idp)
            last.then_inc(s_rows, 1)
            for n in range(3):
                eng.wait_ge(s_edge, n + 1)
                nc.tensor.transpose(PX[0:H, 0:T], EDGE[:, :], idt).then_inc(s_edge_t, 1)
                eng.wait_ge(s_carry, n + 1)
                nc.tensor.transpose(PX[0:T, 256:256 + H], RS[:, :], idh).then_inc(s_carry_t, 1)
            eng.wait_ge(s_exp, 2)
            for h in range(H):
                nc.tensor.transpose(PA[:, h, 0:T], SC[:, h, :], idt)
                last = nc.tensor.transpose(PB[:, h, 0:T], ES[:, h, :], idt)
            last.then_inc(s_cols, 1)

        @block.scalar
        def _(eng):
            eng.wait_ge(s_exp_in, 1)
            nc.scalar.activation(flat(SC[:, :, :]), flat(SC[:, :, :]), ACT.Exp).then_inc(s_exp, 1)
            nc.scalar.activation(flat(ES[:, :, :]), flat(ES[:, :, :]), ACT.Exp).then_inc(s_exp, 1)

        @block.vector
        def _(eng):
            v = nc.vector
            n = [0]
            m = [0]

            def done(ins_):
                n[0] += 1
                ins_.then_inc(s_v, 1)
                eng.wait_ge(s_v, n[0])

            def over_rows(scan):
                m[0] += 1
                v.tensor_scalar(EDGE[:, :], EDGE[:, :], 0.0, None, ALU.add).then_inc(s_edge, 1)
                eng.wait_ge(s_edge_t, m[0])
                scan(PX[0:H, 0:T])
                eng.wait_ge(s_carry_t, m[0])
                done(v.tensor_copy(CI[:, :], PX[0:T, 256:256 + H]))

            def hold(out, values):
                done(v.tensor_tensor(T1[:, :, :], values, wide(k["is_last"]), ALU.mult))
                done(v.tensor_tensor_scan(flat(out)[:, ::-1], flat(k["nl0"][:, 0:H, :])[:, ::-1], flat(T1[:, :, :])[:, ::-1],
                                          0.0, ALU.mult, ALU.add))
                done(v.tensor_copy(EDGE[:, :], out[:, :, 0]))

                def scan(edge):
                    done(v.tensor_tensor_scan(RC[:, ::-1], k["row_nl"][0:H, ::-1], edge[:, ::-1], 0.0, ALU.mult, ALU.add))
                    done(v.memset(RS[:, T - 1:T], 0.0))
                    v.tensor_copy(RS[:, 0:T - 1], RC[:, 1:T]).then_inc(s_carry, 1)

                over_rows(scan)
                done(v.tensor_tensor(T1[:, :, :], wide(k["post"]), CI[:, :, None].to_broadcast([T, H, P]), ALU.mult))
                done(v.tensor_tensor(out, out, T1[:, :, :], ALU.add))

            eng.wait_ge(s_rows, 1)
            done(v.tensor_copy(SR[:, :, :], PA[0:T, 0:H, :]))
            done(v.tensor_copy(DS[:, :, :], PB[0:T, 0:H, :]))
            done(v.tensor_copy(DD[:, :, :], PC[0:T, 0:H, :]))
            hold(HD[:, :, :], DD[:, :, :])
            for out, a in ((SC, SR), (ES, DS)):
                done(v.tensor_tensor(T1[:, :, :], a[:, :, :], HD[:, :, :], ALU.add))
                done(v.scalar_tensor_tensor(out[:, :, :], T1[:, :, :], SLOPE, T1[:, :, :], ALU.mult, ALU.max))
            done(v.tensor_tensor(T1[:, :, :], ES[:, :, :], wide(k["last_pen"]), ALU.add))
            done(v.tensor_tensor(T1[:, :, :], T1[:, :, :], SC[:, :, :], ALU.max))
            done(v.tensor_tensor_scan(flat(MX[:, :, :]), flat(k["pen0"][:, 0:H, :]), flat(T1[:, :, :]), 0.0, ALU.add, ALU.max))
            done(v.tensor_copy(EDGE[:, :], MX[:, :, P - 1]))

            def scan_max(edge):
                done(v.tensor_tensor_scan(RC[:, :], k["row_pen"][0:H, :], edge, -BIG, ALU.add, ALU.max))
                done(v.memset(RS[:, 0:1], -BIG))
                v.tensor_copy(RS[:, 1:T], RC[:, 0:T - 1]).then_inc(s_carry, 1)

            over_rows(scan_max)
            done(v.tensor_tensor(T1[:, :, :], wide(k["pre_pen"]), CI[:, :, None].to_broadcast([T, H, P]), ALU.add))
            done(v.tensor_tensor(MX[:, :, :], MX[:, :, :], T1[:, :, :], ALU.max))
            hold(SR[:, :, :], MX[:, :, :])
            done(v.tensor_tensor(SC[:, :, :], SC[:, :, :], SR[:, :, :], ALU.subtract))
            done(v.tensor_tensor(ES[:, :, :], ES[:, :, :], SR[:, :, :], ALU.subtract))
            v.tensor_scalar(ES[:, :, :], ES[:, :, :], 0.0, None, ALU.min).then_inc(s_exp_in, 1)
            eng.wait_ge(s_cols, 1)
            done(v.tensor_copy(wm[:, :, 0:H], PA[:, 0:H, 0:T].rearrange("p h t -> p t h")))
            done(v.tensor_copy(ws[:, :, 0:H], PB[:, 0:H, 0:T].rearrange("p h t -> p t h")))


def aggregate(nc, w, k, t, r, kind, heads, keep, wm, ws, bias_row, plus_x):
    H = heads
    M = C + H
    sigmoid = kind == "sigmoid"
    with phase(nc) as ctx:
        pre = f"c{r}_"
        sb = lambda n, s: ctx.enter_context(nc.sbuf_tensor(pre + n, s, F32))
        sem = lambda n: ctx.semaphore(pre + n)
        KB = sb("kb", [P, GE, J, P])
        SEL = sb("sel", [P, GE, J, P])
        CAR = sb("car", [P, GE, J, P])
        MS = sb("ms", [P, GE, J, M])
        SUM = sb("sum", [P, GE, J, M])
        U = MS[:, :, :, 0:C]
        DN = sb("dn", [P, GE, J, H])
        XD = KB
        A = sb("a", [P, GE, J, C]) if sigmoid else KB
        PS = [ctx.enter_context(nc.psum_tensor(f"{pre}ps{n}", [P, 512], F32)) for n in range(J)]
        s_sel, s_ms, s_pe, s_sum, s_own, s_num, s_den, s_bias, s_sig, s_next, s_x, s_zero = (
            sem(n) for n in "sel ms pe sum own num den bias sig next x zero".split())
        s_kb = [sem(f"kb{g}") for g in range(GE)]
        s_load = [sem(f"load{g}") for g in range(GE)]
        s_xd = [sem(f"xd{g}") for g in range(GE)]
        s_out = [sem(f"out{g}") for g in range(GE)]
        block = ctx.enter_context(nc.Block())
        heads_of = lambda x: x.rearrange("p j (h c) -> p j h c", h=H)
        over = lambda x: x[:, :, :, None].to_broadcast([P, J, H, C // H])
        state_table = t[f"d{r}"]

        @block.sync
        def _(eng):
            def load_keys(b, g):
                if sigmoid:
                    wait(eng, *((s_x, b - GE + 1) if plus_x else (s_sel, (b - GE + 1) * 2)))
                else:
                    wait(eng, s_out[g], (b // GE) * 16)
                carry_waits(eng, w)
                eng.dma_start(KB[:, g, :, :].rearrange("p j q -> p (j q)"),
                              t["dst_row"][0:1, bass.ds(number(b) * (J * P), J * P)].to_broadcast([P, J * P])).then_inc(s_kb[g], 16)
                if sigmoid:
                    wait(eng, s_out[g], (b // GE) * 16)
                    carry_waits(eng, w)
                    eng.dma_start(A[:, g, :, :], block_rows(state_table, b)).then_inc(s_load[g], 16)

            def load(b, g):
                wait(eng, s_sel, (b + 1) * 2)
                carry_waits(eng, w)
                if plus_x:
                    eng.dma_start(XD[:, g, :, :], block_rows(t["xd"], b)).then_inc(s_xd[g], 16)
                elif not sigmoid:
                    eng.dma_start(A[:, g, :, :], block_rows(state_table, b)).then_inc(s_load[g], 16)

            def store(b, g):
                wait(eng, s_next, b + 1)
                carry_waits(eng, w)
                eng.dma_start(block_rows(t[f"d{r + 1}"], b), A[:, g, :, :]).then_inc(s_out[g], 16)

            stream(eng, (load_keys, 0), (load, 2), (store, 4))
            for g in range(GE):
                eng.wait_ge(s_out[g], 16 * ROUNDS_E)

        @block.gpsimd
        def _(eng):
            def own(b, g):
                wait(eng, s_pe, (b + 1) * J)
                carry_waits(eng, w)
                nc.gpsimd.tensor_tensor(heads_of(U[:, g, :, :]), heads_of(tiles_of(keep["dst"], b)[:, :, 0:C]),
                                        over(tiles_of(ws, b)[:, :, 0:H]), ALU.mult).then_inc(s_own, 1)

            def bias(b, g):
                wide = bias_row[:, None, :].to_broadcast([P, J, C])
                if sigmoid:
                    wait(eng, s_num, (b + 1) * 2)
                    nc.gpsimd.tensor_tensor(U[:, g, :, :], U[:, g, :, :], wide, ALU.add).then_inc(s_bias, 1)
                else:
                    wait(eng, s_load[g], (b // GE + 1) * 16)
                    nc.gpsimd.tensor_tensor(A[:, g, :, :], A[:, g, :, :], wide, ALU.add).then_inc(s_bias, 1)
                if plus_x:
                    wait(eng, s_load[g], (b // GE + 1) * 16)
                    wait(eng, s_xd[g], (b // GE + 1) * 16)
                    nc.gpsimd.tensor_tensor(A[:, g, :, :], A[:, g, :, :], XD[:, g, :, :], ALU.add).then_inc(s_x, 1)

            stream(eng, (bias, 1), (own, 0))

        @block.vector
        def _(eng):
            v = nc.vector
            v.memset(SUM[:, GE - 1, J - 1, :], 0.0).then_inc(s_zero, 1)

            def select(b, g):
                wait(eng, s_pe, (b - GE + 1) * J)
                wait(eng, s_kb[g], (b // GE + 1) * 16)
                carry_waits(eng, w)
                v.tensor_tensor(SEL[:, g, :, :], KB[:, g, :, :], tiles_of(k["dst_col"], b)[:, :, None].to_broadcast([P, J, P]), ALU.is_equal).then_inc(s_sel, 1)
                v.tensor_tensor(CAR[:, g, :, :], KB[:, g, :, :], tiles_of(k["prev_col"], b)[:, :, None].to_broadcast([P, J, P]), ALU.is_equal).then_inc(s_sel, 1)

            def messages(b, g):
                wait(eng, s_next, b - GE + 1)
                carry_waits(eng, w)
                wt = tiles_of(wm, b)[:, :, 0:H]
                v.tensor_tensor(heads_of(MS[:, g, :, 0:C]), heads_of(tiles_of(keep["src"], b)[:, :, 0:C]), over(wt), ALU.mult).then_inc(s_ms, 1)
                v.tensor_scalar(MS[:, g, :, C:M], wt, 0.0, None, ALU.add).then_inc(s_ms, 1)

            def merge(b, g):
                wait(eng, s_sum, (b + 1) * J)
                carry_waits(eng, w)
                v.tensor_tensor(DN[:, g, :, :], SUM[:, g, :, C:M], tiles_of(ws, b)[:, :, 0:H], ALU.add).then_inc(s_den, 1)
                wait(eng, s_own, b + 1)
                v.tensor_tensor(U[:, g, :, :], U[:, g, :, :], SUM[:, g, :, 0:C], ALU.add).then_inc(s_num, 1)
                wait(eng, s_den, b * 3 + 1)
                v.tensor_scalar(DN[:, g, :, :], DN[:, g, :, :], GAT_EPS if sigmoid else 0.0, None, ALU.add).then_inc(s_den, 1)
                wait(eng, s_den, b * 3 + 2)
                v.reciprocal(DN[:, g, :, :], DN[:, g, :, :]).then_inc(s_den, 1)
                wait(eng, s_num, b * 2 + 1)
                wait(eng, s_den, b * 3 + 3)
                v.tensor_tensor(heads_of(U[:, g, :, :]), heads_of(U[:, g, :, :]), over(DN[:, g, :, :]), ALU.mult).then_inc(s_num, 1)

            def add(b, g):
                if sigmoid:
                    wait(eng, s_sig, b + 1)
                    wait(eng, s_load[g], (b // GE + 1) * 16)
                    if plus_x:
                        wait(eng, s_x, b + 1)
                else:
                    wait(eng, s_num, b * 2 + 2)
                    wait(eng, s_bias, b + 1)
                v.tensor_tensor(A[:, g, :, :], A[:, g, :, :], U[:, g, :, :], ALU.add).then_inc(s_next, 1)

            stream(eng, (select, 0), (messages, 0), (merge, 2), (add, 3))

        @block.scalar
        def _(eng):
            def sums(b, g):
                wait(eng, s_num, (b - GE) * 2 + 1)
                wait(eng, s_den, (b - GE) * 3 + 1)
                for j in range(J):
                    wait(eng, s_pe, b * J + j + 1)
                    nc.scalar.activation(SUM[:, g, j, :], PS[j][:, 0:M], ACT.Copy).then_inc(s_sum, 1)

            def squash(b, g):
                wait(eng, s_bias, b + 1)
                nc.scalar.activation(U[:, g, :, :], U[:, g, :, :], ACT.Sigmoid).then_inc(s_sig, 1)

            stream(eng, (sums, 0), *([(squash, 2)] if sigmoid else []))

        @block.tensor
        def _(eng):
            eng.wait_ge(s_zero, 1)

            def tiles(b, g):
                wait(eng, s_ms, (b + 1) * 2)
                wait(eng, s_sel, (b + 1) * 2)
                for j in range(J):
                    wait(eng, s_sum, (b - 1) * J + j + 1)
                    nc.tensor.matmul(PS[j][:, 0:M], SEL[:, g, j, :], MS[:, g, j, :], start=True, stop=False)
                    wait(eng, s_sum, b * J + j)
                    before = SUM[:, g, j - 1, :] if j else SUM[:, (g - 1) % GE, J - 1, :]
                    nc.tensor.matmul(PS[j][:, 0:M], CAR[:, g, j, :], before, start=False, stop=True).then_inc(s_pe, 1)

            stream(eng, (tiles, 0))


def relate(nc, w, k, t, r):
    M = C + 1
    with phase(nc) as ctx:
        pre = f"r{r}_"
        sb = lambda n, s: ctx.enter_context(nc.sbuf_tensor(pre + n, s, F32))
        sem = lambda n: ctx.semaphore(pre + n)
        ps = lambda n, s: ctx.enter_context(nc.psum_tensor(pre + n, s, F32))
        ends = Ends(nc, ctx, pre + "ends", w, k, t, f"s{r}", f"d{r}", True)
        A = ends.A
        HT = sb("ht", [P, GE, 2, J * C])
        NR = HT[:, :, :, :].rearrange("p g s (j c) -> p g s j c", j=J)
        LOOP = NR[:, :, DST]
        KB = sb("kb", [P, GE, J, P])
        SEL, CAR = sb("sel", [P, GE, J, P]), sb("car", [P, GE, J, P])
        MS, SUM = sb("ms", [P, GE, J, M]), sb("sum", [P, GE, J, M])
        UP = sb("up", [P, GE, J, C])
        DN = sb("dn", [P, GE, J, 1])
        CF = sb("cf", [P, GE, J, BASES])
        nb = Norms(nc, ctx, pre + "nb", w)
        PT = [ps(f"pt{n}", [P, J, C]) for n in range(2)]
        PM = [ps(f"pm{n}", [P, J, C]) for n in range(2)]
        PB = [ps(f"pb{n}", [P, BASES, C]) for n in range(2)]
        PS = [ps(f"ps{n}", [P, 512]) for n in range(2)]
        s_tp, s_ht, s_mm, s_loop, s_next, s_next_dst, s_basis, s_mix, s_sel, s_pe, s_sum, s_zero, s_deg, s_pow, s_mean, s_num, s_coef = (
            sem(n) for n in "tp ht mm loop next next_dst basis mix sel pe sum zero deg pow mean num coef".split())
        s_kb = [sem(f"kb{g}") for g in range(GE)]
        s_out = [sem(f"out{g}") for g in range(GE)]
        block = ctx.enter_context(nc.Block())

        @block.sync
        def _(eng):
            def load(b, g):
                wait(eng, s_out[g], (b // GE) * 32)
                carry_waits(eng, w)
                ends.load(eng, b, g)
                wait(eng, s_sel, (b - GE + 1) * 2)
                carry_waits(eng, w)
                eng.dma_start(KB[:, g, :, :].rearrange("p j q -> p (j q)"),
                              t["dst_row"][0:1, bass.ds(number(b) * (J * P), J * P)].to_broadcast([P, J * P])).then_inc(s_kb[g], 16)

            def store(b, g):
                wait(eng, s_next, b + 1)
                carry_waits(eng, w)
                eng.dma_start(block_rows(t[f"s{r + 1}"], b), A[:, g, SRC, :, :]).then_inc(s_out[g], 16)
                wait(eng, s_next_dst, b + 1)
                carry_waits(eng, w)
                eng.dma_start(block_rows(t[f"d{r + 1}"], b), A[:, g, DST, :, :]).then_inc(s_out[g], 16)

            stream(eng, (load, 0), (store, 4))
            for g in range(GE):
                eng.wait_ge(s_out[g], 32 * ROUNDS_E)

        @block.gpsimd
        def _(eng):
            def mean(b, g):
                wait(eng, s_deg, b + 1)
                wait(eng, s_next_dst, b - GE + 1)
                nc.gpsimd.tensor_tensor(DN[:, g, :, 0], DN[:, g, :, 0], w["neg_half"][:, 0:J], ALU.pow).then_inc(s_pow, 1)
                wait(eng, s_pow, b + 1)
                nc.gpsimd.tensor_tensor(UP[:, g, :, :], SUM[:, g, :, 0:C], DN[:, g, :, :].to_broadcast([P, J, C]), ALU.mult).then_inc(s_mean, 1)

            stream(eng, (lambda b, g: ends.gather(eng, b, g), 0), (lambda b, g: nb.invert(eng, b, g), 1), (mean, 2))

        @block.vector
        def _(eng):
            v = nc.vector
            v.memset(SUM[:, GE - 1, J - 1, :], 0.0).then_inc(s_zero, 1)
            v.memset(MS[:, :, :, C:M], 1.0).then_inc(s_zero, 1)

            def stats(b, g):
                ends.there(eng, b, g)
                nb.take(eng, A[:, g, :, :, :], b, g)

            def apply(b, g):
                nb.shifts(eng, b, g)
                wait(eng, s_mm, (b - GE) * 2 + 1)
                wait(eng, s_basis, (b - GE + 1) * J)
                nb.apply(eng, NR[:, g, SRC, :, :], A[:, g, SRC, :, :], SRC, b, g)

            def select(b, g):
                wait(eng, s_pe, (b - GE + 1) * J)
                wait(eng, s_kb[g], (b // GE + 1) * 16)
                carry_waits(eng, w)
                v.tensor_scalar(CF[:, g, :, :], tiles_of(k["coef"], b), 0.0, None, ALU.add).then_inc(s_coef, 1)
                v.tensor_tensor(SEL[:, g, :, :], KB[:, g, :, :], tiles_of(k["dst_col"], b)[:, :, None].to_broadcast([P, J, P]), ALU.is_equal).then_inc(s_sel, 1)
                v.tensor_tensor(CAR[:, g, :, :], KB[:, g, :, :], tiles_of(k["prev_col"], b)[:, :, None].to_broadcast([P, J, P]), ALU.is_equal).then_inc(s_sel, 1)

            def mix(b, g):
                wait(eng, s_mm, b * 2 + 1)
                wait(eng, nb.s_normed[SRC], (b + 1) * J)
                v.scalar_tensor_tensor(A[:, g, SRC, :, :], PM[SRC][:, :, :], 0.0, A[:, g, SRC, :, :], ALU.max, ALU.add).then_inc(s_next, 1)
                wait(eng, s_pe, (b - GE + 1) * J)
                wait(eng, s_coef, b + 1)
                for j in range(J):
                    coef = [CF[:, g, j, base:base + 1] for base in range(BASES)]
                    wait(eng, s_basis, b * J + j + 1)
                    v.tensor_scalar(MS[:, g, j, 0:C], PB[j % 2][:, 0, :], coef[0], None, ALU.mult).then_inc(s_mix, 1)
                    for base in range(1, BASES):
                        wait(eng, s_mix, (b * J + j) * BASES + base)
                        v.scalar_tensor_tensor(MS[:, g, j, 0:C], PB[j % 2][:, base, :], coef[base], MS[:, g, j, 0:C], ALU.mult, ALU.add).then_inc(s_mix, 1)

            def degree(b, g):
                wait(eng, s_sum, (b + 1) * J)
                wait(eng, s_mean, b - GE + 1)
                v.tensor_scalar(DN[:, g, :, :], SUM[:, g, :, C:M], 1.0, None, ALU.max).then_inc(s_deg, 1)

            def finish(b, g):
                wait(eng, s_mean, b + 1)
                wait(eng, s_loop, b + 1)
                v.tensor_tensor(UP[:, g, :, :], UP[:, g, :, :], LOOP[:, g, :, :], ALU.add).then_inc(s_num, 1)
                wait(eng, s_num, b + 1)
                wait(eng, nb.s_normed[DST], (b + 1) * J)
                v.scalar_tensor_tensor(A[:, g, DST, :, :], UP[:, g, :, :], 0.0, A[:, g, DST, :, :], ALU.max, ALU.add).then_inc(s_next_dst, 1)

            stream(eng, (lambda b, g: ends.index(eng, b, g), 0), (degree, 4), (stats, 2), (mix, 3), (apply, 2), (select, 2), (finish, 4))

        @block.scalar
        def _(eng):
            def apply(b, g):
                wait(eng, s_num, b - GE + 1)
                nb.apply_scalar(eng, NR[:, g, DST, :, :], A[:, g, DST, :, :], DST, b, g)

            def copy(b, g):
                for side in (SRC, DST):
                    wait(eng, s_tp, b * 2 + side + 1)
                    nc.scalar.activation(HT[:, g, side, :], PT[side][:, :, :].rearrange("p j c -> p (j c)"), ACT.Relu).then_inc(s_ht, 1)

            def loop(b, g):
                wait(eng, s_mm, b * 2 + 2)
                nc.scalar.activation(LOOP[:, g, :, :], PM[DST][:, :, :], ACT.Copy).then_inc(s_loop, 1)

            def sums(b, g):
                wait(eng, s_mean, b - GE + 1)
                for j in range(J):
                    wait(eng, s_pe, b * J + j + 1)
                    nc.scalar.activation(SUM[:, g, j, :], PS[j % 2][:, 0:M], ACT.Copy).then_inc(s_sum, 1)

            stream(eng, (apply, 0), (copy, 0), (loop, 0), (sums, 0))

        @block.tensor
        def _(eng):
            eng.wait_ge(s_zero, 2)

            def turn(b, g):
                for side in (SRC, DST):
                    wait(eng, nb.s_normed[side], (b + 1) * J)
                    wait(eng, s_ht, (b - 1) * 2 + side + 1)
                    for j in range(J):
                        last = nc.tensor.transpose(PT[side][:, j, :], NR[:, g, side, j, :], w["ident"][:, :])
                    last.then_inc(s_tp, 1)

            def product(b, g, side=SRC):
                wait(eng, s_ht, b * 2 + side + 1)
                wait(eng, s_loop if side else s_next, b)
                for j in range(J):
                    last = nc.tensor.matmul(PM[side][:, j, :], HT[:, g, side, j * C:(j + 1) * C], w["loop"][:, :], start=True, stop=True)
                last.then_inc(s_mm, 1)

            def tiles(b, g):
                def summed(j):
                    wait(eng, s_mix, (b * J + j + 1) * BASES)
                    wait(eng, s_sum, b * J + j - 1)
                    nc.tensor.matmul(PS[j % 2][:, 0:M], SEL[:, g, j, :], MS[:, g, j, :], start=True, stop=False)
                    wait(eng, s_sum, b * J + j)
                    before = SUM[:, g, j - 1, :] if j else SUM[:, (g - 1) % GE, J - 1, :]
                    nc.tensor.matmul(PS[j % 2][:, 0:M], CAR[:, g, j, :], before, start=False, stop=True).then_inc(s_pe, 1)

                wait(eng, s_sel, (b + 1) * 2)
                for j in range(J):
                    wait(eng, s_mix, (b * J + j - 1) * BASES)
                    nc.tensor.matmul(PB[j % 2][:, :, :].rearrange("p b c -> p (b c)"), HT[:, g, SRC, j * C:(j + 1) * C],
                                     w["basis"][:, :, :].rearrange("p b c -> p (b c)"), start=True, stop=True).then_inc(s_basis, 1)
                    if j == 1:
                        product(b, g, DST)
                    if j:
                        summed(j - 1)
                summed(J - 1)

            stream(eng, (turn, 0), (product, 0), (tiles, 0))


def edge_messages(nc, w, k, t, r, out):
    M = C + 1
    MAP, HOLD, ACC, OUT = range(4)
    with phase(nc) as ctx:
        sb = lambda n, s, d=F32: ctx.enter_context(nc.sbuf_tensor("e_" + n, s, d))
        sem = lambda n: ctx.semaphore("e_" + n)
        IX = sb("ix", [P, GE, 4, J], I32)
        A = sb("a", [P, GE, 2, J, C])
        HT = sb("ht", [P, GE, 2, J * C])
        NR = HT[:, :, :, :].rearrange("p g s (j c) -> p g s j c", j=J)
        GT = sb("gt", [P, GE, 2, J * C])
        AD = sb("ad", [P, GE, J * C])
        KB = sb("kb", [P, GE, J, P])
        SEL = sb("sel", [P, GE, J, P])
        MS = sb("ms", [P, GE, J, M])
        TOT = sb("tot", [P, GE, J, M])
        nb = Norms(nc, ctx, "e_nb", w)
        ps = lambda n, s: ctx.enter_context(nc.psum_tensor("e_" + n, s, F32))
        PT = [ps(f"pt{n}", [P, J, C]) for n in range(2)]
        PG, PM, PZ, PD = (ps(n, [P, J, C]) for n in "pg pm pz pd".split())
        PO = [ps(f"po{n}", [P, 2, 256]) for n in range(2)]
        s_ix, s_tp, s_ht, s_pg, s_nm, s_gt, s_sel, s_diff, s_abs, s_nh, s_ms, s_po, s_tot, s_z, s_d, s_one, s_acc = (
            sem(n) for n in "ix tp ht pg nm gt sel diff abs nh ms po tot z d one acc".split())
        s_kb = [sem(f"kb{g}") for g in range(GE)]
        s_load = [sem(f"load{g}") for g in range(GE)]
        s_over = [sem(f"over{g}") for g in range(GE)]
        s_hold = [sem(f"hold{g}") for g in range(GE)]
        s_out = [sem(f"out{g}") for g in range(GE)]
        s_gt_out = [sem(f"gt_out{g}") for g in range(GE)]
        s_sz_out = [sem(f"sz_out{g}") for g in range(GE)]
        block = ctx.enter_context(nc.Block())

        @block.sync
        def _(eng):
            def load(b, g):
                wait(eng, s_sz_out[g], (b // GE) * 16)
                carry_waits(eng, w)
                eng.dma_start(A[:, g, SRC, :, :], block_rows(t[f"s{r}"], b)).then_inc(s_load[g], 16)
                wait(eng, s_sel, b - GE + 1)
                carry_waits(eng, w)
                eng.dma_start(KB[:, g, :, :].rearrange("p j q -> p (j q)"),
                              t["src_row"][0:1, bass.ds(number(b) * (J * P), J * P)].to_broadcast([P, J * P])).then_inc(s_kb[g], 16)

            def store(b, g):
                wait(eng, s_gt, b * 2 + 1)
                carry_waits(eng, w)
                eng.dma_start(t["gt"][bass.ds(number(b) * P, P), :], GT[:, g, SRC, :]).then_inc(s_gt_out[g], 16)
                wait(eng, s_z, (b + 1) * 2)
                carry_waits(eng, w)
                eng.dma_start(block_rows(t["sz"], b), A[:, g, SRC, :, :]).then_inc(s_sz_out[g], 16)

            stream(eng, (load, 0), (store, 3))
            for g in range(GE):
                eng.wait_ge(s_gt_out[g], 16 * ROUNDS_E)
                eng.wait_ge(s_sz_out[g], 16 * ROUNDS_E)

        @block.gpsimd
        def _(eng):
            def gather(b, g, what, side, j, s):
                eng.indirect_dma_start(out=A[:, g, side, j, :], out_offset=None, in_=t[f"d{r}"],
                                       in_offset=bass.IndirectOffsetOnAxis(ap=IX[:, g, what, j:j + 1], axis=0),
                                       bounds_check=EP - 1, oob_is_err=False).then_inc(s, 16)

            def transfers(j):
                def states(b, g):
                    if j == 0:
                        wait(eng, s_ix, b + 1)
                        wait(eng, s_load[g], (b // GE + 1) * 16)
                        wait(eng, s_out[g], (b // GE) * (16 * J))
                    carry_waits(eng, w)
                    gather(b, g, MAP, SRC, j, s_over[g])
                    gather(b, g, HOLD, DST, j, s_hold[g])

                def results(b, g):
                    wait(eng, s_tot, b * 2 + j // 2 + 1)
                    wait(eng, s_acc, (b * J + j) * 16)
                    carry_waits(eng, w)
                    eng.indirect_dma_start(out=t["acc"], out_offset=bass.IndirectOffsetOnAxis(ap=IX[:, g, ACC, j:j + 1], axis=0),
                                           in_=TOT[:, g, j, :], in_offset=None, compute_op=ALU.add).then_inc(s_acc, 16)
                    wait(eng, s_d, (b + 1) * 2)
                    carry_waits(eng, w)
                    eng.indirect_dma_start(out=out, out_offset=bass.IndirectOffsetOnAxis(ap=IX[:, g, OUT, j:j + 1], axis=0),
                                           in_=A[:, g, DST, j, :], in_offset=None,
                                           bounds_check=N - 1, oob_is_err=False).then_inc(s_out[g], 16)

                return (states, 0), (results, 3)

            stream(eng, *transfers(0), (lambda b, g: nb.invert(eng, b, g), 1), *transfers(1), *transfers(2), *transfers(3))
            eng.wait_ge(s_acc, 16 * T)
            for g in range(GE):
                eng.wait_ge(s_out[g], 16 * J * ROUNDS_E)

        @block.vector
        def _(eng):
            v = nc.vector
            v.memset(MS[:, :, :, C:M], 1.0).then_inc(s_one, 1)

            def index(b, g):
                for s in (s_out[g], s_over[g], s_hold[g]):
                    wait(eng, s, (b // GE) * (16 * J))
                    carry_waits(eng, w)
                wait(eng, s_acc, (b - GE + 1) * (16 * J))
                carry_waits(eng, w)
                for n, name in enumerate(("map_ix", "hold_ix", "acc_ix", "out_d_ix")):
                    last = v.tensor_scalar(IX[:, g, n, :], tiles_of(k[name], b), 0.0, None, ALU.add)
                last.then_inc(s_ix, 1)

            def stats(b, g):
                wait(eng, s_over[g], (b // GE + 1) * (16 * J))
                wait(eng, s_hold[g], (b // GE + 1) * (16 * J))
                nb.take(eng, A[:, g, :, :, :], b, g)

            def apply(b, g):
                nb.shifts(eng, b, g)
                wait(eng, s_nm, (b - GE) * 2 + 1)
                nb.apply(eng, NR[:, g, SRC, :, :], A[:, g, SRC, :, :], SRC, b, g)

            def select(b, g):
                wait(eng, s_kb[g], (b // GE + 1) * 16)
                wait(eng, s_po, (b - GE + 1) * 2)
                carry_waits(eng, w)
                v.tensor_tensor(SEL[:, g, :, :], KB[:, g, :, :], tiles_of(k["src_col"], b)[:, :, None].to_broadcast([P, J, P]), ALU.is_equal).then_inc(s_sel, 1)

            def combine(b, g):
                wait(eng, s_gt, (b + 1) * 2)
                wait(eng, s_nh, b - GE + 1)
                v.tensor_tensor(AD[:, g, :], GT[:, g, SRC, :], GT[:, g, DST, :], ALU.subtract).then_inc(s_diff, 1)
                for side, ps_, row, s in ((SRC, PZ, w["bl_row"], s_z), (DST, PD, w["bias_rows"][1], s_d)):
                    wait(eng, s_nm, b * 2 + side + 1)
                    wait(eng, nb.s_normed[side], (b + 1) * J)
                    v.tensor_tensor(A[:, g, side, :, :], A[:, g, side, :, :], ps_[:, :, :], ALU.add).then_inc(s, 1)
                    wait(eng, s, b * 2 + 1)
                    v.tensor_tensor(A[:, g, side, :, :], A[:, g, side, :, :], row[:, None, :].to_broadcast([P, J, C]), ALU.add).then_inc(s, 1)

            def messages(b, g):
                wait(eng, s_nh, b + 1)
                wait(eng, s_po, (b - GE + 1) * 2)
                v.tensor_tensor(MS[:, g, :, 0:C], PM[:, :, :], w["be_row"][:, None, :].to_broadcast([P, J, C]), ALU.add).then_inc(s_ms, 1)

            stream(eng, (stats, 2), (apply, 2), (index, 0), (select, 2), (combine, 2), (messages, 2))

        @block.scalar
        def _(eng):
            def apply(b, g):
                wait(eng, s_nm, (b - GE + 1) * 2)
                nb.apply_scalar(eng, NR[:, g, DST, :, :], A[:, g, DST, :, :], DST, b, g)

            def copy(b, g):
                for side in (SRC, DST):
                    wait(eng, s_tp, b * 2 + side + 1)
                    nc.scalar.activation(HT[:, g, side, :], PT[side][:, :, :].rearrange("p j c -> p (j c)"), ACT.Relu).then_inc(s_ht, 1)

            def features(b, g):
                wait(eng, s_diff, b - GE + 1)
                wait(eng, s_nh, b - GE + 1)
                wait(eng, s_gt_out[g], (b // GE) * 16)
                for side in (SRC, DST):
                    wait(eng, s_pg, b * 2 + side + 1)
                    carry_waits(eng, w)
                    nc.scalar.activation(GT[:, g, side, :], PG[:, :, :].rearrange("p j c -> p (j c)"), ACT.Identity,
                                         bias=w["bn_col"][:, 0:1]).then_inc(s_gt, 1)

            def absolute(b, g):
                wait(eng, s_diff, b + 1)
                nc.scalar.activation(AD[:, g, :], AD[:, g, :], ACT.Abs).then_inc(s_abs, 1)

            def totals(b, g):
                wait(eng, s_acc, (b - GE + 1) * (16 * J))
                for q in range(2):
                    wait(eng, s_po, b * 2 + q + 1)
                    nc.scalar.activation(TOT[:, g, 2 * q:2 * q + 2, :], PO[q][:, :, 0:M], ACT.Copy).then_inc(s_tot, 1)

            stream(eng, (apply, 0), (copy, 0), (features, 0), (absolute, 0), (totals, 0))

        @block.tensor
        def _(eng):
            eng.wait_ge(s_one, 1)

            def turn(b, g):
                for side in (SRC, DST):
                    wait(eng, nb.s_normed[side], (b + 1) * J)
                    wait(eng, s_ht, (b - 1) * 2 + side + 1)
                    for j in range(J):
                        last = nc.tensor.transpose(PT[side][:, j, :], NR[:, g, side, j, :], w["ident"][:, :])
                    last.then_inc(s_tp, 1)

            def product(b, g):
                for side in (SRC, DST):
                    wait(eng, s_ht, b * 2 + side + 1)
                    wait(eng, s_gt, b * 2 + side)
                    nc.tensor.matmul(PG[:, :, :].rearrange("p j c -> p (j c)"), w["wnT"][:, :], HT[:, g, side, :], start=True, stop=True).then_inc(s_pg, 1)
                for side in (SRC, DST):
                    wait(eng, s_d if side else s_z, b * 2)
                    for j in range(J):
                        last = nc.tensor.matmul((PD if side else PZ)[:, j, :], HT[:, g, side, j * C:(j + 1) * C],
                                                w["fused3"][:, :] if side else w["wlT"][:, 0, :], start=True, stop=True)
                    last.then_inc(s_nm, 1)

            def edges(b, g):
                wait(eng, s_abs, b + 1)
                wait(eng, s_ms, b)
                for j in range(J):
                    nc.tensor.matmul(PM[:, j, :], GT[:, g, DST, j * C:(j + 1) * C], w["weT"][:, 0, :], start=True, stop=False)
                    last = nc.tensor.matmul(PM[:, j, :], AD[:, g, j * C:(j + 1) * C], w["weT"][:, 1, :], start=False, stop=True)
                last.then_inc(s_nh, 1)
                wait(eng, s_ms, b + 1)
                wait(eng, s_sel, b + 1)
                for q in range(2):
                    wait(eng, s_tot, (b - 1) * 2 + q + 1)
                    for n in range(2):
                        last = nc.tensor.matmul(PO[q][:, n, 0:M], SEL[:, g, 2 * q + n, :], MS[:, g, 2 * q + n, :], start=True, stop=True)
                    last.then_inc(s_po, 1)

            stream(eng, (turn, 0), (product, 0), (edges, 0))


def edge_outputs(nc, w, k, t, out):
    M = C + 1
    with phase(nc) as ctx:
        sb = lambda n, s, d=F32: ctx.enter_context(nc.sbuf_tensor("o_" + n, s, d))
        sem = lambda n: ctx.semaphore("o_" + n)
        IX = sb("ix", [P, GE, J], I32)
        ACC = sb("acc", [P, GE, J, M])
        GT = sb("gt", [P, GE, J * C])
        SZ = sb("sz", [P, GE, J, C])
        UP = sb("up", [P, GE, J, C])
        CN = sb("cn", [P, GE, J, 1])
        PT = [ctx.enter_context(nc.psum_tensor(f"o_pt{n}", [P, J, C], F32)) for n in range(2)]
        PM = [ctx.enter_context(nc.psum_tensor(f"o_pm{n}", [P, J, C], F32)) for n in range(2)]
        s_ix, s_cnt, s_tp, s_s, s_mm, s_up, s_out_in = (sem(n) for n in "ix cnt tp s mm up out_in".split())
        s_load = [sem(f"load{g}") for g in range(GE)]
        s_out = [sem(f"out{g}") for g in range(GE)]
        block = ctx.enter_context(nc.Block())
        before = lambda b, g: b - (1 if g == 0 else 2)

        @block.sync
        def _(eng):
            def load(b, g):
                wait(eng, s_out[g], (b // GE) * (16 * J))
                carry_waits(eng, w)
                eng.dma_start(ACC[:, g, :, :], block_rows(t["acc"], b)).then_inc(s_load[g], 16)
                eng.dma_start(GT[:, g, :], t["gt"][bass.ds(number(b) * P, P), :]).then_inc(s_load[g], 16)
                eng.dma_start(SZ[:, g, :, :], block_rows(t["sz"], b)).then_inc(s_load[g], 16)

            stream(eng, (load, 0))

        @block.gpsimd
        def _(eng):
            def write(b, g):
                wait(eng, s_ix, b + 1)
                wait(eng, s_out_in, b + 1)
                carry_waits(eng, w)
                for j in range(J):
                    eng.indirect_dma_start(out=out, out_offset=bass.IndirectOffsetOnAxis(ap=IX[:, g, j:j + 1], axis=0),
                                           in_=SZ[:, g, j, :], in_offset=None,
                                           bounds_check=N - 1, oob_is_err=False).then_inc(s_out[g], 16)

            stream(eng, (write, 0))
            for g in range(GE):
                eng.wait_ge(s_out[g], 16 * J * ROUNDS_E)

        @block.vector
        def _(eng):
            v = nc.vector

            def count_(b, g):
                wait(eng, s_out[g], (b // GE) * (16 * J))
                carry_waits(eng, w)
                v.tensor_scalar(IX[:, g, :], tiles_of(k["out_s_ix"], b), 0.0, None, ALU.add).then_inc(s_ix, 1)
                wait(eng, s_load[g], (b // GE + 1) * 48)
                v.tensor_scalar(CN[:, g, :, :], ACC[:, g, :, C:M], 1.0, None, ALU.max).then_inc(s_cnt, 1)
                wait(eng, s_cnt, b * 2 + 1)
                v.reciprocal(CN[:, g, :, :], CN[:, g, :, :]).then_inc(s_cnt, 1)

            def summed(b, g):
                wait(eng, s_tp, b + 1)
                v.tensor_tensor(GT[:, g, :], PT[g % 2][:, :, :].rearrange("p j c -> p (j c)"), GT[:, g, :], ALU.add).then_inc(s_s, 1)

            def finish(b, g):
                wait(eng, s_mm, b + 1)
                wait(eng, s_cnt, b * 2 + 2)
                v.tensor_tensor(UP[:, g, :, :], PM[g % 2][:, :, :], CN[:, g, :, :].to_broadcast([P, J, C]), ALU.mult).then_inc(s_up, 1)
                wait(eng, s_up, b + 1)
                v.tensor_tensor(SZ[:, g, :, :], SZ[:, g, :, :], UP[:, g, :, :], ALU.add).then_inc(s_out_in, 1)

            stream(eng, (count_, 0), (finish, 1), (summed, 0))

        @block.tensor
        def _(eng):
            def turn(b, g):
                wait(eng, s_load[g], (b // GE + 1) * 48)
                wait(eng, s_s, before(b, g) + 1)
                for j in range(J):
                    last = nc.tensor.transpose(PT[g % 2][:, j, :], ACC[:, g, j, 0:C], w["ident"][:, :])
                last.then_inc(s_tp, 1)

            def product(b, g):
                wait(eng, s_s, b + 1)
                wait(eng, s_up, before(b, g) + 1)
                for j in range(J):
                    last = nc.tensor.matmul(PM[g % 2][:, j, :], GT[:, g, j * C:(j + 1) * C], w["wlT"][:, 1, :], start=True, stop=True)
                last.then_inc(s_mm, 1)

            stream(eng, (turn, 0), (product, 0))


def held(nc, ctx, name, width):
    return {s: ctx.enter_context(nc.sbuf_tensor(f"{name}_{s}", [P, T, width], F32)) for s in ("src", "dst")}


def softmax_weights(nc, ctx, name, heads):
    return [ctx.enter_context(nc.sbuf_tensor(f"{name}_{s}_weight", [P, T, heads], F32)) for s in ("edge", "self")]


def layer0_at_edges(nc, w, k, f, t):
    with ExitStack() as ctx:
        keep, (wm, ws) = held(nc, ctx, "layer0", C + 2), softmax_weights(nc, ctx, "layer0", 1)
        for r in range(3):
            project(nc, w, k, t, r, 1, w["aug0"][:, r, :], w["b0_rows"][:, r, :], "plain" if r else "first", r == 2, keep, f)
            if r == 0:
                rows_found(nc, k, f)
            attend(nc, w, k, r, 1, keep, wm, ws)
            aggregate(nc, w, k, t, r, "sigmoid", 1, keep, wm, ws, w["b0_rows"][:, r, :], r == 2)


def layers12_at_edges(nc, w, k, t):
    relate(nc, w, k, t, 3)
    with ExitStack() as ctx:
        keep, (wm, ws) = held(nc, ctx, "layer2", C + 2 * HEADS), softmax_weights(nc, ctx, "layer2", HEADS)
        project(nc, w, k, t, 4, HEADS, w["aug2"][:, :], w["bias_rows"][0][:, :], "normed", False, keep)
        attend(nc, w, k, 4, HEADS, keep, wm, ws)
        aggregate(nc, w, k, t, 4, "linear", HEADS, keep, wm, ws, w["bias_rows"][0][:, :], False)


def program(nc, ins, out):
    with ExitStack() as ctx:
        w = alloc_weights(nc, ctx)
        setup(nc, w, ins)
        t = alloc_tables(nc)
        k = alloc_keys(nc, ctx, w)
        with ExitStack() as search:
            f = alloc_search(nc, search)
            keys(nc, w, k, f, t, ins)
            local_chain(nc, ins["x"], out, w, f, t, G=7, rounds_n=CHAIN_ROUNDS)
            layer0_at_edges(nc, w, k, f, t)
        layers12_at_edges(nc, w, k, t)
        edge_messages(nc, w, k, t, 5, out)
        edge_outputs(nc, w, k, t, out)


def kernel(**a):
    import numpy as np
    import concourse.bacc as bacc
    from concourse.bass_utils import run_bass_kernel_spmd

    a = {k: np.asarray(v) for k, v in a.items()}
    t = lambda v, *axes: np.ascontiguousarray(np.transpose(v, axes or None))
    arrays = {
        "x": a["x"], "src": a["src"], "dst": a["dst"], "etype": a["edge_type_100"],
        "L0_Ws": a["L0_gnn_Ws"], "L0_WsT": t(a["L0_gnn_Ws"], 0, 2, 1),
        "L0_as": t(a["L0_gnn_att_src"]), "L0_ad": t(a["L0_gnn_att_dst"]),
        "L0_b": a["L0_gnn_bias"], "L0_bT": t(a["L0_gnn_bias"]),
        "L1_basis": a["L1_gnn_basis_weights"], "L1_coef": a["L1_gnn_coefficients"], "L1_loop": a["L1_gnn_loop_weight"],
        "L2_W": a["L2_gnn_W_src"], "L2_WT": t(a["L2_gnn_W_src"]),
        "L2_as": a["L2_gnn_attn_src"].reshape(128, 1), "L2_ad": a["L2_gnn_attn_dst"].reshape(128, 1),
        "L2_b": a["L2_gnn_bias"].reshape(1, 128),
        "L3_Wn": a["L3_gnn_W_neigh"], "L3_WnT": t(a["L3_gnn_W_neigh"]), "L3_bn": a["L3_gnn_b_neigh"].reshape(128, 1),
        "L3_WeT": t(a["L3_gnn_W_edge"]), "L3_be": a["L3_gnn_b_edge"].reshape(1, 128),
        "L3_WlT": t(a["L3_gnn_W_lin"]), "L3_bl": a["L3_gnn_b_lin"].reshape(1, 128),
    }
    nc = bacc.Bacc("TRN2", target_bir_lowering=False, num_devices=1)
    ins = {k: nc.dram_tensor("in_" + k, v.shape, mybir.dt.from_np(v.dtype), kind="ExternalInput").ap() for k, v in arrays.items()}
    out = nc.dram_tensor("out", (N, C), F32, kind="ExternalOutput").ap()
    program(nc, ins, out)
    r = run_bass_kernel_spmd(nc, [{"in_" + k: v for k, v in arrays.items()}], core_ids=[0])
    return r.results[0]["out"]
```
